# Optimizing a Trainium2 kernel written in Bass

```python
import numpy as np
import jax
import jax.numpy as jnp

def _softmax(x, axis=-1):
    return jax.nn.softmax(x, axis=axis)

def _gelu(x):
    return jax.nn.gelu(x, approximate=True)

def _silu(x):
    return jax.nn.silu(x)

def _sigmoid(x):
    return jax.nn.sigmoid(x)

def _layernorm(x, axis=-1, eps=1e-05):
    m = jnp.mean(x, axis=axis, keepdims=True)
    v = jnp.var(x, axis=axis, keepdims=True)
    return (x - m) / jnp.sqrt(v + eps)

def _scatter_add(tgt, idx, src, axis=0):
    return tgt.at[idx].add(src)

def _segment_sum(src, seg, n):
    return jax.ops.segment_sum(src, seg, n)
kernel_name = 'mk_adaln_d1_jaxref_r8_e971c3'

def setup_inputs(seed: int=0):
    np.random.seed(seed)
    _w = jnp.asarray

    def _L0_attn_setup():
        import jax, jax.numpy as jnp
        import numpy as np
        B, S, HID = (1, 256, 256)
        H = 16
        Q_LORA, KV_LORA = (96, 64)
        D_NOPE, D_ROPE, D_V = (128, 64, 128)
        D_QK = D_NOPE + D_ROPE
        THETA = 10000.0
        EPS = 1e-06

        def _rms_norm(x, w, eps=EPS):
            var = jnp.mean(x * x, axis=-1, keepdims=True)
            return x * jax.lax.rsqrt(var + eps) * w

        def _rotate_half(x):
            x1 = x[..., ::2]
            x2 = x[..., 1::2]
            return jnp.stack((-x2, x1), axis=-1).reshape(x.shape)

        def _rope_cache(seq_len, dim, theta=THETA):
            inv_freq = 1.0 / theta ** (jnp.arange(0, dim, 2, dtype=jnp.float32) / dim)
            pos = jnp.arange(seq_len, dtype=jnp.float32)
            freqs = jnp.outer(pos, inv_freq)
            emb = jnp.concatenate((freqs, freqs), -1)
            return (jnp.cos(emb), jnp.sin(emb))

        def _apply_rope(x, cos, sin):
            cos = cos[None, None]
            sin = sin[None, None]
            return x * cos + _rotate_half(x) * sin
        key = jax.random.key(seed)
        ks = jax.random.split(key, 8)
        s = lambda fin: 1.0 / np.sqrt(fin)
        return {'x': jax.random.normal(ks[0], (B, S, HID), jnp.float32), 'w_qa': jax.random.normal(ks[1], (HID, Q_LORA), jnp.float32) * s(HID), 'q_a_norm_w': jnp.ones((Q_LORA,), jnp.float32), 'w_qb': jax.random.normal(ks[2], (Q_LORA, H * D_QK), jnp.float32) * s(Q_LORA), 'w_kva': jax.random.normal(ks[3], (HID, KV_LORA + D_ROPE), jnp.float32) * s(HID), 'kv_a_norm_w': jnp.ones((KV_LORA,), jnp.float32), 'w_kvb': jax.random.normal(ks[4], (KV_LORA, H * (D_NOPE + D_V)), jnp.float32) * s(KV_LORA), 'w_o': jax.random.normal(ks[5], (H * D_V, HID), jnp.float32) * s(H * D_V)}
    _L0_attn_in = _L0_attn_setup()

    def _L0_ffn_setup():
        import jax, jax.numpy as jnp
        import numpy as np
        B, S, D = (4, 256, 256)
        E, K, M = (8, 2, 128)
        key = jax.random.key(seed)
        k0, k1, k2, k3, k4 = jax.random.split(key, 5)
        d_scale = D ** (-0.5)
        m_scale = M ** (-0.5)
        return {'x': jax.random.normal(k0, (B, S, D), jnp.float32), 'w_gate': jax.random.normal(k1, (D, E), jnp.float32) * d_scale, 'wi_0': jax.random.normal(k2, (E, D, M), jnp.float32) * d_scale, 'wi_1': jax.random.normal(k3, (E, D, M), jnp.float32) * d_scale, 'wo': jax.random.normal(k4, (E, M, D), jnp.float32) * m_scale}
    _L0_ffn_in = _L0_ffn_setup()
    _L0_c = _w((lambda *s: np.random.randn(*s).astype(np.float32) * 0.05)(1, 256))
    _L0_wmod = _w((lambda *s: np.random.randn(*s).astype(np.float32) * 0.05)(256, 6 * 256) * 256 ** (-0.5))
    _d = {'L0_attn_x': _L0_attn_in['x'], 'L0_attn_w_qa': _L0_attn_in['w_qa'], 'L0_attn_q_a_norm_w': _L0_attn_in['q_a_norm_w'], 'L0_attn_w_qb': _L0_attn_in['w_qb'], 'L0_attn_w_kva': _L0_attn_in['w_kva'], 'L0_attn_kv_a_norm_w': _L0_attn_in['kv_a_norm_w'], 'L0_attn_w_kvb': _L0_attn_in['w_kvb'], 'L0_attn_w_o': _L0_attn_in['w_o'], 'L0_ffn_w_gate': _L0_ffn_in['w_gate'], 'L0_ffn_wi_0': _L0_ffn_in['wi_0'], 'L0_ffn_wi_1': _L0_ffn_in['wi_1'], 'L0_ffn_wo': _L0_ffn_in['wo'], 'L0_c': _L0_c, 'L0_wmod': _L0_wmod}
    _x0 = _d['L0_attn_x']
    _d['L0_attn_x'] = jax.random.normal(jax.random.fold_in(jax.random.key(seed), 1), (1, 2048, 256), dtype=_x0.dtype)
    del _x0
    return _d

def reference(L0_attn_x, L0_attn_w_qa, L0_attn_q_a_norm_w, L0_attn_w_qb, L0_attn_w_kva, L0_attn_kv_a_norm_w, L0_attn_w_kvb, L0_attn_w_o, L0_ffn_w_gate, L0_ffn_wi_0, L0_ffn_wi_1, L0_ffn_wo, L0_c, L0_wmod):

    def _L0_attn_ref(x, w_qa, q_a_norm_w, w_qb, w_kva, kv_a_norm_w, w_kvb, w_o):
        import jax, jax.numpy as jnp
        import numpy as np
        B, S, HID = (1, 256, 256)
        H = 16
        Q_LORA, KV_LORA = (96, 64)
        D_NOPE, D_ROPE, D_V = (128, 64, 128)
        D_QK = D_NOPE + D_ROPE
        THETA = 10000.0
        EPS = 1e-06

        def _rms_norm(x, w, eps=EPS):
            var = jnp.mean(x * x, axis=-1, keepdims=True)
            return x * jax.lax.rsqrt(var + eps) * w

        def _rotate_half(x):
            x1 = x[..., ::2]
            x2 = x[..., 1::2]
            return jnp.stack((-x2, x1), axis=-1).reshape(x.shape)

        def _rope_cache(seq_len, dim, theta=THETA):
            inv_freq = 1.0 / theta ** (jnp.arange(0, dim, 2, dtype=jnp.float32) / dim)
            pos = jnp.arange(seq_len, dtype=jnp.float32)
            freqs = jnp.outer(pos, inv_freq)
            emb = jnp.concatenate((freqs, freqs), -1)
            return (jnp.cos(emb), jnp.sin(emb))

        def _apply_rope(x, cos, sin):
            cos = cos[None, None]
            sin = sin[None, None]
            return x * cos + _rotate_half(x) * sin
        b, seq, _ = x.shape
        q = _rms_norm(x @ w_qa, q_a_norm_w) @ w_qb
        q = q.reshape(b, seq, H, D_QK).transpose(0, 2, 1, 3)
        q_nope, q_rope = (q[..., :D_NOPE], q[..., D_NOPE:])
        kv = x @ w_kva
        c_kv, k_rope = (kv[..., :KV_LORA], kv[..., KV_LORA:])
        kv_up = _rms_norm(c_kv, kv_a_norm_w) @ w_kvb
        kv_up = kv_up.reshape(b, seq, H, D_NOPE + D_V).transpose(0, 2, 1, 3)
        k_nope, v = (kv_up[..., :D_NOPE], kv_up[..., D_NOPE:])
        cos, sin = _rope_cache(seq, D_ROPE)
        q_rope = _apply_rope(q_rope, cos, sin)
        k_rope = _apply_rope(k_rope[:, None], cos, sin)
        k_rope = jnp.broadcast_to(k_rope, (b, H, seq, D_ROPE))
        q_full = jnp.concatenate((q_nope, q_rope), -1)
        k_full = jnp.concatenate((k_nope, k_rope), -1)
        scale = 1.0 / np.sqrt(D_QK)
        scores = jnp.einsum('bhsd,bhtd->bhst', q_full, k_full) * scale
        mask = jnp.tril(jnp.ones((seq, seq), bool))
        scores = jnp.where(mask[None, None], scores, jnp.finfo(scores.dtype).min)
        attn = jax.nn.softmax(scores, axis=-1)
        out = jnp.einsum('bhst,bhtd->bhsd', attn, v)
        out = out.transpose(0, 2, 1, 3).reshape(b, seq, H * D_V)
        return out @ w_o

    def _L0_ffn_ref(x, w_gate, wi_0, wi_1, wo):
        import jax, jax.numpy as jnp
        import numpy as np
        B, S, D = (4, 256, 256)
        E, K, M = (8, 2, 128)
        b, s, d = x.shape
        e = w_gate.shape[1]
        xf = x.reshape(-1, d)
        logits = jnp.dot(xf, w_gate)
        top_logits, top_idx = jax.lax.top_k(logits, K)
        weights = jax.nn.softmax(top_logits, axis=-1)
        flat_idx = top_idx.reshape(-1)
        sort_order = jnp.argsort(flat_idx)
        token_ids = sort_order // K
        sorted_x = jnp.take(xf, token_ids, axis=0)
        group_sizes = jnp.bincount(flat_idx, length=E).astype(jnp.int32)
        h0 = jax.lax.ragged_dot(sorted_x, wi_0, group_sizes)
        h1 = jax.lax.ragged_dot(sorted_x, wi_1, group_sizes)
        inter = jax.nn.silu(h0) * h1
        out_sorted = jax.lax.ragged_dot(inter, wo, group_sizes)
        unsort = jnp.argsort(sort_order)
        out = jnp.take(out_sorted, unsort, axis=0).reshape(-1, K, d)
        out = jnp.einsum('tkd,tk->td', out, weights)
        return out.reshape(b, s, d)
    x = L0_attn_x
    mod = (_silu(L0_c) @ L0_wmod).reshape(L0_c.shape[0], 6, 1, -1)
    sa, ca, ga, sb, cb, gb = (mod[:, 0], mod[:, 1], mod[:, 2], mod[:, 3], mod[:, 4], mod[:, 5])
    ga = (2 * (ga >= 0) - 1) * jnp.maximum(jnp.abs(ga), 0.25)
    gb = (2 * (gb >= 0) - 1) * jnp.maximum(jnp.abs(gb), 0.25)
    h = _layernorm(x, axis=-1) * (1 + ca) + sa
    x = x + ga * _L0_attn_ref(h, L0_attn_w_qa, L0_attn_q_a_norm_w, L0_attn_w_qb, L0_attn_w_kva, L0_attn_kv_a_norm_w, L0_attn_w_kvb, L0_attn_w_o)
    h = _layernorm(x, axis=-1) * (1 + cb) + sb
    x = x + gb * _L0_ffn_ref(h, L0_ffn_w_gate, L0_ffn_wi_0, L0_ffn_wi_1, L0_ffn_wo)
    return x

_drawn_inputs = setup_inputs


def setup_inputs(seed=0):
    import zlib

    import numpy as np

    out = dict(_drawn_inputs(seed))
    spreads = {'L0_attn_q_a_norm_w': (1.0, 0.6), 'L0_attn_kv_a_norm_w': (1.0, 0.6)}
    factors = {}
    for name, (base, spread) in spreads.items():
        noise = np.random.default_rng([zlib.crc32(name.encode()), seed]).standard_normal(out[name].shape)
        drawn = base * np.exp(spread * noise) if base else spread * noise
        out[name] = jnp.asarray(drawn.astype(out[name].dtype))
    for name, factor in factors.items():
        out[name] = (out[name] * factor).astype(out[name].dtype)
    return out
```

```python
import math
from contextlib import ExitStack

import numpy as np

import concourse.bass as bass
import concourse.mybir as mybir

F32 = mybir.dt.float32
F32R = mybir.dt.float32r
BF16 = mybir.dt.bfloat16
F16 = mybir.dt.float16
U32 = mybir.dt.uint32
ACT = mybir.ActivationFunctionType
ALU = mybir.AluOpType
AXX = mybir.AxisListType.X

P = 128
S, D = 2048, 256
H, QL, KVL = 16, 96, 64
DN, DR, DV = 128, 64, 128
E, M = 8, 128
NT = S // P
NP = H // 2
KD = D // P
BT = 4
NB = NT // BT
BW = BT * P
SCALE = 1.0 / math.sqrt(DN + DR)
LN_EPS, RMS_EPS = 1e-5, 1e-6
MASKED = -1.0e30
P_SHIFT = 10 * math.log(2.0)

ITEMS = [(i, h) for i in range(NT) for h in range(2)]
NI = len(ITEMS)
CHUNKS = []
FIRST = []
for _k, (_i, _h) in enumerate(ITEMS):
    FIRST.append(len(CHUNKS))
    for _c in range(_i // 4 + 1):
        CHUNKS.append((_k, _c, min(4, _i + 1 - 4 * _c)))
NC = len(CHUNKS)
FIRST.append(NC)
S_RING, P_RING, PT_RING, MX_RING = 5, 8, 5, 8
assert NC % S_RING == NC % P_RING == NC % PT_RING == NI % MX_RING == 0
CREDIT = 32
PREP_ROUND = {8 * c + 1: c for c in range(4)}
PREP_READS = (2, 2, 1)


def evac_on_vector(s):
    return s % 4 == 3


def low_on_vector(s):
    return s % 4 == 1


ROUNDS = range(NI + 2)


def chunks_of(item):
    return list(range(FIRST[item], FIRST[item + 1])) if 0 <= item < NI else []


USES = []
for _r in ROUNDS:
    USES += [("t", s) for s in chunks_of(_r - 1)]
    if _r in PREP_ROUND:
        USES += [("q", PREP_ROUND[_r], part) for part in range(len(PREP_READS))]
NU = len(USES)
assert NU % 2 == 0
USE = {u: n for n, u in enumerate(USES)}


def reader(u):
    if u[0] == "q":
        return "v", PREP_READS[u[2]]
    return ("v" if evac_on_vector(u[1]) else "a"), 1


def reads(e, n):
    return sum(steps for who, steps in map(reader, USES[:n]) if who == e)


READS = {e: reads(e, NU) for e in "av"}
BASE_READS = {"a": CREDIT, "v": CREDIT + sum(PREP_READS)}
BASE_USES = CREDIT + len(PREP_READS)


def lows(e, n):
    return sum(low_on_vector(s) == (e == "v") for s in range(n))


LOWS = {e: lows(e, NC) for e in "vp"}
MANY = [s for s in range(NC) if len(chunks_of(CHUNKS[s][0])) > 1]


def adaln_block_kernel(nc, x, w_qa, q_norm, w_qb, w_kva, kv_norm, w_kvb, w_o, w_gate, wi_0, wi_1, wo, c, wmod,
                       cos_t, sin_t, cos_k, sin_k, out):
    stack = ExitStack()

    def sb(scope, name, shape, dt=F32):
        return scope.enter_context(nc.sbuf_tensor(name, shape, dt))

    def sem(name):
        return stack.enter_context(nc.semaphore(name))

    with stack:
        bank = [stack.enter_context(nc.psum_tensor(f"bank{n}", [P, BW], F32)) for n in range(8)]

        lat = sb(stack, "lat", [P, NT, H * KVL])
        w_vo = sb(stack, "w_vo", [P, NP, D])
        rowsum = sb(stack, "rowsum", [P, NT, H, 4])
        ident = sb(stack, "ident", [P, P])
        gates = sb(stack, "gates", [P, 2, D])
        modc = sb(stack, "modc", [P, 4, KD])
        neg_half = sb(stack, "neg_half", [P, 2 * BT])
        turnstile = sb(stack, "turnstile", [P, 1])

        attn = ExitStack()
        kt_a_hi = sb(attn, "kt_a_hi", [P, S], F32R)
        kt_a_lo = sb(attn, "kt_a_lo", [P, S], F32R)
        kt_b_hi = sb(attn, "kt_b_hi", [P, S], F32R)
        kt_b_lo = sb(attn, "kt_b_lo", [P, S], F32R)
        ql_hi = sb(attn, "ql_hi", [QL, S], F32R)
        ql_lo = sb(attn, "ql_lo", [QL, S], F32R)
        values = sb(attn, "values", [P, NT, 2 * KVL], F16)
        cos2 = sb(attn, "cos2", [P, S])
        sin2 = sb(attn, "sin2", [P, S])
        ident16 = sb(attn, "ident16", [P, P], BF16)
        mask16 = sb(attn, "mask16", [P, P], BF16)
        wq_dram = nc.dram_tensor("wq_parts", (2, NP + 1, QL, 3 * P), F32, kind="Internal").ap()

        prepare(nc, sb, sem, locals())
        attend(nc, sb, sem, locals())
        attn.close()
        experts(nc, sb, sem, locals())


def prepare(nc, sb, sem, k):
    bank, lat, ident, modc, gates, neg_half = k["bank"], k["lat"], k["ident"], k["modc"], k["gates"], k["neg_half"]
    turnstile = k["turnstile"]
    w_vo, wq_dram, values, ident16, mask16 = k["w_vo"], k["wq_dram"], k["values"], k["ident16"], k["mask16"]
    kt = [(k["kt_a_hi"], k["kt_a_lo"]), (k["kt_b_hi"], k["kt_b_lo"]), (k["ql_hi"], k["ql_lo"])]
    with ExitStack() as own:
        flat = lat[:, :, :].rearrange("p t n -> p (t n)")
        ends = np.cumsum([0, H * (DN + DR), H * (DN + DV), H * D, KD * 6 * D, NT * DR, NT * DR]).tolist()
        wqb, wkvb, wov, wm, ck, sk = (flat[:, a:b] for a, b in zip(ends[:-1], ends[1:]))
        wqb = wqb[0:QL].rearrange("p (h n) -> p h n", h=H)
        wkvb = wkvb[0:KVL].rearrange("p (h n) -> p h n", h=H)
        wov = wov.rearrange("p (h n) -> p h n", h=H)
        wm = wm.rearrange("p (k n) -> p k n", k=KD)
        ck = ck.rearrange("p (t n) -> p t n", t=NT)
        sk = sk.rearrange("p (t n) -> p t n", t=NT)
        xs = sb(own, "xs", [P, NT, D])
        wa = sb(own, "wa", [P, KD, QL + KVL + DR])
        qnw = sb(own, "qnw", [QL, 1])
        kvnw = sb(own, "kvnw", [KVL, 1])
        wqb_t = sb(own, "wqb_t", [P, H, QL])
        wk_t = sb(own, "wk_t", [P, H, KVL])
        wv_t = sb(own, "wv_t", [P, H, KVL])
        wq_hi = sb(own, "wq_hi", [QL, NP, 3 * P], F32R)
        wq_lo = sb(own, "wq_lo", [QL, NP, 3 * P], F32R)
        ccol = sb(own, "ccol", [P, KD])
        csilu = sb(own, "csilu", [P, KD])
        crep = sb(own, "crep", [P, KD, P])
        stats = sb(own, "stats", [P, BT, 6])
        mv = sb(own, "mv", [P, BT, 2])
        rstd = sb(own, "rstd", [P, BT])
        junk = sb(own, "junk", [P, BT, QL + KVL])
        ms = sb(own, "ms", [P, BT, 2])
        rms = sb(own, "rms", [P, BT, 2])
        gate_place, xn_place, ht_place = (w[:, :, :].rearrange("p h n -> p (h n)") for w in (wv_t, wqb_t, wk_t))
        sign = gate_place[:, 0:2 * D].rearrange("p (a n) -> p a n", a=2)
        size = gate_place[:, 2 * D:4 * D].rearrange("p (a n) -> p a n", a=2)
        xn = xn_place[:, 0:BT * D].rearrange("p (t n) -> p t n", t=BT)
        qn = xn_place[:, BT * D:BT * (D + QL)].rearrange("p (t n) -> p t n", t=BT)
        ht = ht_place.rearrange("p (k n) -> p k n", k=KD)
        n_kk = BT * (2 * KVL + DR)
        kk = gate_place[:, 0:n_kk].rearrange("p (t n) -> p t n", t=BT)
        krot = gate_place[:, n_kk:n_kk + BT * DR].rearrange("p (t n) -> p t n", t=BT)

        ld_mod, ld_x, ld_qb, ld_kvb = sem("ld_mod"), sem("ld_x"), sem("ld_qb"), sem("ld_kvb")
        ld_o, ld_a, ld_rope, consts, wq_out = sem("ld_o"), sem("ld_a"), sem("ld_rope"), sem("consts"), sem("wq_out")
        silu_c, crep_ok, mod_mm, mod_ok, gate_ok = (sem(n) for n in ("silu_c", "crep_ok", "mod_mm", "mod_ok", "gate_ok"))
        gate_in, gate_parts, wscaled, wt_mm = sem("gate_in"), sem("gate_parts"), sem("wscaled"), sem("wt_mm")
        wt_a, wt_v, abs_mm, wqh_ok, wql_ok = sem("wt_a"), sem("wt_v"), sem("abs_mm"), sem("wqh_ok"), sem("wql_ok")
        vo_mm, vo_ok = sem("vo_mm"), sem("vo_ok")
        st_ok, mv_ok, var_ok, rstd_ok, xn_ok, xt_mm = (sem(n) for n in ("st_ok", "mv_ok", "var_ok", "rstd_ok", "xn_ok", "xt_mm"))
        ht_ok, a_mm, ms_ok, mse_ok, rms_ok, kk_v, kk_ok, kk_mm, hi_ok, lo_ok, vh_ok, vl_ok = (
            sem(n) for n in ("ht_ok", "a_mm", "ms_ok", "mse_ok", "rms_ok", "kk_v", "kk_ok", "kk_mm", "hi_ok", "lo_ok", "vh_ok", "vl_ok"))

        groups = [("q", g) for g in range(4)] + [("k", g) for g in range(2)] + [("v", g) for g in range(2)]

        def group_out(kind, g):
            if kind == "q":
                return wqb_t[:, 4 * g:4 * g + 4, :], bank[g][:, :].rearrange("p (h n) -> p h n", h=4)[:, :, 0:QL]
            n = 4 + g if kind == "k" else 6 + g
            to = wk_t if kind == "k" else wv_t
            return to[:, 8 * g:8 * g + 8, :], bank[n][:, :].rearrange("p (h n) -> p h n", h=8)

        even, odd = (wqb.rearrange("p (g two) n -> p g two n", two=2)[:, :, :, DN:].rearrange(
            "p g two (i e) -> p g two i e", e=2)[:, :, :, :, e] for e in range(2))

        def pair_cols(w, at, e):
            return w[:, :, at:at + DR].rearrange("p g (i e) -> p g i e", e=2)[:, :, :, e]

        moves = []
        for at, hd in ((KVL, 0), (P, 1)):
            moves += [(at, 0, even[:, :, hd], 1.0), (at, 1, odd[:, :, hd], 1.0)]
        for at, hd in ((2 * P, 1), (2 * P + DR, 0)):
            moves += [(at, 0, odd[:, :, hd], -1.0), (at, 1, even[:, :, hd], 1.0)]

        def abs_view(w, g, hd):
            at = 0 if hd == 0 else P + DR
            return w[:, 4 * g:4 * g + 4, at:at + KVL], bank[g][0:QL, :].rearrange(
                "p (j two n) -> p j two n", two=2, n=KVL)[:, :, hd, :]

        with nc.Block() as block:

            @block.sync
            def _(sp):
                for kd in range(KD):
                    sp.dma_start(ccol[:, kd:kd + 1], k["c"][0, kd * P:kd * P + P].rearrange("(p a) -> p a", a=1)).then_inc(ld_mod, 16)
                sp.dma_start(wm, k["wmod"].rearrange("(k p) n -> p k n", p=P)).then_inc(ld_mod, 16)
                sp.dma_start(qnw[:, :], k["q_norm"].rearrange("(p a) -> p a", a=1)).then_inc(ld_qb, 16)
                sp.dma_start(wqb, k["w_qb"].rearrange("p (h n) -> p h n", h=H)).then_inc(ld_qb, 16)
                sp.dma_start(wa[:, :, 0:QL], k["w_qa"].rearrange("(k p) n -> p k n", p=P)).then_inc(ld_a, 16)
                sp.dma_start(wa[:, :, QL:], k["w_kva"].rearrange("(k p) n -> p k n", p=P)).then_inc(ld_a, 16)
                sp.dma_start(wov, k["w_o"].rearrange("(h p) n -> p h n", p=P)).then_inc(ld_o, 16)
                sp.wait_ge(wqh_ok, 4 + len(moves))
                sp.wait_ge(wql_ok, 4 + len(moves))
                for part, w in enumerate((wq_hi, wq_lo)):
                    raw = w[:, :, :].bitcast(F32)
                    sp.dma_start(wq_dram[part, 0:NP].rearrange("g p n -> p g n"), raw).then_inc(wq_out, 16)
                    sp.dma_start(wq_dram[part, NP:NP + 1].rearrange("g p n -> p g n"), raw[:, 0:1, :]).then_inc(wq_out, 16)
                sp.wait_ge(wq_out, 64)

            @block.gpsimd
            def _(pool):
                pool.memset(ident[:, :], 0.0).then_inc(consts, 1)
                pool.memset(ident16[:, :], 0.0).then_inc(consts, 1)
                pool.memset(mask16[:, :], 0.0).then_inc(consts, 1)
                pool.memset(neg_half[:, :], -0.5).then_inc(consts, 1)
                pool.wait_ge(consts, 4)
                for m in (ident, ident16):
                    pool.affine_select(out=m[:, :], in_=m[:, :], compare_op=ALU.not_equal, fill=1.0, base=0,
                                       pattern=[[-1, P]], channel_multiplier=1).then_inc(consts, 1)
                pool.affine_select(out=mask16[:, :], in_=mask16[:, :], compare_op=ALU.is_ge, fill=MASKED, base=0,
                                   pattern=[[-1, P]], channel_multiplier=1).then_inc(consts, 1)
                with pool.Fori(0, NB) as b:
                    pool.wait_ge(var_ok, b + 1)
                    pool.tensor_tensor(out=rstd[:, :], in0=rstd[:, :], in1=neg_half[:, 0:BT], op=ALU.pow).then_inc(rstd_ok, 1)
                    pool.wait_ge(mse_ok, b + 1)
                    pool.tensor_tensor(out=rms[:, :, :].rearrange("p t n -> p (t n)"),
                                       in0=rms[:, :, :].rearrange("p t n -> p (t n)"), in1=neg_half[:, :],
                                       op=ALU.pow).then_inc(rms_ok, 1)
                    pool.wait_ge(kk_v, b * 12 + 12)
                    pool.tensor_tensor(out=kk[:, :, KVL:KVL + DR], in0=kk[:, :, KVL:KVL + DR], in1=krot[:, :, :],
                                       op=ALU.add).then_inc(kk_ok, 1)
                    vb = values[:, bass.ds(b * BT, BT), :]
                    pool.tensor_copy(vb[:, :, 0:KVL], kk[:, :, 0:KVL]).then_inc(vh_ok, 1)
                    pool.wait_ge(vh_ok, b + 1)
                    pool.tensor_tensor(out=vb[:, :, KVL:], in0=kk[:, :, 0:KVL], in1=vb[:, :, 0:KVL],
                                       op=ALU.subtract).then_inc(vl_ok, 1)

            @block.scalar
            def _(act):
                act.dma_start(xs[:, :, :], k["x"].rearrange("a (t p) d -> p (a t) d", p=P)).then_inc(ld_x, 16)
                act.dma_start(kvnw[:, :], k["kv_norm"].rearrange("(p a) -> p a", a=1)).then_inc(ld_kvb, 16)
                act.dma_start(wkvb, k["w_kvb"].rearrange("p (h n) -> p h n", h=H)).then_inc(ld_kvb, 16)
                act.dma_start(ck[:, :, :], k["cos_k"].rearrange("(t p) n -> p t n", p=P)).then_inc(ld_rope, 16)
                act.dma_start(sk[:, :, :], k["sin_k"].rearrange("(t p) n -> p t n", p=P)).then_inc(ld_rope, 16)
                for half in range(2):
                    act.dma_start(k["cos2"][half * DR:half * DR + DR, :], k["cos_t"]).then_inc(ld_rope, 16)
                    act.dma_start(k["sin2"][half * DR:half * DR + DR, :], k["sin_t"]).then_inc(ld_rope, 16)
                act.wait_ge(ld_mod, 16 * (KD + 1))
                act.activation(csilu[:, :], ccol[:, :], ACT.Silu).then_inc(silu_c, 1)
                for n, (kind, g) in enumerate(groups):
                    if n % 2 == 0:
                        act.wait_ge(wt_mm, n + 1)
                        to, of = group_out(kind, g)
                        act.activation(to, of, ACT.Copy).then_inc(wt_a, 1)
                act.wait_ge(wscaled, 2)
                for at, e, of, sgn in moves:
                    act.activation(pair_cols(wq_hi, at, e), of, ACT.Copy, scale=sgn).then_inc(wqh_ok, 1)
                for g in range(2):
                    act.wait_ge(abs_mm, g + 1)
                    for hd in range(2):
                        to, of = abs_view(wq_hi, g, hd)
                        act.activation(to, of, ACT.Copy).then_inc(wqh_ok, 1)
                act.wait_ge(mod_ok, 2)
                with act.Fori(0, NB) as b:
                    for kd in range(KD):
                        act.wait_ge(xt_mm, b * KD + kd + 1)
                        act.activation(ht[:, kd, :], bank[kd][:, :], ACT.Identity, scale=modc[:, 1, kd:kd + 1],
                                       bias=modc[:, 0, kd:kd + 1]).then_inc(ht_ok, 1)
                    for t in range(BT):
                        act.wait_ge(a_mm, b * BT + t + 1)
                        of = bank[2 + t][:, :]
                        for n, (a, w) in enumerate(((0, QL), (QL, KVL))):
                            act.activation(junk[:, t, a:a + w], of[:, a:a + w], ACT.Square, scale=1.0 / math.sqrt(w),
                                           accum_out=ms[:, t, n:n + 1]).then_inc(ms_ok, 1)
                    for n, (hi, _) in enumerate(kt):
                        act.wait_ge(kk_mm, b * 3 + n + 1)
                        rows = QL if n == 2 else P
                        act.activation(hi[:, bass.ds(b * BW, BW)], bank[(6, 7, 0)[n]][0:rows, :], ACT.Copy).then_inc(hi_ok, 1)

            @block.vector
            def _(dve):
                dve.wait_ge(silu_c, 1)
                for kd in range(KD):
                    dve.tensor_copy(crep[:, kd, :], csilu[:, kd:kd + 1].to_broadcast([P, P])).then_inc(crep_ok, 1)
                dve.wait_ge(ld_kvb, 32)
                dve.tensor_scalar(wkvb, wkvb, kvnw[:, :], None, ALU.mult).then_inc(wscaled, 1)
                dve.wait_ge(ld_qb, 32)
                dve.tensor_scalar(wqb, wqb, qnw[:, :], SCALE, ALU.mult, ALU.mult).then_inc(wscaled, 1)
                dve.wait_ge(mod_mm, 1)
                dve.tensor_copy(modc[:, :, :], bank[0][:, 0:4 * KD].rearrange("p (j k) -> p j k", k=KD)).then_inc(mod_ok, 1)
                dve.wait_ge(mod_ok, 1)
                odd_rows = modc[:, :, :].rearrange("p (a two) k -> p a two k", two=2)[:, :, 1, :]
                dve.tensor_scalar(odd_rows, odd_rows, 1.0, None, ALU.add).then_inc(mod_ok, 1)
                dve.wait_ge(mod_mm, 2)
                dve.tensor_copy(gates[:, :, :].rearrange("p a n -> p (a n)"), bank[1][:, :]).then_inc(gate_in, 1)
                dve.wait_ge(gate_in, 1)
                dve.tensor_scalar(sign[:, :, :], gates[:, :, :], 0.0, 2.0, ALU.is_ge, ALU.mult).then_inc(gate_parts, 1)
                dve.scalar_tensor_tensor(out=size[:, :, :], in0=gates[:, :, :], scalar=-1.0, in1=gates[:, :, :],
                                         op0=ALU.mult, op1=ALU.max).then_inc(gate_parts, 1)
                dve.wait_ge(gate_parts, 2)
                dve.tensor_scalar(size[:, :, :], size[:, :, :], 0.25, None, ALU.max).then_inc(gate_parts, 1)
                dve.wait_ge(gate_parts, 3)
                dve.scalar_tensor_tensor(out=gates[:, :, :], in0=sign[:, :, :], scalar=-1.0, in1=size[:, :, :],
                                         op0=ALU.add, op1=ALU.mult).then_inc(gate_ok, 1)
                for n, (kind, g) in enumerate(groups):
                    if n % 2 == 1:
                        dve.wait_ge(wt_mm, n + 1)
                        to, of = group_out(kind, g)
                        dve.tensor_copy(to, of).then_inc(wt_v, 1)
                for n, (at, e, of, sgn) in enumerate(moves):
                    dve.wait_ge(wqh_ok, n + 1)
                    hi = pair_cols(wq_hi, at, e).bitcast(F32)
                    dve.scalar_tensor_tensor(out=pair_cols(wq_lo, at, e), in0=of, scalar=sgn, in1=hi, op0=ALU.mult,
                                             op1=ALU.subtract).then_inc(wql_ok, 1)
                for g in range(2):
                    for hd in range(2):
                        dve.wait_ge(wqh_ok, len(moves) + 2 * g + 2)
                        to, of = abs_view(wq_lo, g, hd)
                        hi, _ = abs_view(wq_hi, g, hd)
                        dve.tensor_tensor(out=to, in0=of, in1=hi.bitcast(F32), op=ALU.subtract).then_inc(wql_ok, 1)
                dve.wait_ge(gate_ok, 1)
                for n in range(NP // 2):
                    dve.wait_ge(vo_mm, n + 1)
                    dve.tensor_tensor(out=w_vo[:, 2 * n:2 * n + 2, :], in0=bank[2 + n][:, :].rearrange("p (a n) -> p a n", a=2),
                                      in1=gates[:, 0:1, :].to_broadcast([P, 2, D]), op=ALU.mult).then_inc(vo_ok, 1)
                dve.wait_ge(ld_x, 16)
                dve.wait_ge(ld_rope, 96)
                with dve.Fori(0, NB) as b:
                    xb = xs[:, bass.ds(b * BT, BT), :]
                    for t in range(BT):
                        dve.bn_stats(stats[:, t, :], xb[:, t, :]).then_inc(st_ok, 1)
                    dve.wait_ge(st_ok, b * BT + BT)
                    dve.memset(turnstile[:, :], 0.0)
                    for t in range(BT):
                        dve.bn_aggr(mv[:, t, :], stats[:, t, :]).then_inc(mv_ok, 1)
                    dve.wait_ge(mv_ok, b * BT + BT)
                    dve.tensor_scalar(rstd[:, :], mv[:, :, 1], LN_EPS, None, ALU.add).then_inc(var_ok, 1)
                    dve.wait_ge(rstd_ok, b + 1)
                    for t in range(BT):
                        dve.tensor_scalar(xn[:, t, :], xb[:, t, :], mv[:, t, 0:1], rstd[:, t:t + 1], ALU.subtract,
                                          ALU.mult).then_inc(xn_ok, 1)
                    dve.wait_ge(ms_ok, b * 2 * BT + 2 * BT)
                    dve.tensor_scalar(rms[:, :, :], ms[:, :, :], RMS_EPS, None, ALU.add).then_inc(mse_ok, 1)
                    dve.wait_ge(rms_ok, b + 1)
                    for t in range(BT):
                        of = bank[2 + t][:, :]
                        dve.tensor_scalar(qn[:, t, :], of[:, 0:QL], rms[:, t, 0:1], None, ALU.mult)
                        for at in (0, KVL + DR):
                            dve.tensor_scalar(kk[:, t, at:at + KVL], of[:, QL:QL + KVL], rms[:, t, 1:2], None, ALU.mult)
                        rope = of[:, QL + KVL:QL + KVL + DR]
                        ckt = ck[:, bass.ds(b * BT + t, 1), :].rearrange("p a n -> p (a n)")
                        skt = sk[:, bass.ds(b * BT + t, 1), :].rearrange("p a n -> p (a n)").rearrange("p (i e) -> p i e", e=2)
                        dve.tensor_tensor(out=kk[:, t, KVL:KVL + DR], in0=rope, in1=ckt, op=ALU.mult).then_inc(kk_v, 1)
                        swapped = rope.rearrange("p (i e) -> p i e", e=2)
                        to = krot[:, t, :].rearrange("p (i e) -> p i e", e=2)
                        for e in range(2):
                            dve.tensor_tensor(out=to[:, :, e], in0=swapped[:, :, 1 - e], in1=skt[:, :, e],
                                              op=ALU.mult).then_inc(kk_v, 1)
                    for n, (hi, lo) in enumerate(kt):
                        dve.wait_ge(hi_ok, b * 3 + n + 1)
                        rows = QL if n == 2 else P
                        at = bass.ds(b * BW, BW)
                        dve.tensor_tensor(out=lo[:, at], in0=bank[(6, 7, 0)[n]][0:rows, :], in1=hi[:, at].bitcast(F32),
                                          op=ALU.subtract).then_inc(lo_ok, 1)

            @block.tensor
            def _(pe):
                pe.wait_ge(ld_mod, 16 * (KD + 1))
                pe.wait_ge(silu_c, 1)
                for j, part in enumerate((0, 1, 3, 4)):
                    for kd in range(KD):
                        at = part * D + kd * P
                        for kk_ in range(KD):
                            last = pe.matmul(bank[0][:, j * KD + kd:j * KD + kd + 1], wm[:, kk_, at:at + P],
                                             csilu[:, kk_:kk_ + 1], start=(kk_ == 0), stop=(kk_ == KD - 1))
                last.then_inc(mod_mm, 1)
                pe.wait_ge(crep_ok, KD)
                for j, part in enumerate((2, 5)):
                    for kk_ in range(KD):
                        last = pe.matmul(bank[1][:, j * D:j * D + D], crep[:, kk_, :], wm[:, kk_, part * D:part * D + D],
                                         start=(kk_ == 0), stop=(kk_ == KD - 1))
                last.then_inc(mod_mm, 1)
                pe.wait_ge(consts, 7)
                pe.wait_ge(wscaled, 2)
                pe.wait_ge(mod_ok, 1)
                pe.wait_ge(gate_ok, 1)
                for kind, g in groups:
                    n, step, rows, of = {"q": (g, 4, QL, wqb), "k": (4 + g, 8, KVL, wkvb), "v": (6 + g, 8, KVL, wkvb)}[kind]
                    at = DN if kind == "v" else 0
                    for j in range(step):
                        last = pe.transpose(bank[n][:, j * (BW // step):j * (BW // step) + rows],
                                            of[:, step * g + j, at:at + P], ident[0:rows, 0:rows])
                    last.then_inc(wt_mm, 1)
                pe.wait_ge(wt_a, 4)
                pe.wait_ge(wt_v, 4)
                for g in range(2):
                    for j in range(8):
                        last = pe.matmul(bank[g][0:QL, j * KVL:j * KVL + KVL], wqb_t[:, 8 * g + j, :], wk_t[:, 8 * g + j, :],
                                         start=True, stop=True)
                    last.then_inc(abs_mm, 1)
                pe.wait_ge(ld_o, 16)
                for n in range(NP // 2):
                    for j in range(4):
                        h = 4 * n + j
                        last = pe.matmul(bank[2 + n][(h % 2) * KVL:(h % 2) * KVL + KVL, (j // 2) * D:(j // 2) * D + D],
                                         wv_t[:, h, :], wov[:, h, :], start=True, stop=True)
                    last.then_inc(vo_mm, 1)
                pe.wait_ge(wql_ok, 4 + len(moves))
                pe.wait_ge(vo_ok, NP // 2)
                pe.wait_ge(ld_a, 32)
                with pe.Fori(0, NB) as b:
                    pe.wait_ge(xn_ok, b * BT + BT)
                    for kd in range(KD):
                        for t in range(BT):
                            last = pe.transpose(bank[kd][:, t * P:t * P + P], xn[:, t, kd * P:kd * P + P], ident[:, :])
                        last.then_inc(xt_mm, 1)
                    pe.wait_ge(ht_ok, b * KD + KD)
                    for t in range(BT):
                        for kd in range(KD):
                            last = pe.matmul(bank[2 + t][:, 0:QL + KVL + DR], ht[:, kd, t * P:t * P + P], wa[:, kd, :],
                                             start=(kd == 0), stop=(kd == KD - 1))
                        last.then_inc(a_mm, 1)
                    pe.wait_ge(kk_ok, b + 1)
                    for n, at in enumerate((0, KVL)):
                        for t in range(BT):
                            last = pe.transpose(bank[6 + n][:, t * P:t * P + P], kk[:, t, at:at + P], ident[:, :])
                        last.then_inc(kk_mm, 1)
                    for t in range(BT):
                        last = pe.transpose(bank[0][0:QL, t * P:t * P + P], qn[:, t, :], ident[:, :])
                    last.then_inc(kk_mm, 1)


def attend(nc, sb, sem, k):
    bank, lat, rowsum, ident, wq_dram, values = k["bank"], k["lat"], k["rowsum"], k["ident"], k["wq_dram"], k["values"]
    cos2, sin2, ident16, mask16 = k["cos2"], k["sin2"], k["ident16"], k["mask16"]
    kt_hi, kt_lo = (k["kt_a_hi"], k["kt_b_hi"]), (k["kt_a_lo"], k["kt_b_lo"])
    ql = (k["ql_hi"], k["ql_lo"])
    s_bank, t_bank, o_bank = bank[0:S_RING], bank[S_RING:S_RING + 2], bank[S_RING + 2]
    with ExitStack() as own:
        wq = [sb(own, f"wq_pair_{p}", [QL, 3 * P], F32R) for p in ("hi", "lo")]
        q_hi = sb(own, "q_hi", [P, 2, 2, BW], F32R)
        q_lo = sb(own, "q_lo", [P, 2, 2, BW], F32R)
        qf = sb(own, "qf", [P, 2, BW])
        qs = sb(own, "qs", [P, BW])
        probs = sb(own, "probs", [P, P_RING, BW])
        pt = sb(own, "pt", [P, PT_RING, BW])
        pt_lo = sb(own, "pt_lo", [P, PT_RING, BW], F16)
        mx = sb(own, "mx", [P, MX_RING, 4])
        nmx = sb(own, "nmx", [P, MX_RING])
        shift = sb(own, "shift", [P, MX_RING])

        wq_in = sem("wq_in")
        q_sum = sem("q_sum")
        q_hi_ok = sem("q_hi_ok")
        q_lo_ok = sem("q_lo_ok")
        sc_done = sem("sc_done")
        chunk_max = sem("chunk_max")
        row_max = sem("row_max")
        max_ok = sem("max_ok")
        exp_done = sem("exp_done")
        use_done = sem("use_done")
        bank_read = {e: sem(f"bank_read_{e}") for e in "av"}
        low_ok = {e: sem(f"low_ok_{e}") for e in "vp"}
        pv_done = sem("pv_done")
        sum_read = sem("sum_read")
        zeroed = sem("zeroed")

        def wait_read(eng, hp, n):
            e, steps = reader(USES[n % NU])
            before = reads(e, n % NU) - (READS[e] if n < 0 else 0)
            eng.wait_ge(bank_read[e], hp * READS[e] + (BASE_READS[e] + before + steps))

        def bank_of(use):
            return t_bank[use % 2]

        def query_products(pe, c, part, use):
            w = [wq[p][:, part * P:part * P + P] for p in range(2)]
            x = [ql[p][:, c * BW:c * BW + BW] for p in range(2)]
            for n, (a, b) in enumerate(((0, 0), (0, 1), (1, 0))):
                last = pe.matmul(bank_of(use)[:, :], w[a], x[b], start=(n == 0), stop=(n == 2))
            last.then_inc(use_done, 1)

        def query_rotation(dve, c, use, done, read):
            at = slice(c * BW, c * BW + BW)
            for part, rot, rest in ((0, slice(DR, P), slice(0, DR)), (1, slice(0, DR), slice(DR, P))):
                dve.wait_ge(use_done, done + part + 1)
                of = bank_of(use + part)
                dve.tensor_tensor(out=qf[rot, part, :], in0=of[rot, :], in1=cos2[rot, at], op=ALU.mult).then_inc(bank_read["v"], 1)
                dve.tensor_copy(qf[rest, part, :], of[rest, :]).then_inc(bank_read["v"], 1)
            dve.wait_ge(use_done, done + 3)
            dve.tensor_tensor(out=qs[:, :], in0=bank_of(use + 2)[:, :], in1=sin2[:, at], op=ALU.mult).then_inc(bank_read["v"], 1)
            dve.wait_ge(bank_read["v"], read)
            for hd, rot in ((0, slice(DR, P)), (1, slice(0, DR))):
                dve.tensor_tensor(out=qf[rot, hd, :], in0=qf[rot, hd, :], in1=qs[rot, :], op=ALU.add).then_inc(q_sum, 1)

        def query_high(act, c, n):
            for hd in range(2):
                act.wait_ge(q_sum, n * 2 + (hd + 1))
                act.activation(q_hi[:, c % 2, hd, :], qf[:, hd, :], ACT.Copy).then_inc(q_hi_ok, 1)

        def query_low(pool, c, n):
            for hd in range(2):
                pool.wait_ge(q_hi_ok, n * 2 + (hd + 1))
                pool.tensor_tensor(out=q_lo[:, c % 2, hd, :], in0=qf[:, hd, :], in1=q_hi[:, c % 2, hd, :].bitcast(F32),
                                   op=ALU.subtract).then_inc(q_lo_ok, 1)

        with nc.Block() as block:

            @block.sync
            def _(sp):
                for part in range(2):
                    sp.dma_start(wq[part][:, :].bitcast(F32), wq_dram[part, 0]).then_inc(wq_in, 16)
                with sp.Fori(0, NP) as hp:
                    sp.wait_ge(use_done, hp * NU + (BASE_USES + USE["q", 2, 2] + 1))
                    for part in range(2):
                        sp.dma_start(wq[part][:, :].bitcast(F32),
                                     wq_dram[part, bass.ds(hp + 1, 1)].rearrange("g p n -> (g p) n")).then_inc(wq_in, 16)
                sp.wait_ge(wq_in, 32 * (NP + 1))

            @block.gpsimd
            def _(pool):
                pool.memset(rowsum[:, :, :, :], 0.0).then_inc(zeroed, 1)
                query_low(pool, 0, 0)
                with pool.Fori(0, NP) as hp:
                    for r in ROUNDS:
                        for s in chunks_of(r - 1):
                            if not low_on_vector(s):
                                wait_read(pool, hp, USE["t", s])
                                full = pt[:, s % PT_RING, 0:CHUNKS[s][2] * P]
                                pool.tensor_tensor(out=pt_lo[:, s % PT_RING, 0:CHUNKS[s][2] * P], in0=full, in1=cut(full),
                                                   op=ALU.subtract).then_inc(low_ok["p"], 1)
                        if r in PREP_ROUND:
                            c = PREP_ROUND[r]
                            query_low(pool, (c + 1) % 4, hp * 4 + (c + 1))

            @block.scalar
            def _(act):
                act.sem_inc(exp_done, CREDIT)
                act.sem_inc(bank_read["a"], CREDIT)
                act.wait_ge(zeroed, 1)
                query_high(act, 0, 0)

                def exponentials(hp, s):
                    item, c, n = CHUNKS[s]
                    i, h = ITEMS[item]
                    act.wait_ge(max_ok, hp * NI + (item + 1))
                    u = USE["t", (s - P_RING) % NC] - (NU if s < P_RING else 0)
                    act.wait_ge(use_done, hp * NU + (BASE_USES + u + 1))
                    act.activation(probs[:, s % P_RING, 0:n * P], s_bank[s % S_RING][:, 0:n * P], ACT.Exp,
                                   bias=shift[:, item % MX_RING:item % MX_RING + 1],
                                   accum_out=rowsum[:, i, bass.ds(hp * 2 + h, 1), c]).then_inc(exp_done, 1)

                def evacuate(hp, s):
                    u, n = USE["t", s], CHUNKS[s][2]
                    act.wait_ge(use_done, hp * NU + (BASE_USES + u + 1))
                    act.wait_ge(pv_done, hp * NC + (CREDIT + s - PT_RING + 1))
                    act.activation(pt[:, s % PT_RING, 0:n * P], bank_of(u)[:, 0:n * P], ACT.Copy).then_inc(bank_read["a"], 1)

                with act.Fori(0, NP) as hp:
                    for r in ROUNDS:
                        moves = [s for s in chunks_of(r - 1) if not evac_on_vector(s)]
                        for s in moves[:2]:
                            evacuate(hp, s)
                        moves = moves[2:]
                        for s in chunks_of(r):
                            exponentials(hp, s)
                            if moves:
                                evacuate(hp, moves.pop(0))
                        for s in moves:
                            evacuate(hp, s)
                        if r in PREP_ROUND:
                            c = PREP_ROUND[r]
                            query_high(act, (c + 1) % 4, hp * 4 + (c + 1))

            @block.vector
            def _(dve):
                dve.sem_inc(bank_read["v"], CREDIT)
                dve.sem_inc(sum_read, 1)
                query_rotation(dve, 0, -3, CREDIT, BASE_READS["v"])

                def maximum(hp, item):
                    n_chunks, slot = len(chunks_of(item)), item % MX_RING
                    for s in chunks_of(item):
                        _, c, n = CHUNKS[s]
                        of = s_bank[s % S_RING][:, 0:n * P]
                        dve.wait_ge(sc_done, hp * NC + (s + 1))
                        if n_chunks > 1:
                            dve.tensor_reduce(out=mx[:, slot, c:c + 1], in_=of, axis=AXX, op=ALU.max).then_inc(chunk_max, 1)
                        else:
                            dve.tensor_reduce(out=nmx[:, slot:slot + 1], in_=of, axis=AXX, op=ALU.max,
                                              negate=True).then_inc(row_max, 1)
                    if n_chunks > 1:
                        dve.wait_ge(chunk_max, hp * len(MANY) + (MANY.index(FIRST[item + 1] - 1) + 1))
                        dve.tensor_reduce(out=nmx[:, slot:slot + 1], in_=mx[:, slot, 0:n_chunks], axis=AXX, op=ALU.max,
                                          negate=True).then_inc(row_max, 1)
                    dve.wait_ge(row_max, hp * NI + (item + 1))
                    dve.tensor_scalar(shift[:, slot:slot + 1], nmx[:, slot:slot + 1], P_SHIFT, None, ALU.add).then_inc(max_ok, 1)

                with dve.Fori(0, NP) as hp:
                    for r in ROUNDS:
                        if r < NI:
                            maximum(hp, r)
                        for s in chunks_of(r - 1):
                            u, n = USE["t", s], CHUNKS[s][2]
                            full = pt[:, s % PT_RING, 0:n * P]
                            if evac_on_vector(s):
                                dve.wait_ge(use_done, hp * NU + (BASE_USES + u + 1))
                                dve.wait_ge(pv_done, hp * NC + (CREDIT + s - PT_RING + 1))
                                dve.tensor_copy(full, bank_of(u)[:, 0:n * P]).then_inc(bank_read["v"], 1)
                            if low_on_vector(s):
                                wait_read(dve, hp, u)
                                dve.tensor_tensor(out=pt_lo[:, s % PT_RING, 0:n * P], in0=full, in1=cut(full),
                                                  op=ALU.subtract).then_inc(low_ok["v"], 1)
                        if r >= 2:
                            i, h = ITEMS[r - 2]
                            dve.wait_ge(pv_done, hp * NC + (CREDIT + FIRST[r - 1]))
                            dve.tensor_reduce(out=lat[:, i, bass.ds(hp * (2 * KVL) + h * KVL, KVL)],
                                              in_=o_bank[:, 0:2 * KVL].rearrange("p (a n) -> p n a", a=2), axis=AXX,
                                              op=ALU.add).then_inc(sum_read, 1)
                        if r in PREP_ROUND:
                            c = PREP_ROUND[r]
                            use = USE["q", c, 0]
                            dve.wait_ge(q_lo_ok, hp * 8 + (2 * (c + 1)))
                            read = hp * READS["v"] + (BASE_READS["v"] + reads("v", use + 3))
                            query_rotation(dve, (c + 1) % 4, use, hp * NU + (BASE_USES + use), read)

            @block.tensor
            def _(pe):
                pe.sem_inc(use_done, CREDIT)
                pe.sem_inc(pv_done, CREDIT)
                pe.wait_ge(wq_in, 32)
                for part in range(3):
                    if part == 2:
                        pe.wait_ge(bank_read["v"], CREDIT + PREP_READS[0])
                    query_products(pe, 0, part, part - 3)
                pe.wait_ge(bank_read["v"], BASE_READS["v"])

                def scores(hp, item):
                    i, h = ITEMS[item]
                    tok = (i % 4) * P
                    q = [w[:, (i // 4) % 2, h, tok:tok + P] for w in (q_hi, q_lo)]
                    if i % 4 == 0 and h == 0:
                        pe.wait_ge(q_lo_ok, hp * 8 + (2 * (i // 4) + 2))
                    for s in chunks_of(item):
                        _, c, n = CHUNKS[s]
                        to = s_bank[s % S_RING]
                        cols = max(n * P, 2 * P)
                        at = slice(c * BW, c * BW + cols)
                        keys = [kt_hi[h][:, at], kt_lo[h][:, at]]
                        last_chunk = s == FIRST[item + 1] - 1
                        pe.wait_ge(exp_done, hp * NC + (CREDIT + s - S_RING + 1))
                        for m, (a, b) in enumerate(((0, 0), (0, 1), (1, 0))):
                            last = pe.matmul(to[:, 0:cols], q[a], keys[b], start=(m == 0), stop=(m == 2 and not last_chunk))
                        if last_chunk:
                            last = pe.matmul(to[:, (n - 1) * P:n * P], ident16[:, :], mask16[:, :], start=False, stop=True)
                        last.then_inc(sc_done, 1)

                def transpose(hp, s):
                    u, n = USE["t", s], CHUNKS[s][2]
                    pe.wait_ge(exp_done, hp * NC + (CREDIT + s + 1))
                    wait_read(pe, hp, u - 2)
                    for j in range(n):
                        last = pe.transpose(bank_of(u)[:, j * P:j * P + P], probs[:, s % P_RING, j * P:j * P + P], ident[:, :])
                    last.then_inc(use_done, 1)

                def weigh(hp, s):
                    item, c, n = CHUNKS[s]
                    e = "v" if low_on_vector(s) else "p"
                    pe.wait_ge(low_ok[e], hp * LOWS[e] + lows(e, s + 1))
                    if s == FIRST[item]:
                        pe.wait_ge(sum_read, hp * NI + (item + 1))
                    for j in range(n):
                        key = 4 * c + j
                        high = cut(pt[:, s % PT_RING, j * P:j * P + P])
                        end = s == FIRST[item + 1] - 1 and j == n - 1
                        pe.matmul(o_bank[:, 0:2 * KVL], high, values[:, key, :], start=(c == 0 and j == 0), stop=False)
                        last = pe.matmul(o_bank[:, 0:KVL], pt_lo[:, s % PT_RING, j * P:j * P + P], values[:, key, 0:KVL],
                                         start=False, stop=end)
                    last.then_inc(pv_done, 1)

                with pe.Fori(0, NP) as hp:
                    for r in ROUNDS:
                        if r < NI:
                            scores(hp, r)
                        new, old = chunks_of(r - 1), chunks_of(r - 2)
                        for s in new[:2]:
                            transpose(hp, s)
                        for s in old[:2]:
                            weigh(hp, s)
                        new, old = new[2:], old[2:]
                        while new or old:
                            if new:
                                transpose(hp, new.pop(0))
                            if old:
                                weigh(hp, old.pop(0))
                        if r in PREP_ROUND:
                            c = PREP_ROUND[r]
                            if c == 3:
                                pe.wait_ge(wq_in, hp * 32 + 64)
                            for part in range(3):
                                use = USE["q", c, part]
                                wait_read(pe, hp, use - 2)
                                query_products(pe, (c + 1) % 4, part, use)


def cut(a):
    return a.bitcast(BF16).rearrange("p (n e) -> p n e", e=2)[:, :, 1]


def experts(nc, sb, sem, k):
    bank, lat, rowsum, ident, gates = k["bank"], k["lat"], k["rowsum"], k["ident"], k["gates"]
    modc, neg_half, w_vo, turnstile = k["modc"], k["neg_half"], k["w_vo"], k["turnstile"]
    with ExitStack() as own:
        xs = sb(own, "xs_again", [P, NT, D])
        wi = [sb(own, f"wi_{n}", [P, KD, E, M]) for n in range(2)]
        wo = sb(own, "wo_sb", [P, E, D])
        wg = sb(own, "wg", [P, KD, E])
        den = sb(own, "den", [P, BT, H])
        rden = sb(own, "rden", [P, BT, H])
        lat_n = sb(own, "lat_n", [P, 2, H, KVL])
        lat_t = sb(own, "lat_t", [P, 2, NP, P])
        y = sb(own, "y", [P, BT, D])
        stats = sb(own, "stats2", [P, BT, 6])
        mv = sb(own, "mv2", [P, BT, 2])
        rstd = sb(own, "rstd2", [P, BT])
        xn = sb(own, "xn2", [P, BT, D])
        ht = sb(own, "ht2", [P, KD, BW])
        places = sb(own, "places", [P, E], mybir.dt.int32)
        placesf = sb(own, "placesf", [P, E])
        logits = sb(own, "logits", [P, BT, E])
        top = sb(own, "top", [P, BT, 8])
        top_at = sb(own, "top_at", [P, BT, 8], U32)
        top_f = sb(own, "top_f", [P, BT, 2])
        gap = sb(own, "gap", [P, BT])
        ratio = sb(own, "ratio", [P, BT])
        total = sb(own, "total", [P, BT])
        first_w = sb(own, "first_w", [P, BT])
        second_w = sb(own, "second_w", [P, BT])
        route = sb(own, "route", [P, BT, E])
        route2 = sb(own, "route2", [P, BT, E])
        silu = sb(own, "silu", [P, 2, BW])
        inner = sb(own, "inner", [P, 2, BW])

        names = ("x2_in wi_in wo_in wg_in place_i place_f wo_ok den_ok rden_ok latn_ok latt_mm latt_ok att_mm y_ok st2_ok mv2_ok "
                 "var2_ok rstd2_ok xn2_ok xt2_mm ht2_ok lg_mm lg_ok top_ok at_ok gap_ok ratio_ok tot_ok w1_ok w2_ok topf_ok "
                 "route_a route_ok up_mm silu_ok inner_ok down_mm down_read out_ok").split()
        q = {n: sem(n) for n in names}

        with nc.Block() as block:

            @block.sync
            def _(sp):
                sp.dma_start(xs[:, :, :], k["x"].rearrange("a (t p) d -> p (a t) d", p=P)).then_inc(q["x2_in"], 16)
                sp.dma_start(wg[:, :, :], k["w_gate"].rearrange("(k p) e -> p k e", p=P)).then_inc(q["wg_in"], 16)
                sp.dma_start(wo[:, :, :], k["wo"].rearrange("e p d -> p e d")).then_inc(q["wo_in"], 16)
                for n, w in enumerate(("wi_0", "wi_1")):
                    for kd in range(KD):
                        sp.dma_start(wi[n][:, kd], k[w].rearrange("e (k p) m -> k p e m", p=P)[kd]).then_inc(q["wi_in"], 16)
                rows = k["out"].rearrange("a (t p) d -> p (a t) d", p=P)
                with sp.Fori(0, NB) as b:
                    sp.wait_ge(q["down_read"], b * (BT * E) + BT * E)
                    sp.dma_start(rows[:, bass.ds(b * BT, BT), :], y[:, :, :]).then_inc(q["out_ok"], 16)
                sp.wait_ge(q["out_ok"], 16 * NB)

            @block.gpsimd
            def _(pool):
                pool.iota(places[:, :], pattern=[[1, E]], base=0, channel_multiplier=0).then_inc(q["place_i"], 1)
                pool.wait_ge(q["place_i"], 1)
                pool.tensor_copy(placesf[:, :], places[:, :]).then_inc(q["place_f"], 1)
                pool.wait_ge(q["wo_in"], 16)
                for e in range(E):
                    pool.tensor_tensor(out=wo[:, e, :], in0=wo[:, e, :], in1=gates[:, 1, :], op=ALU.mult).then_inc(q["wo_ok"], 1)
                with pool.Fori(0, NB) as b:
                    pool.wait_ge(q["var2_ok"], b + 1)
                    pool.tensor_tensor(out=rstd[:, :], in0=rstd[:, :], in1=neg_half[:, 0:BT], op=ALU.pow).then_inc(q["rstd2_ok"], 1)

            @block.scalar
            def _(act):
                with act.Fori(0, NB) as b:
                    for t in range(BT):
                        for half in range(2):
                            act.wait_ge(q["latt_mm"], b * 8 + (2 * t + half + 1))
                            if t >= 2:
                                act.wait_ge(q["att_mm"], b * BT + (t - 1))
                            act.activation(lat_t[:, t % 2, 4 * half:4 * half + 4, :],
                                           bank[half][:, :].rearrange("p (j n) -> p j n", n=P), ACT.Copy).then_inc(q["latt_ok"], 1)
                    for kd in range(KD):
                        act.wait_ge(q["xt2_mm"], b * KD + (kd + 1))
                        act.activation(ht[:, kd, :], bank[4 + kd][:, :], ACT.Identity, scale=modc[:, 3, kd:kd + 1],
                                       bias=modc[:, 2, kd:kd + 1]).then_inc(q["ht2_ok"], 1)
                    act.wait_ge(q["gap_ok"], b + 1)
                    act.activation(ratio[:, :], gap[:, :], ACT.Exp).then_inc(q["ratio_ok"], 1)
                    for e in range(E):
                        act.wait_ge(q["up_mm"], b * E + (e + 1))
                        if e >= 2:
                            act.wait_ge(q["inner_ok"], b * E + (e - 1))
                        act.activation(silu[:, e % 2, :], bank[(0, 6)[e % 2]][:, :], ACT.Silu).then_inc(q["silu_ok"], 1)

            @block.vector
            def _(dve):
                dve.wait_ge(q["x2_in"], 16)
                dve.wait_ge(q["place_f"], 1)
                with dve.Fori(0, NB) as b:
                    dve.tensor_reduce(out=den[:, :, :], in_=rowsum[:, bass.ds(b * BT, BT), :, :], axis=AXX,
                                      op=ALU.add).then_inc(q["den_ok"], 1)
                    dve.wait_ge(q["den_ok"], b + 1)
                    dve.reciprocal(rden[:, :, :], den[:, :, :]).then_inc(q["rden_ok"], 1)
                    dve.wait_ge(q["rden_ok"], b + 1)
                    for t in range(BT):
                        if t >= 2:
                            dve.wait_ge(q["latt_mm"], b * 8 + (2 * t - 2))
                        dve.tensor_tensor(out=lat_n[:, t % 2], in0=lat[:, bass.ds(b * BT + t, 1), :].rearrange(
                            "p a (h n) -> p (a h) n", h=H), in1=rden[:, t, :].unsqueeze(2).to_broadcast([P, H, KVL]),
                            op=ALU.mult).then_inc(q["latn_ok"], 1)
                    with_x = xs[:, bass.ds(b * BT, BT), :]
                    for t in range(BT):
                        dve.wait_ge(q["att_mm"], b * BT + (t + 1))
                        dve.tensor_tensor(out=y[:, t, :], in0=bank[2 + t % 2][:, 0:D], in1=with_x[:, t, :],
                                          op=ALU.add).then_inc(q["y_ok"], 1)
                    for t in range(BT):
                        dve.wait_ge(q["y_ok"], b * BT + (t + 1))
                        dve.bn_stats(stats[:, t, :], y[:, t, :]).then_inc(q["st2_ok"], 1)
                    dve.wait_ge(q["st2_ok"], b * BT + BT)
                    dve.memset(turnstile[:, :], 0.0)
                    for t in range(BT):
                        dve.bn_aggr(mv[:, t, :], stats[:, t, :]).then_inc(q["mv2_ok"], 1)
                    dve.wait_ge(q["mv2_ok"], b * BT + BT)
                    dve.tensor_scalar(rstd[:, :], mv[:, :, 1], LN_EPS, None, ALU.add).then_inc(q["var2_ok"], 1)
                    dve.wait_ge(q["rstd2_ok"], b + 1)
                    for t in range(BT):
                        dve.tensor_scalar(xn[:, t, :], y[:, t, :], mv[:, t, 0:1], rstd[:, t:t + 1], ALU.subtract,
                                          ALU.mult).then_inc(q["xn2_ok"], 1)
                    dve.wait_ge(q["lg_mm"], b + 1)
                    dve.tensor_copy(logits[:, :, :], bank[3][:, 0:BT * E].rearrange("p (t e) -> p t e", e=E)).then_inc(q["lg_ok"], 1)
                    dve.wait_ge(q["lg_ok"], b + 1)
                    dve.memset(turnstile[:, :], 0.0)
                    for t in range(BT):
                        dve.max(top[:, t, :], logits[:, t, :]).then_inc(q["top_ok"], 1)
                    dve.wait_ge(q["top_ok"], b * BT + BT)
                    dve.tensor_tensor(out=gap[:, :], in0=top[:, :, 1], in1=top[:, :, 0], op=ALU.subtract).then_inc(q["gap_ok"], 1)
                    for t in range(BT):
                        dve.max_index(top_at[:, t, :], top[:, t, :], logits[:, t, :]).then_inc(q["at_ok"], 1)
                    dve.wait_ge(q["at_ok"], b * BT + BT)
                    dve.tensor_copy(top_f[:, :, :], top_at[:, :, 0:2]).then_inc(q["topf_ok"], 1)
                    dve.wait_ge(q["ratio_ok"], b + 1)
                    dve.tensor_scalar(total[:, :], ratio[:, :], 1.0, None, ALU.add).then_inc(q["tot_ok"], 1)
                    dve.wait_ge(q["tot_ok"], b + 1)
                    dve.reciprocal(first_w[:, :], total[:, :]).then_inc(q["w1_ok"], 1)
                    dve.wait_ge(q["w1_ok"], b + 1)
                    dve.tensor_tensor(out=second_w[:, :], in0=ratio[:, :], in1=first_w[:, :], op=ALU.mult).then_inc(q["w2_ok"], 1)
                    dve.wait_ge(q["topf_ok"], b + 1)
                    dve.wait_ge(q["w2_ok"], b + 1)
                    for t in range(BT):
                        for n, (to, w) in enumerate(((route, first_w), (route2, second_w))):
                            dve.tensor_scalar(to[:, t, :], placesf[:, :], top_f[:, t, n:n + 1], w[:, t:t + 1], ALU.is_equal,
                                              ALU.mult).then_inc(q["route_a"], 1)
                    dve.wait_ge(q["route_a"], b * (2 * BT) + 2 * BT)
                    dve.tensor_tensor(out=route[:, :, :], in0=route[:, :, :], in1=route2[:, :, :], op=ALU.add).then_inc(q["route_ok"], 1)
                    dve.wait_ge(q["route_ok"], b + 1)
                    for e in range(E):
                        dve.wait_ge(q["silu_ok"], b * E + (e + 1))
                        dve.tensor_tensor(out=inner[:, e % 2, :], in0=silu[:, e % 2, :], in1=bank[(1, 7)[e % 2]][:, :],
                                          op=ALU.mult).then_inc(q["inner_ok"], 1)
                        for t in range(BT):
                            dve.wait_ge(q["down_mm"], b * (BT * E) + (BT * e + t + 1))
                            dve.scalar_tensor_tensor(out=y[:, t, :], in0=bank[2 + t][:, 0:D], scalar=route[:, t, e:e + 1],
                                                     in1=y[:, t, :], op0=ALU.mult, op1=ALU.add).then_inc(q["down_read"], 1)
                    dve.wait_ge(q["out_ok"], b * 16 + 16)

            @block.tensor
            def _(pe):
                pe.wait_ge(q["wg_in"], 16)
                pe.wait_ge(q["wi_in"], 16 * 2 * KD)
                pe.wait_ge(q["wo_ok"], E)
                with pe.Fori(0, NB) as b:
                    def flip(t):
                        pe.wait_ge(q["latn_ok"], b * BT + (t + 1))
                        flat = lat_n[:, t % 2].rearrange("p h n -> p (h n)")
                        for half in range(2):
                            if t >= 1:
                                pe.wait_ge(q["latt_ok"], b * 8 + (2 * t - 1 + half))
                            for j in range(4):
                                at = (4 * half + j) * P
                                last = pe.transpose(bank[half][:, j * P:j * P + P], flat[:, at:at + P], ident[:, :])
                            last.then_inc(q["latt_mm"], 1)

                    def project(t):
                        pe.wait_ge(q["latt_ok"], b * 8 + (2 * t + 2))
                        if t >= 2:
                            pe.wait_ge(q["y_ok"], b * BT + (t - 1))
                        for g in range(NP):
                            last = pe.matmul(bank[2 + t % 2][:, 0:D], lat_t[:, t % 2, g, :], w_vo[:, g, :], start=(g == 0),
                                             stop=(g == NP - 1))
                        last.then_inc(q["att_mm"], 1)

                    for t in range(BT):
                        flip(t)
                        project(t)
                    pe.wait_ge(q["xn2_ok"], b * BT + BT)
                    for kd in range(KD):
                        for t in range(BT):
                            last = pe.transpose(bank[4 + kd][:, t * P:t * P + P], xn[:, t, kd * P:kd * P + P], ident[:, :])
                        last.then_inc(q["xt2_mm"], 1)
                    pe.wait_ge(q["ht2_ok"], b * KD + KD)
                    for t in range(BT):
                        for kd in range(KD):
                            last = pe.matmul(bank[3][:, t * E:t * E + E], ht[:, kd, t * P:t * P + P], wg[:, kd, :],
                                             start=(kd == 0), stop=(kd == KD - 1))
                    last.then_inc(q["lg_mm"], 1)

                    def up(e):
                        if e >= 2:
                            pe.wait_ge(q["inner_ok"], b * E + (e - 1))
                        for n in range(2):
                            for kd in range(KD):
                                last = pe.matmul(bank[((0, 6)[e % 2], (1, 7)[e % 2])[n]][:, :], wi[n][:, kd, e, :], ht[:, kd, :],
                                                 start=(kd == 0), stop=(kd == KD - 1))
                        last.then_inc(q["up_mm"], 1)

                    up(0)
                    for e in range(E):
                        if e + 1 < E:
                            up(e + 1)
                        pe.wait_ge(q["inner_ok"], b * E + (e + 1))
                        for t in range(BT):
                            if e >= 1:
                                pe.wait_ge(q["down_read"], b * (BT * E) + (BT * (e - 1) + t + 1))
                            else:
                                pe.wait_ge(q["lg_ok"], b + 1)
                            pe.matmul(bank[2 + t][:, 0:D], inner[:, e % 2, t * P:t * P + P], wo[:, e, :], start=True,
                                      stop=True).then_inc(q["down_mm"], 1)


NAMES = ["L0_attn_x", "L0_attn_w_qa", "L0_attn_q_a_norm_w", "L0_attn_w_qb", "L0_attn_w_kva", "L0_attn_kv_a_norm_w",
         "L0_attn_w_kvb", "L0_attn_w_o", "L0_ffn_w_gate", "L0_ffn_wi_0", "L0_ffn_wi_1", "L0_ffn_wo", "L0_c", "L0_wmod"]


def rotary_tables():
    inv = (np.float32(1.0) / np.float32(10000.0) ** (np.arange(0, DR, 2, dtype=np.float32) / np.float32(DR))).astype(np.float32)
    freqs = np.outer(np.arange(S, dtype=np.float32), inv).astype(np.float32)
    emb = np.concatenate((freqs, freqs), -1)
    return np.cos(emb).astype(np.float32), np.sin(emb).astype(np.float32)


def kernel(**inputs):
    import concourse.bacc as bacc
    from concourse.bass_utils import run_bass_kernel_spmd

    nc = bacc.Bacc("TRN2", target_bir_lowering=False, num_devices=1)
    cos, sin = rotary_tables()
    signs = np.where(np.arange(DR) % 2 == 0, np.float32(-1), np.float32(1))
    tables = {"rope_cos_by_feature": np.ascontiguousarray(cos.T), "rope_sin_by_feature": np.ascontiguousarray(sin.T),
              "rope_cos_by_token": cos, "rope_sin_by_token": sin * signs}
    arrays = {f"in_{n}": np.ascontiguousarray(inputs[n]) for n in NAMES} | tables
    args = [nc.dram_tensor(n, a.shape, mybir.dt.from_np(a.dtype), kind="ExternalInput").ap() for n, a in arrays.items()]
    out = nc.dram_tensor("out_0", (1, S, D), F32, kind="ExternalOutput").ap()
    adaln_block_kernel(nc, *args, out)
    result = run_bass_kernel_spmd(nc, [arrays], core_ids=[0])
    return result.results[0]["out_0"]
```

```python
import math
from contextlib import ExitStack

import numpy as np

import concourse.bass as bass
import concourse.mybir as mybir

F32 = mybir.dt.float32
F32R = mybir.dt.float32r
BF16 = mybir.dt.bfloat16
F16 = mybir.dt.float16
U32 = mybir.dt.uint32
ACT = mybir.ActivationFunctionType
ALU = mybir.AluOpType
AXX = mybir.AxisListType.X

P = 128
S, D = 2048, 256
H, QL, KVL = 16, 96, 64
DN, DR, DV = 128, 64, 128
E, M = 8, 128
NT = S // P
NP = H // 2
KD = D // P
BT = 4
NB = NT // BT
BW = BT * P
SCALE = 1.0 / math.sqrt(DN + DR)
LN_EPS, RMS_EPS = 1e-5, 1e-6
MASKED = -1.0e30
P_SHIFT = 10 * math.log(2.0)

NG = NT // BT
ITEMS = [(g + NG * j, h) for g in range(NG) for j in ((0, 1, 2, 3) if g % 2 else (3, 2, 1, 0)) for h in range(2)]
NI = len(ITEMS)
CHUNKS = []
FIRST = []
for _k, (_i, _h) in enumerate(ITEMS):
    FIRST.append(len(CHUNKS))
    for _c in range(_i // 4 + 1):
        CHUNKS.append((_k, _c, min(4, _i + 1 - 4 * _c)))
NC = len(CHUNKS)
FIRST.append(NC)
S_RING, P_RING, PT_RING, MX_RING = 5, 8, 5, 8
assert NC % S_RING == NC % P_RING == NC % PT_RING == NI % MX_RING == 0
CREDIT = 32
ROUNDS = range(2, NI + 2)
PREP = {2 * BT * c + (3 if c % 2 else 2): c for c in range(NG)}
PART_ROUNDS = (0, 1, 2)
ADD_ROUND = 3
PREP_READS = ({"v": 1, "a": 1}, {"v": 1, "a": 1}, {"v": 1})


def chunks_of(item):
    ahead, k = divmod(item, NI)
    return [ahead * NC + s for s in range(FIRST[k], FIRST[k + 1])]


def evac_on_vector(s):
    return CHUNKS[s % NC][1] == 3


def low_on_vector(s):
    return CHUNKS[s % NC][1] == 0


def prep_parts(r):
    return [(c, part) for start, c in PREP.items() for part, after in enumerate(PART_ROUNDS) if start + after == r]


def prep_sums(r):
    return [c for start, c in PREP.items() if start + ADD_ROUND == r]


USES = []
for _r in ROUNDS:
    USES += [("t", s) for s in chunks_of(_r - 1)] + [("q", c, part) for c, part in prep_parts(_r)]
NU = len(USES)
assert NU % 2 == 0
USE = {u: n for n, u in enumerate(USES)}


def use_of(s):
    turn, at = divmod(s - FIRST[1], NC)
    return turn * NU + USE["t", FIRST[1] + at]


def readers(u):
    if u[0] == "q":
        return PREP_READS[u[2]]
    return {"v" if evac_on_vector(u[1]) else "a": 1}


def reads(e, n):
    return sum(readers(u).get(e, 0) for u in USES[:n])


READS = {e: reads(e, NU) for e in "av"}
FIRST_READS = {e: sum(r.get(e, 0) for r in PREP_READS) for e in "av"}
BASE_READS = {e: CREDIT + FIRST_READS[e] + READS[e] - reads(e, NU - FIRST[1]) for e in "av"}
BASE_USES = CREDIT + len(PREP_READS) + FIRST[1]


def lows(e, n):
    return sum(low_on_vector(s) == (e == "v") for s in range(n))


LOWS = {e: lows(e, NC) for e in "vp"}
MANY = [s for s in range(NC) if ITEMS[CHUNKS[s][0]][0] >= 4]


def adaln_block_kernel(nc, x, w_qa, q_norm, w_qb, w_kva, kv_norm, w_kvb, w_o, w_gate, wi_0, wi_1, wo, c, wmod,
                       cos_t, sin_t, cos_k, sin_k, out):
    stack = ExitStack()

    def sb(scope, name, shape, dt=F32):
        return scope.enter_context(nc.sbuf_tensor(name, shape, dt))

    def sem(name):
        return stack.enter_context(nc.semaphore(name))

    with stack:
        bank = [stack.enter_context(nc.psum_tensor(f"bank{n}", [P, BW], F32)) for n in range(8)]

        lat = sb(stack, "lat", [P, NT, H * KVL])
        w_vo = sb(stack, "w_vo", [P, NP, D])
        rowsum = sb(stack, "rowsum", [P, NT, H + 2, 4])
        ident = sb(stack, "ident", [P, P])
        gates = sb(stack, "gates", [P, 2, D])
        modc = sb(stack, "modc", [P, 4, KD])
        neg_half = sb(stack, "neg_half", [P, 2 * BT])
        turnstile = sb(stack, "turnstile", [P, 1])

        attn = ExitStack()
        kt_a_hi = sb(attn, "kt_a_hi", [P, S], F32R)
        kt_a_lo = sb(attn, "kt_a_lo", [P, S], F32R)
        kt_b_hi = sb(attn, "kt_b_hi", [P, S], F32R)
        kt_b_lo = sb(attn, "kt_b_lo", [P, S], F32R)
        ql_hi = sb(attn, "ql_hi", [QL, NG, BT, P], F32R)
        ql_lo = sb(attn, "ql_lo", [QL, NG, BT, P], F32R)
        values = sb(attn, "values", [P, NT, 2 * KVL], F16)
        cos2 = sb(attn, "cos2", [P, S])
        sin2 = sb(attn, "sin2", [P, S])
        ident16 = sb(attn, "ident16", [P, P], BF16)
        mask16 = sb(attn, "mask16", [P, P], BF16)
        wq_dram = nc.dram_tensor("wq_parts", (2, NP + 1, QL, 3 * P), F32, kind="Internal").ap()

        prepare(nc, sb, sem, locals())
        attend(nc, sb, sem, locals())
        attn.close()
        experts(nc, sb, sem, locals())


def prepare(nc, sb, sem, k):
    bank, lat, ident, modc, gates, neg_half = k["bank"], k["lat"], k["ident"], k["modc"], k["gates"], k["neg_half"]
    turnstile = k["turnstile"]
    w_vo, wq_dram, values, ident16, mask16 = k["w_vo"], k["wq_dram"], k["values"], k["ident16"], k["mask16"]
    kt = [(k["kt_a_hi"], k["kt_a_lo"]), (k["kt_b_hi"], k["kt_b_lo"]), (k["ql_hi"], k["ql_lo"])]
    with ExitStack() as own:
        flat = lat[:, :, :].rearrange("p t n -> p (t n)")
        ends = np.cumsum([0, H * (DN + DR), H * (DN + DV), H * D, KD * 6 * D, NT * DR, NT * DR]).tolist()
        wqb, wkvb, wov, wm, ck, sk = (flat[:, a:b] for a, b in zip(ends[:-1], ends[1:]))
        wqb = wqb[0:QL].rearrange("p (h n) -> p h n", h=H)
        wkvb = wkvb[0:KVL].rearrange("p (h n) -> p h n", h=H)
        wov = wov.rearrange("p (h n) -> p h n", h=H)
        wm = wm.rearrange("p (k n) -> p k n", k=KD)
        ck = ck.rearrange("p (t n) -> p t n", t=NT)
        sk = sk.rearrange("p (t n) -> p t n", t=NT)
        xs = sb(own, "xs", [P, NT, D])
        wa = sb(own, "wa", [P, KD, QL + KVL + DR])
        qnw = sb(own, "qnw", [QL, 1])
        kvnw = sb(own, "kvnw", [KVL, 1])
        wqb_t = sb(own, "wqb_t", [P, H, QL])
        wk_t = sb(own, "wk_t", [P, H, KVL])
        wv_t = sb(own, "wv_t", [P, H, KVL])
        wq_hi = sb(own, "wq_hi", [QL, NP, 3 * P], F32R)
        wq_lo = sb(own, "wq_lo", [QL, NP, 3 * P], F32R)
        ccol = sb(own, "ccol", [P, KD])
        csilu = sb(own, "csilu", [P, KD])
        crep = sb(own, "crep", [P, KD, P])
        stats = sb(own, "stats", [P, BT, 6])
        mv = sb(own, "mv", [P, BT, 2])
        rstd = sb(own, "rstd", [P, BT])
        junk = sb(own, "junk", [P, BT, QL + KVL])
        ms = sb(own, "ms", [P, BT, 2])
        rms = sb(own, "rms", [P, BT, 2])
        gate_place, xn_place, ht_place = (w[:, :, :].rearrange("p h n -> p (h n)") for w in (wv_t, wqb_t, wk_t))
        sign = gate_place[:, 0:2 * D].rearrange("p (a n) -> p a n", a=2)
        size = gate_place[:, 2 * D:4 * D].rearrange("p (a n) -> p a n", a=2)
        xn = xn_place[:, 0:BT * D].rearrange("p (t n) -> p t n", t=BT)
        qn = xn_place[:, BT * D:BT * (D + QL)].rearrange("p (t n) -> p t n", t=BT)
        ht = ht_place.rearrange("p (k n) -> p k n", k=KD)
        n_kk = BT * (2 * KVL + DR)
        kk = gate_place[:, 0:n_kk].rearrange("p (t n) -> p t n", t=BT)
        krot = gate_place[:, n_kk:n_kk + BT * DR].rearrange("p (t n) -> p t n", t=BT)

        ld_mod, ld_x, ld_qb, ld_kvb = sem("ld_mod"), sem("ld_x"), sem("ld_qb"), sem("ld_kvb")
        ld_o, ld_a, ld_rope, consts, wq_out = sem("ld_o"), sem("ld_a"), sem("ld_rope"), sem("consts"), sem("wq_out")
        silu_c, crep_ok, mod_mm, mod_ok, gate_ok = (sem(n) for n in ("silu_c", "crep_ok", "mod_mm", "mod_ok", "gate_ok"))
        gate_in, gate_parts, wscaled, wt_mm = sem("gate_in"), sem("gate_parts"), sem("wscaled"), sem("wt_mm")
        wt_a, wt_v, abs_mm, wqh_ok, wql_ok = sem("wt_a"), sem("wt_v"), sem("abs_mm"), sem("wqh_ok"), sem("wql_ok")
        vo_mm, vo_ok = sem("vo_mm"), sem("vo_ok")
        st_ok, mv_ok, var_ok, rstd_ok, xn_ok, xt_mm = (sem(n) for n in ("st_ok", "mv_ok", "var_ok", "rstd_ok", "xn_ok", "xt_mm"))
        ht_ok, a_mm, ms_ok, mse_ok, rms_ok, kk_v, kk_ok, kk_mm, hi_ok, lo_ok, vh_ok, vl_ok = (
            sem(n) for n in ("ht_ok", "a_mm", "ms_ok", "mse_ok", "rms_ok", "kk_v", "kk_ok", "kk_mm", "hi_ok", "lo_ok", "vh_ok", "vl_ok"))

        groups = [("q", g) for g in range(4)] + [("k", g) for g in range(2)] + [("v", g) for g in range(2)]

        def group_out(kind, g):
            if kind == "q":
                return wqb_t[:, 4 * g:4 * g + 4, :], bank[g][:, :].rearrange("p (h n) -> p h n", h=4)[:, :, 0:QL]
            n = 4 + g if kind == "k" else 6 + g
            to = wk_t if kind == "k" else wv_t
            return to[:, 8 * g:8 * g + 8, :], bank[n][:, :].rearrange("p (h n) -> p h n", h=8)

        even, odd = (wqb.rearrange("p (g two) n -> p g two n", two=2)[:, :, :, DN:].rearrange(
            "p g two (i e) -> p g two i e", e=2)[:, :, :, :, e] for e in range(2))

        def pair_cols(w, at, e):
            return w[:, :, at:at + DR].rearrange("p g (i e) -> p g i e", e=2)[:, :, :, e]

        moves = []
        for at, hd in ((KVL, 0), (P, 1)):
            moves += [(at, 0, even[:, :, hd], 1.0), (at, 1, odd[:, :, hd], 1.0)]
        for at, hd in ((2 * P, 1), (2 * P + DR, 0)):
            moves += [(at, 0, odd[:, :, hd], -1.0), (at, 1, even[:, :, hd], 1.0)]

        def block_of(w, n, b):
            return w[:, :, bass.ds(b, 1), :].rearrange("p g a n -> p g (a n)") if n == 2 else w[:, bass.ds(b * BW, BW)]

        def product_of(n):
            return bank[0][0:QL, :].rearrange("p (g n) -> p g n", n=P) if n == 2 else bank[6 + n][:, :]

        def abs_view(w, g, hd):
            at = 0 if hd == 0 else P + DR
            return w[:, 4 * g:4 * g + 4, at:at + KVL], bank[g][0:QL, :].rearrange(
                "p (j two n) -> p j two n", two=2, n=KVL)[:, :, hd, :]

        with nc.Block() as block:

            @block.sync
            def _(sp):
                for kd in range(KD):
                    sp.dma_start(ccol[:, kd:kd + 1], k["c"][0, kd * P:kd * P + P].rearrange("(p a) -> p a", a=1)).then_inc(ld_mod, 16)
                sp.dma_start(wm, k["wmod"].rearrange("(k p) n -> p k n", p=P)).then_inc(ld_mod, 16)
                sp.dma_start(qnw[:, :], k["q_norm"].rearrange("(p a) -> p a", a=1)).then_inc(ld_qb, 16)
                sp.dma_start(wqb, k["w_qb"].rearrange("p (h n) -> p h n", h=H)).then_inc(ld_qb, 16)
                sp.dma_start(wa[:, :, 0:QL], k["w_qa"].rearrange("(k p) n -> p k n", p=P)).then_inc(ld_a, 16)
                sp.dma_start(wa[:, :, QL:], k["w_kva"].rearrange("(k p) n -> p k n", p=P)).then_inc(ld_a, 16)
                sp.dma_start(wov, k["w_o"].rearrange("(h p) n -> p h n", p=P)).then_inc(ld_o, 16)
                sp.wait_ge(wqh_ok, 4 + len(moves))
                sp.wait_ge(wql_ok, 4 + len(moves))
                for part, w in enumerate((wq_hi, wq_lo)):
                    raw = w[:, :, :].bitcast(F32)
                    sp.dma_start(wq_dram[part, 0:NP].rearrange("g p n -> p g n"), raw).then_inc(wq_out, 16)
                    sp.dma_start(wq_dram[part, NP:NP + 1].rearrange("g p n -> p g n"), raw[:, 0:1, :]).then_inc(wq_out, 16)
                sp.wait_ge(wq_out, 64)

            @block.gpsimd
            def _(pool):
                pool.memset(ident[:, :], 0.0).then_inc(consts, 1)
                pool.memset(ident16[:, :], 0.0).then_inc(consts, 1)
                pool.memset(mask16[:, :], 0.0).then_inc(consts, 1)
                pool.memset(neg_half[:, :], -0.5).then_inc(consts, 1)
                pool.wait_ge(consts, 4)
                for m in (ident, ident16):
                    pool.affine_select(out=m[:, :], in_=m[:, :], compare_op=ALU.not_equal, fill=1.0, base=0,
                                       pattern=[[-1, P]], channel_multiplier=1).then_inc(consts, 1)
                pool.affine_select(out=mask16[:, :], in_=mask16[:, :], compare_op=ALU.is_ge, fill=MASKED, base=0,
                                   pattern=[[-1, P]], channel_multiplier=1).then_inc(consts, 1)
                with pool.Fori(0, NB) as b:
                    pool.wait_ge(var_ok, b + 1)
                    pool.tensor_tensor(out=rstd[:, :], in0=rstd[:, :], in1=neg_half[:, 0:BT], op=ALU.pow).then_inc(rstd_ok, 1)
                    pool.wait_ge(mse_ok, b + 1)
                    pool.tensor_tensor(out=rms[:, :, :].rearrange("p t n -> p (t n)"),
                                       in0=rms[:, :, :].rearrange("p t n -> p (t n)"), in1=neg_half[:, :],
                                       op=ALU.pow).then_inc(rms_ok, 1)
                    pool.wait_ge(kk_v, b * 12 + 12)
                    pool.tensor_tensor(out=kk[:, :, KVL:KVL + DR], in0=kk[:, :, KVL:KVL + DR], in1=krot[:, :, :],
                                       op=ALU.add).then_inc(kk_ok, 1)
                    vb = values[:, bass.ds(b * BT, BT), :]
                    pool.tensor_copy(vb[:, :, 0:KVL], kk[:, :, 0:KVL]).then_inc(vh_ok, 1)
                    pool.wait_ge(vh_ok, b + 1)
                    pool.tensor_tensor(out=vb[:, :, KVL:], in0=kk[:, :, 0:KVL], in1=vb[:, :, 0:KVL],
                                       op=ALU.subtract).then_inc(vl_ok, 1)

            @block.scalar
            def _(act):
                act.dma_start(xs[:, :, :], k["x"].rearrange("a (t p) d -> p (a t) d", p=P)).then_inc(ld_x, 16)
                act.dma_start(kvnw[:, :], k["kv_norm"].rearrange("(p a) -> p a", a=1)).then_inc(ld_kvb, 16)
                act.dma_start(wkvb, k["w_kvb"].rearrange("p (h n) -> p h n", h=H)).then_inc(ld_kvb, 16)
                act.dma_start(ck[:, :, :], k["cos_k"].rearrange("(t p) n -> p t n", p=P)).then_inc(ld_rope, 16)
                act.dma_start(sk[:, :, :], k["sin_k"].rearrange("(t p) n -> p t n", p=P)).then_inc(ld_rope, 16)
                for half in range(2):
                    act.dma_start(k["cos2"][half * DR:half * DR + DR, :], k["cos_t"]).then_inc(ld_rope, 16)
                    act.dma_start(k["sin2"][half * DR:half * DR + DR, :], k["sin_t"]).then_inc(ld_rope, 16)
                act.wait_ge(ld_mod, 16 * (KD + 1))
                act.activation(csilu[:, :], ccol[:, :], ACT.Silu).then_inc(silu_c, 1)
                for n, (kind, g) in enumerate(groups):
                    if n % 2 == 0:
                        act.wait_ge(wt_mm, n + 1)
                        to, of = group_out(kind, g)
                        act.activation(to, of, ACT.Copy).then_inc(wt_a, 1)
                act.wait_ge(wscaled, 2)
                for at, e, of, sgn in moves:
                    act.activation(pair_cols(wq_hi, at, e), of, ACT.Copy, scale=sgn).then_inc(wqh_ok, 1)
                for g in range(2):
                    act.wait_ge(abs_mm, g + 1)
                    for hd in range(2):
                        to, of = abs_view(wq_hi, g, hd)
                        act.activation(to, of, ACT.Copy).then_inc(wqh_ok, 1)
                act.wait_ge(mod_ok, 2)
                with act.Fori(0, NB) as b:
                    for kd in range(KD):
                        act.wait_ge(xt_mm, b * KD + kd + 1)
                        act.activation(ht[:, kd, :], bank[kd][:, :], ACT.Identity, scale=modc[:, 1, kd:kd + 1],
                                       bias=modc[:, 0, kd:kd + 1]).then_inc(ht_ok, 1)
                    for t in range(BT):
                        act.wait_ge(a_mm, b * BT + t + 1)
                        of = bank[2 + t][:, :]
                        for n, (a, w) in enumerate(((0, QL), (QL, KVL))):
                            act.activation(junk[:, t, a:a + w], of[:, a:a + w], ACT.Square, scale=1.0 / math.sqrt(w),
                                           accum_out=ms[:, t, n:n + 1]).then_inc(ms_ok, 1)
                    for n, (hi, _) in enumerate(kt):
                        act.wait_ge(kk_mm, b * 3 + n + 1)
                        act.activation(block_of(hi, n, b), product_of(n), ACT.Copy).then_inc(hi_ok, 1)

            @block.vector
            def _(dve):
                dve.wait_ge(silu_c, 1)
                for kd in range(KD):
                    dve.tensor_copy(crep[:, kd, :], csilu[:, kd:kd + 1].to_broadcast([P, P])).then_inc(crep_ok, 1)
                dve.wait_ge(ld_kvb, 32)
                dve.tensor_scalar(wkvb, wkvb, kvnw[:, :], None, ALU.mult).then_inc(wscaled, 1)
                dve.wait_ge(ld_qb, 32)
                dve.tensor_scalar(wqb, wqb, qnw[:, :], SCALE, ALU.mult, ALU.mult).then_inc(wscaled, 1)
                dve.wait_ge(mod_mm, 1)
                dve.tensor_copy(modc[:, :, :], bank[0][:, 0:4 * KD].rearrange("p (j k) -> p j k", k=KD)).then_inc(mod_ok, 1)
                dve.wait_ge(mod_ok, 1)
                odd_rows = modc[:, :, :].rearrange("p (a two) k -> p a two k", two=2)[:, :, 1, :]
                dve.tensor_scalar(odd_rows, odd_rows, 1.0, None, ALU.add).then_inc(mod_ok, 1)
                dve.wait_ge(mod_mm, 2)
                dve.tensor_copy(gates[:, :, :].rearrange("p a n -> p (a n)"), bank[1][:, :]).then_inc(gate_in, 1)
                dve.wait_ge(gate_in, 1)
                dve.tensor_scalar(sign[:, :, :], gates[:, :, :], 0.0, 2.0, ALU.is_ge, ALU.mult).then_inc(gate_parts, 1)
                dve.scalar_tensor_tensor(out=size[:, :, :], in0=gates[:, :, :], scalar=-1.0, in1=gates[:, :, :],
                                         op0=ALU.mult, op1=ALU.max).then_inc(gate_parts, 1)
                dve.wait_ge(gate_parts, 2)
                dve.tensor_scalar(size[:, :, :], size[:, :, :], 0.25, None, ALU.max).then_inc(gate_parts, 1)
                dve.wait_ge(gate_parts, 3)
                dve.scalar_tensor_tensor(out=gates[:, :, :], in0=sign[:, :, :], scalar=-1.0, in1=size[:, :, :],
                                         op0=ALU.add, op1=ALU.mult).then_inc(gate_ok, 1)
                for n, (kind, g) in enumerate(groups):
                    if n % 2 == 1:
                        dve.wait_ge(wt_mm, n + 1)
                        to, of = group_out(kind, g)
                        dve.tensor_copy(to, of).then_inc(wt_v, 1)
                for n, (at, e, of, sgn) in enumerate(moves):
                    dve.wait_ge(wqh_ok, n + 1)
                    hi = pair_cols(wq_hi, at, e).bitcast(F32)
                    dve.scalar_tensor_tensor(out=pair_cols(wq_lo, at, e), in0=of, scalar=sgn, in1=hi, op0=ALU.mult,
                                             op1=ALU.subtract).then_inc(wql_ok, 1)
                for g in range(2):
                    for hd in range(2):
                        dve.wait_ge(wqh_ok, len(moves) + 2 * g + 2)
                        to, of = abs_view(wq_lo, g, hd)
                        hi, _ = abs_view(wq_hi, g, hd)
                        dve.tensor_tensor(out=to, in0=of, in1=hi.bitcast(F32), op=ALU.subtract).then_inc(wql_ok, 1)
                dve.wait_ge(gate_ok, 1)
                for n in range(NP // 2):
                    dve.wait_ge(vo_mm, n + 1)
                    dve.tensor_tensor(out=w_vo[:, 2 * n:2 * n + 2, :], in0=bank[2 + n][:, :].rearrange("p (a n) -> p a n", a=2),
                                      in1=gates[:, 0:1, :].to_broadcast([P, 2, D]), op=ALU.mult).then_inc(vo_ok, 1)
                dve.wait_ge(ld_x, 16)
                dve.wait_ge(ld_rope, 96)
                with dve.Fori(0, NB) as b:
                    xb = xs[:, bass.ds(b * BT, BT), :]
                    for t in range(BT):
                        dve.bn_stats(stats[:, t, :], xb[:, t, :]).then_inc(st_ok, 1)
                    dve.wait_ge(st_ok, b * BT + BT)
                    dve.memset(turnstile[:, :], 0.0)
                    for t in range(BT):
                        dve.bn_aggr(mv[:, t, :], stats[:, t, :]).then_inc(mv_ok, 1)
                    dve.wait_ge(mv_ok, b * BT + BT)
                    dve.tensor_scalar(rstd[:, :], mv[:, :, 1], LN_EPS, None, ALU.add).then_inc(var_ok, 1)
                    dve.wait_ge(rstd_ok, b + 1)
                    for t in range(BT):
                        dve.tensor_scalar(xn[:, t, :], xb[:, t, :], mv[:, t, 0:1], rstd[:, t:t + 1], ALU.subtract,
                                          ALU.mult).then_inc(xn_ok, 1)
                    dve.wait_ge(ms_ok, b * 2 * BT + 2 * BT)
                    dve.tensor_scalar(rms[:, :, :], ms[:, :, :], RMS_EPS, None, ALU.add).then_inc(mse_ok, 1)
                    dve.wait_ge(rms_ok, b + 1)
                    for t in range(BT):
                        of = bank[2 + t][:, :]
                        dve.tensor_scalar(qn[:, t, :], of[:, 0:QL], rms[:, t, 0:1], None, ALU.mult)
                        for at in (0, KVL + DR):
                            dve.tensor_scalar(kk[:, t, at:at + KVL], of[:, QL:QL + KVL], rms[:, t, 1:2], None, ALU.mult)
                        rope = of[:, QL + KVL:QL + KVL + DR]
                        ckt = ck[:, bass.ds(b * BT + t, 1), :].rearrange("p a n -> p (a n)")
                        skt = sk[:, bass.ds(b * BT + t, 1), :].rearrange("p a n -> p (a n)").rearrange("p (i e) -> p i e", e=2)
                        dve.tensor_tensor(out=kk[:, t, KVL:KVL + DR], in0=rope, in1=ckt, op=ALU.mult).then_inc(kk_v, 1)
                        swapped = rope.rearrange("p (i e) -> p i e", e=2)
                        to = krot[:, t, :].rearrange("p (i e) -> p i e", e=2)
                        for e in range(2):
                            dve.tensor_tensor(out=to[:, :, e], in0=swapped[:, :, 1 - e], in1=skt[:, :, e],
                                              op=ALU.mult).then_inc(kk_v, 1)
                    for n, (hi, lo) in enumerate(kt):
                        dve.wait_ge(hi_ok, b * 3 + n + 1)
                        dve.tensor_tensor(out=block_of(lo, n, b), in0=product_of(n), in1=block_of(hi, n, b).bitcast(F32),
                                          op=ALU.subtract).then_inc(lo_ok, 1)

            @block.tensor
            def _(pe):
                pe.wait_ge(ld_mod, 16 * (KD + 1))
                pe.wait_ge(silu_c, 1)
                for j, part in enumerate((0, 1, 3, 4)):
                    for kd in range(KD):
                        at = part * D + kd * P
                        for kk_ in range(KD):
                            last = pe.matmul(bank[0][:, j * KD + kd:j * KD + kd + 1], wm[:, kk_, at:at + P],
                                             csilu[:, kk_:kk_ + 1], start=(kk_ == 0), stop=(kk_ == KD - 1))
                last.then_inc(mod_mm, 1)
                pe.wait_ge(crep_ok, KD)
                for j, part in enumerate((2, 5)):
                    for kk_ in range(KD):
                        last = pe.matmul(bank[1][:, j * D:j * D + D], crep[:, kk_, :], wm[:, kk_, part * D:part * D + D],
                                         start=(kk_ == 0), stop=(kk_ == KD - 1))
                last.then_inc(mod_mm, 1)
                pe.wait_ge(consts, 7)
                pe.wait_ge(wscaled, 2)
                pe.wait_ge(mod_ok, 1)
                pe.wait_ge(gate_ok, 1)
                for kind, g in groups:
                    n, step, rows, of = {"q": (g, 4, QL, wqb), "k": (4 + g, 8, KVL, wkvb), "v": (6 + g, 8, KVL, wkvb)}[kind]
                    at = DN if kind == "v" else 0
                    for j in range(step):
                        last = pe.transpose(bank[n][:, j * (BW // step):j * (BW // step) + rows],
                                            of[:, step * g + j, at:at + P], ident[0:rows, 0:rows])
                    last.then_inc(wt_mm, 1)
                pe.wait_ge(wt_a, 4)
                pe.wait_ge(wt_v, 4)
                for g in range(2):
                    for j in range(8):
                        last = pe.matmul(bank[g][0:QL, j * KVL:j * KVL + KVL], wqb_t[:, 8 * g + j, :], wk_t[:, 8 * g + j, :],
                                         start=True, stop=True)
                    last.then_inc(abs_mm, 1)
                pe.wait_ge(ld_o, 16)
                for n in range(NP // 2):
                    for j in range(4):
                        h = 4 * n + j
                        last = pe.matmul(bank[2 + n][(h % 2) * KVL:(h % 2) * KVL + KVL, (j // 2) * D:(j // 2) * D + D],
                                         wv_t[:, h, :], wov[:, h, :], start=True, stop=True)
                    last.then_inc(vo_mm, 1)
                pe.wait_ge(wql_ok, 4 + len(moves))
                pe.wait_ge(vo_ok, NP // 2)
                pe.wait_ge(ld_a, 32)
                with pe.Fori(0, NB) as b:
                    pe.wait_ge(xn_ok, b * BT + BT)
                    for kd in range(KD):
                        for t in range(BT):
                            last = pe.transpose(bank[kd][:, t * P:t * P + P], xn[:, t, kd * P:kd * P + P], ident[:, :])
                        last.then_inc(xt_mm, 1)
                    pe.wait_ge(ht_ok, b * KD + KD)
                    for t in range(BT):
                        for kd in range(KD):
                            last = pe.matmul(bank[2 + t][:, 0:QL + KVL + DR], ht[:, kd, t * P:t * P + P], wa[:, kd, :],
                                             start=(kd == 0), stop=(kd == KD - 1))
                        last.then_inc(a_mm, 1)
                    pe.wait_ge(kk_ok, b + 1)
                    for n, at in enumerate((0, KVL)):
                        for t in range(BT):
                            last = pe.transpose(bank[6 + n][:, t * P:t * P + P], kk[:, t, at:at + P], ident[:, :])
                        last.then_inc(kk_mm, 1)
                    for t in range(BT):
                        last = pe.transpose(bank[0][0:QL, t * P:t * P + P], qn[:, t, :], ident[:, :])
                    last.then_inc(kk_mm, 1)


def attend(nc, sb, sem, k):
    bank, lat, rowsum, ident, wq_dram, values = k["bank"], k["lat"], k["rowsum"], k["ident"], k["wq_dram"], k["values"]
    cos2, sin2, ident16, mask16 = k["cos2"], k["sin2"], k["ident16"], k["mask16"]
    kt_hi, kt_lo = (k["kt_a_hi"], k["kt_b_hi"]), (k["kt_a_lo"], k["kt_b_lo"])
    ql = (k["ql_hi"], k["ql_lo"])
    BEFORE = len(PREP_READS) + FIRST[1]
    s_bank, t_bank, o_bank = bank[0:S_RING], bank[S_RING:S_RING + 2], bank[S_RING + 2]
    with ExitStack() as own:
        wq = [sb(own, f"wq_pair_{p}", [QL, 3 * P], F32R) for p in ("hi", "lo")]
        q_hi = sb(own, "q_hi", [P, 2, 2, BW], F32R)
        q_lo = sb(own, "q_lo", [P, 2, 2, BW], F32R)
        qf = sb(own, "qf", [P, 2, BW])
        qs = sb(own, "qs", [P, BW])
        probs = sb(own, "probs", [P, P_RING, BW])
        pt = sb(own, "pt", [P, PT_RING, BW])
        pt_lo = sb(own, "pt_lo", [P, PT_RING, BW], F16)
        mx = sb(own, "mx", [P, MX_RING, 4])
        nmx = sb(own, "nmx", [P, MX_RING])
        shift = sb(own, "shift", [P, MX_RING])

        wq_in = sem("wq_in")
        q_sum = sem("q_sum")
        q_hi_ok = sem("q_hi_ok")
        q_lo_ok = sem("q_lo_ok")
        sc_done = sem("sc_done")
        chunk_max = sem("chunk_max")
        row_max = sem("row_max")
        max_ok = sem("max_ok")
        exp_done = sem("exp_done")
        use_done = sem("use_done")
        bank_read = {e: sem(f"bank_read_{e}") for e in "av"}
        low_ok = {e: sem(f"low_ok_{e}") for e in "vp"}
        pv_done = sem("pv_done")
        sum_read = sem("sum_read")
        zeroed = sem("zeroed")

        def count(n, turn, per_turn):
            return n if turn is None else turn * per_turn + n

        def wait_read(eng, hp, n):
            for e, steps in readers(USES[n % NU]).items():
                before = reads(e, n % NU) - (READS[e] if n < 0 else 0)
                eng.wait_ge(bank_read[e], count(BASE_READS[e] + before + steps, hp, READS[e]))

        def bank_of(use):
            return t_bank[use % 2]

        def query_products(pe, g, part, use):
            w = [wq[p][:, part * P:part * P + P] for p in range(2)]
            x = [ql[p][:, g].rearrange("p t n -> p (t n)") for p in range(2)]
            for n, (a, b) in enumerate(((0, 0), (0, 1), (1, 0))):
                last = pe.matmul(bank_of(use)[:, :], w[a], x[b], start=(n == 0), stop=(n == 2))
            last.then_inc(use_done, 1)

        ROT, PLAIN = (slice(DR, P), slice(0, DR)), (slice(0, DR), slice(DR, P))

        def query_cosine(dve, g, part, use):
            at = slice(g * BW, g * BW + BW)
            if part < 2:
                rot = ROT[part]
                dve.tensor_tensor(out=qf[rot, part, :], in0=bank_of(use)[rot, :], in1=cos2[rot, at],
                                  op=ALU.mult).then_inc(bank_read["v"], 1)
            else:
                dve.tensor_tensor(out=qs[:, :], in0=bank_of(use)[:, :], in1=sin2[:, at], op=ALU.mult).then_inc(bank_read["v"], 1)

        def query_plain(act, part, use):
            act.activation(qf[PLAIN[part], part, :], bank_of(use)[PLAIN[part], :], ACT.Copy).then_inc(bank_read["a"], 1)

        def query_sum(dve, hd):
            dve.tensor_tensor(out=qf[ROT[hd], hd, :], in0=qf[ROT[hd], hd, :], in1=qs[ROT[hd], :], op=ALU.add).then_inc(q_sum, 1)

        def query_high(act, g, hd, n):
            act.wait_ge(q_sum, n * 2 + (hd + 1))
            act.activation(q_hi[:, g % 2, hd, :], qf[:, hd, :], ACT.Copy).then_inc(q_hi_ok, 1)

        def query_low(pool, g, hd, n):
            pool.wait_ge(q_hi_ok, n * 2 + (hd + 1))
            pool.tensor_tensor(out=q_lo[:, g % 2, hd, :], in0=qf[:, hd, :], in1=q_hi[:, g % 2, hd, :].bitcast(F32),
                               op=ALU.subtract).then_inc(q_lo_ok, 1)

        with nc.Block() as block:

            @block.sync
            def _(sp):
                for part in range(2):
                    sp.dma_start(wq[part][:, :].bitcast(F32), wq_dram[part, 0]).then_inc(wq_in, 16)
                with sp.Fori(0, NP) as hp:
                    sp.wait_ge(use_done, hp * NU + (BASE_USES + USE["q", NG - 2, 2] + 1))
                    for part in range(2):
                        sp.dma_start(wq[part][:, :].bitcast(F32),
                                     wq_dram[part, bass.ds(hp + 1, 1)].rearrange("g p n -> (g p) n")).then_inc(wq_in, 16)
                sp.wait_ge(wq_in, 32 * (NP + 1))

            @block.gpsimd
            def _(pool):
                pool.memset(rowsum[:, :, :, :], 0.0).then_inc(zeroed, 1)
                for hd in range(2):
                    query_low(pool, 0, hd, 0)

                def low_parts(hp, s):
                    wait_read(pool, hp, use_of(s))
                    n = CHUNKS[s % NC][2] * P
                    full = pt[:, s % PT_RING, 0:n]
                    pool.tensor_tensor(out=pt_lo[:, s % PT_RING, 0:n], in0=full, in1=cut(full),
                                       op=ALU.subtract).then_inc(low_ok["p"], 1)

                for s in chunks_of(0):
                    if not low_on_vector(s):
                        low_parts(None, s)
                with pool.Fori(0, NP) as hp:
                    for r in ROUNDS:
                        for s in chunks_of(r - 1):
                            if not low_on_vector(s):
                                low_parts(hp, s)
                        for c in prep_sums(r):
                            for hd in range(2):
                                query_low(pool, (c + 1) % NG, hd, hp * NG + (c + 1))

            @block.scalar
            def _(act):
                act.sem_inc(exp_done, CREDIT)
                act.sem_inc(bank_read["a"], CREDIT)
                act.wait_ge(zeroed, 1)
                for part in range(2):
                    act.wait_ge(use_done, CREDIT + part + 1)
                    query_plain(act, part, part - BEFORE)
                for hd in range(2):
                    query_high(act, 0, hd, 0)

                def exponentials(hp, s):
                    item, c, n = CHUNKS[s % NC]
                    i, h = ITEMS[item]
                    ahead = s // NC
                    act.wait_ge(max_ok, count(ahead * NI + item + 1, hp, NI))
                    if not (hp is None and s < P_RING):
                        act.wait_ge(use_done, count(BASE_USES + use_of(s - P_RING) + 1, hp, NU))
                    act.activation(probs[:, s % P_RING, 0:n * P], s_bank[s % S_RING][:, 0:n * P], ACT.Exp,
                                   bias=shift[:, item % MX_RING:item % MX_RING + 1],
                                   accum_out=rowsum[:, i, h, c:c + 1] if hp is None else
                                   rowsum[:, i, bass.ds(hp * 2 + (2 * ahead + h), 1), c]).then_inc(exp_done, 1)

                def evacuate(hp, s):
                    u, n = use_of(s), CHUNKS[s % NC][2]
                    act.wait_ge(use_done, count(BASE_USES + u + 1, hp, NU))
                    act.wait_ge(pv_done, count(CREDIT + s - PT_RING + 1, hp, NC))
                    act.activation(pt[:, s % PT_RING, 0:n * P], bank_of(u)[:, 0:n * P], ACT.Copy).then_inc(bank_read["a"], 1)

                def round_of(hp, r):
                    moves = [s for s in chunks_of(r - 1) if r >= 1 and not evac_on_vector(s)]
                    for s in moves[:2]:
                        evacuate(hp, s)
                    moves = moves[2:]
                    for s in chunks_of(r):
                        exponentials(hp, s)
                        if moves:
                            evacuate(hp, moves.pop(0))
                    for s in moves:
                        evacuate(hp, s)

                for r in range(2):
                    round_of(None, r)
                with act.Fori(0, NP) as hp:
                    for r in ROUNDS:
                        round_of(hp, r)
                        for c, part in prep_parts(r):
                            if part < 2:
                                use = USE["q", c, part]
                                act.wait_ge(use_done, hp * NU + (BASE_USES + use + 1))
                                act.wait_ge(q_lo_ok, hp * (2 * NG) + (2 * (c + 1)))
                                query_plain(act, part, use)
                        for c in prep_sums(r):
                            for hd in range(2):
                                query_high(act, (c + 1) % NG, hd, hp * NG + (c + 1))

            @block.vector
            def _(dve):
                dve.sem_inc(bank_read["v"], CREDIT)
                dve.sem_inc(sum_read, 1)
                for part in range(3):
                    dve.wait_ge(use_done, CREDIT + part + 1)
                    query_cosine(dve, 0, part, part - BEFORE)
                for e in "va":
                    dve.wait_ge(bank_read[e], CREDIT + FIRST_READS[e])
                for hd in range(2):
                    query_sum(dve, hd)

                def maximum(hp, item):
                    slot, chunks = item % MX_RING, chunks_of(item)
                    for s in chunks:
                        _, c, n = CHUNKS[s % NC]
                        of = s_bank[s % S_RING][:, 0:n * P]
                        dve.wait_ge(sc_done, count(s + 1, hp, NC))
                        if len(chunks) > 1:
                            dve.tensor_reduce(out=mx[:, slot, c:c + 1], in_=of, axis=AXX, op=ALU.max).then_inc(chunk_max, 1)
                        else:
                            dve.tensor_reduce(out=nmx[:, slot:slot + 1], in_=of, axis=AXX, op=ALU.max,
                                              negate=True).then_inc(row_max, 1)
                    if len(chunks) > 1:
                        ahead, s = divmod(chunks[-1], NC)
                        dve.wait_ge(chunk_max, count((ahead * len(MANY) + MANY.index(s) + 1), hp, len(MANY)))
                        dve.tensor_reduce(out=nmx[:, slot:slot + 1], in_=mx[:, slot, 0:len(chunks)], axis=AXX, op=ALU.max,
                                          negate=True).then_inc(row_max, 1)
                    dve.wait_ge(row_max, count(item + 1, hp, NI))
                    dve.tensor_scalar(shift[:, slot:slot + 1], nmx[:, slot:slot + 1], P_SHIFT, None, ALU.add).then_inc(max_ok, 1)

                def move(hp, item):
                    for s in chunks_of(item):
                        u, n = use_of(s), CHUNKS[s % NC][2]
                        full = pt[:, s % PT_RING, 0:n * P]
                        if evac_on_vector(s):
                            dve.wait_ge(use_done, count(BASE_USES + u + 1, hp, NU))
                            dve.wait_ge(pv_done, count(CREDIT + s - PT_RING + 1, hp, NC))
                            dve.tensor_copy(full, bank_of(u)[:, 0:n * P]).then_inc(bank_read["v"], 1)
                        if low_on_vector(s):
                            wait_read(dve, hp, u)
                            dve.tensor_tensor(out=pt_lo[:, s % PT_RING, 0:n * P], in0=full, in1=cut(full),
                                              op=ALU.subtract).then_inc(low_ok["v"], 1)

                for r in range(2):
                    maximum(None, r)
                    if r == 1:
                        move(None, 0)
                with dve.Fori(0, NP) as hp:
                    for r in ROUNDS:
                        maximum(hp, r)
                        for c in prep_sums(r):
                            for hd in range(2):
                                for part in (hd, 2):
                                    wait_read(dve, hp, USE["q", c, part])
                                query_sum(dve, hd)
                        move(hp, r - 1)
                        i, h = ITEMS[r - 2]
                        dve.wait_ge(pv_done, hp * NC + (CREDIT + FIRST[r - 1]))
                        dve.tensor_reduce(out=lat[:, i, bass.ds(hp * (2 * KVL) + h * KVL, KVL)],
                                          in_=o_bank[:, 0:2 * KVL].rearrange("p (a n) -> p n a", a=2), axis=AXX,
                                          op=ALU.add).then_inc(sum_read, 1)
                        for c, part in prep_parts(r):
                            use = USE["q", c, part]
                            dve.wait_ge(q_lo_ok, hp * (2 * NG) + (2 * (c + 1)))
                            dve.wait_ge(use_done, hp * NU + (BASE_USES + use + 1))
                            query_cosine(dve, (c + 1) % NG, part, use)

            @block.tensor
            def _(pe):
                pe.sem_inc(use_done, CREDIT)
                pe.sem_inc(pv_done, CREDIT)
                pe.wait_ge(wq_in, 32)
                for part in range(3):
                    if part == 2:
                        for e in "av":
                            pe.wait_ge(bank_read[e], CREDIT + PREP_READS[0][e])
                    query_products(pe, 0, part, part - BEFORE)
                for e in "av":
                    pe.wait_ge(bank_read[e], CREDIT + FIRST_READS[e])

                def scores(hp, item):
                    i, h = ITEMS[item % NI]
                    g, ahead = i % NG, item // NI
                    tok = (i // NG) * P
                    q = [w[:, g % 2, h, tok:tok + P] for w in (q_hi, q_lo)]
                    if item % (2 * BT) == 0:
                        pe.wait_ge(q_lo_ok, count(2 * (NG * ahead + g + 1), hp, 2 * NG))
                    for s in chunks_of(item):
                        _, c, n = CHUNKS[s % NC]
                        to = s_bank[s % S_RING]
                        cols = max(n * P, 2 * P)
                        at = slice(c * BW, c * BW + cols)
                        keys = [kt_hi[h][:, at], kt_lo[h][:, at]]
                        diagonal = s == chunks_of(item)[-1]
                        pe.wait_ge(exp_done, count(CREDIT + s - S_RING + 1, hp, NC))
                        for m, (a, b) in enumerate(((0, 0), (0, 1), (1, 0))):
                            last = pe.matmul(to[:, 0:cols], q[a], keys[b], start=(m == 0), stop=(m == 2 and not diagonal))
                        if diagonal:
                            last = pe.matmul(to[:, (n - 1) * P:n * P], ident16[:, :], mask16[:, :], start=False, stop=True)
                        last.then_inc(sc_done, 1)

                def transpose(hp, s):
                    u, n = use_of(s), CHUNKS[s % NC][2]
                    pe.wait_ge(exp_done, count(CREDIT + s + 1, hp, NC))
                    if not (hp is None and s < 2):
                        wait_read(pe, hp, u - 2)
                    for j in range(n):
                        last = pe.transpose(bank_of(u)[:, j * P:j * P + P], probs[:, s % P_RING, j * P:j * P + P], ident[:, :])
                    last.then_inc(use_done, 1)

                def weigh(hp, s):
                    item, c, n = CHUNKS[s]
                    e = "v" if low_on_vector(s) else "p"
                    pe.wait_ge(low_ok[e], hp * LOWS[e] + lows(e, s + 1))
                    if s == FIRST[item]:
                        pe.wait_ge(sum_read, hp * NI + (item + 1))
                    for j in range(n):
                        key = 4 * c + j
                        high = cut(pt[:, s % PT_RING, j * P:j * P + P])
                        end = s == FIRST[item + 1] - 1 and j == n - 1
                        pe.matmul(o_bank[:, 0:2 * KVL], high, values[:, key, :], start=(c == 0 and j == 0), stop=False)
                        last = pe.matmul(o_bank[:, 0:KVL], pt_lo[:, s % PT_RING, j * P:j * P + P], values[:, key, 0:KVL],
                                         start=False, stop=end)
                    last.then_inc(pv_done, 1)

                scores(None, 0)
                scores(None, 1)
                for s in chunks_of(0):
                    transpose(None, s)
                with pe.Fori(0, NP) as hp:
                    for r in ROUNDS:
                        scores(hp, r)
                        new, old = chunks_of(r - 1), chunks_of(r - 2)
                        while new or old:
                            for s in new[:2]:
                                transpose(hp, s)
                            for s in old[:2]:
                                weigh(hp, s)
                            new, old = new[2:], old[2:]
                        for c, part in prep_parts(r):
                            if c == NG - 1 and part == 0:
                                pe.wait_ge(wq_in, hp * 32 + 64)
                            use = USE["q", c, part]
                            wait_read(pe, hp, use - 2)
                            query_products(pe, (c + 1) % NG, part, use)


def cut(a):
    return a.bitcast(BF16).rearrange("p (n e) -> p n e", e=2)[:, :, 1]


def experts(nc, sb, sem, k):
    bank, lat, rowsum, ident, gates = k["bank"], k["lat"], k["rowsum"], k["ident"], k["gates"]
    modc, neg_half, turnstile = k["modc"], k["neg_half"], k["turnstile"]
    up_bank = ((bank[0], bank[1]), (bank[6], bank[7]))
    down_bank, front_bank = bank[2:4], bank[4:6]
    with ExitStack() as own:
        xs = sb(own, "xs_again", [P, NT, D])
        w_vo = k["w_vo"]
        wvo_hi = sb(own, "wvo_hi", [P, NP, D], F32R)
        wvo_lo = sb(own, "wvo_lo", [P, NP, D], F32R)
        wi_hi = [sb(own, f"wi_{n}_hi", [P, KD, E, M], F32R) for n in range(2)]
        wi_lo = [sb(own, f"wi_{n}_lo", [P, KD, E, M], F32R) for n in range(2)]
        wo_hi = sb(own, "wo_hi", [P, E, D], F32R)
        wo_lo = sb(own, "wo_lo", [P, E, D], F32R)
        wo = w_vo
        wg = sb(own, "wg", [P, KD, E])
        rden = sb(own, "rden", [P, NT, H])
        lat_n = sb(own, "lat_n", [P, 2, H, KVL])
        lat_hi = sb(own, "lat_hi", [P, NP, P], F32R)
        lat_lo = sb(own, "lat_lo", [P, NP, P], F32R)
        stats = sb(own, "stats2", [P, BT, 6])
        mv = sb(own, "mv2", [P, BT, 2])
        rstd = sb(own, "rstd2", [P, BT])
        xn = sb(own, "xn2", [P, BT, D])
        ht = sb(own, "ht2", [P, KD, BW])
        ht_hi = sb(own, "ht2_hi", [P, KD, BW], F32R)
        ht_lo = sb(own, "ht2_lo", [P, KD, BW], F32R)
        silu = sb(own, "expert_silu", [P, 2, BW])
        stage = [xn[:, :, :].rearrange("p t (a m) -> p (t a) m", m=M), ht[:, :, :].rearrange("p k (a m) -> p (k a) m", m=M),
                 silu[:, :, :].rearrange("p k (a m) -> p (k a) m", m=M)]
        pieces = [(n, kd) for n in range(2) for kd in range(KD)]
        places = sb(own, "places", [P, E], mybir.dt.int32)
        placesf = sb(own, "placesf", [P, E])
        logits = sb(own, "logits", [P, BT, E])
        top = sb(own, "top", [P, BT, 8])
        top_at = sb(own, "top_at", [P, BT, 8], U32)
        top_f = sb(own, "top_f", [P, BT, 2])
        gap = sb(own, "gap", [P, BT])
        ratio = sb(own, "ratio", [P, BT])
        total = sb(own, "total", [P, BT])
        first_w = sb(own, "first_w", [P, BT])
        second_w = sb(own, "second_w", [P, BT])
        route1 = sb(own, "route1", [P, BT, E])
        route2 = sb(own, "route2", [P, BT, E])
        route = sb(own, "route", [P, BT, E])
        inner = silu
        inner_hi = sb(own, "inner_hi", [P, 2, BW], F32R)
        inner_lo = sb(own, "inner_lo", [P, 2, BW], F32R)

        dma = {n: sem(n) for n in "x2_in wo_in wg_in out_ok".split()}
        wi_in = [sem(f"wi_in_{i}") for i in range(len(pieces))]
        place_i, place_f = sem("place_i"), sem("place_f")
        whole_ok, w_hi, w_lo = sem("whole_ok"), sem("w_hi"), sem("w_lo")
        den_ok, rden_ok, latn_ok = sem("den_ok"), sem("rden_ok"), sem("latn_ok")
        flipped = sem("flipped")
        lath_ok, latl_ok = sem("lath_ok"), sem("latl_ok")
        att_mm, y_ok = sem("att_mm"), sem("y_ok")
        st2_ok, mv2_ok, var2_ok, rstd2_ok, xn2_ok = (sem(n) for n in ("st2_ok", "mv2_ok", "var2_ok", "rstd2_ok", "xn2_ok"))
        xt2_mm, ht2_ok, hth_ok, htl_ok = sem("xt2_mm"), sem("ht2_ok"), sem("hth_ok"), sem("htl_ok")
        lg_mm, lg_ok, top_ok, gap_ok, at_ok, topf_ok = (sem(n) for n in ("lg_mm", "lg_ok", "top_ok", "gap_ok", "at_ok", "topf_ok"))
        ratio_ok, tot_ok, w1_ok, w2_ok = sem("ratio_ok"), sem("tot_ok"), sem("w1_ok"), sem("w2_ok")
        routes, route_ok = sem("routes"), sem("route_ok")
        up_mm = sem("up_mm")
        silu_ok = sem("silu_ok")
        inner_ok = sem("inner_ok")
        inh_ok, inl_ok = sem("inh_ok"), sem("inl_ok")
        down_mm = sem("down_mm")
        down_read = sem("down_read")

        PASSES = ((0, 0), (0, 1), (1, 0))
        front_tile = {e: e for e in range(BT)}
        NORM_AT, LOGITS_AT = BT + 1, BT + 2

        with nc.Block() as block:

            @block.sync
            def _(sp):
                sp.dma_start(xs[:, :, :], k["x"].rearrange("a (t p) d -> p (a t) d", p=P)).then_inc(dma["x2_in"], 16)
                for i, (n, kd) in enumerate(pieces):
                    if i == len(stage):
                        sp.wait_ge(w_lo, 1)
                        sp.dma_start(wo[:, :, :], k["wo"].rearrange("e p d -> p e d")).then_inc(dma["wo_in"], 16)
                    if i >= len(stage):
                        sp.wait_ge(w_lo, 2 + i - len(stage))
                    sp.dma_start(stage[i % len(stage)], k[f"wi_{n}"].rearrange("e (k p) m -> k p e m", p=P)[kd]).then_inc(wi_in[i], 16)
                sp.dma_start(wg[:, :, :], k["w_gate"].rearrange("(k p) e -> p k e", p=P)).then_inc(dma["wg_in"], 16)
                rows = k["out"].rearrange("a (t p) d -> p (a t) d", p=P)
                with sp.Fori(0, NB) as b:
                    sp.wait_ge(down_read, b * (BT * E) + (BT + BT * E))
                    sp.dma_start(rows[:, bass.ds(b * BT, BT), :], xs[:, bass.ds(b * BT, BT), :]).then_inc(dma["out_ok"], 16)
                sp.wait_ge(dma["out_ok"], 16 * NB)

            @block.gpsimd
            def _(pool):
                pool.iota(places[:, :], pattern=[[1, E]], base=0, channel_multiplier=0).then_inc(place_i, 1)
                pool.wait_ge(place_i, 1)
                pool.tensor_copy(placesf[:, :], places[:, :]).then_inc(place_f, 1)
                pool.wait_ge(rden_ok, 1)
                with pool.Fori(0, NB) as f:
                    for t in range(BT):
                        pool.wait_ge(flipped, f * (2 * BT) + (2 * t + 2))
                        tile = bass.ds(f * BT + t, 1)
                        pool.tensor_tensor(out=lat_n[:, t % 2], in0=lat[:, tile, :].rearrange("p a (h n) -> p (a h) n", h=H),
                                           in1=rden[:, tile, :].rearrange("p a h -> p (a h)").unsqueeze(2).to_broadcast([P, H, KVL]),
                                           op=ALU.mult).then_inc(latn_ok, 1)
                    pool.wait_ge(var2_ok, f + 1)
                    pool.tensor_tensor(out=rstd[:, :], in0=rstd[:, :], in1=neg_half[:, 0:BT], op=ALU.pow).then_inc(rstd2_ok, 1)

            @block.scalar
            def _(act):
                def flip_high(f, t, first=False):
                    if not (first and t == 0):
                        act.wait_ge(att_mm, f * BT + t)
                    for half in range(2):
                        act.wait_ge(flipped, f * (2 * BT) + (4 + 2 * t + half + 1))
                        act.activation(lat_hi[:, 4 * half:4 * half + 4, :].rearrange("p j n -> p (j n)"),
                                       front_bank[half][:, :], ACT.Copy).then_inc(lath_ok, 1)

                def normed(f):
                    for kd in range(KD):
                        act.wait_ge(xt2_mm, f * KD + (kd + 1))
                        act.activation(ht[:, kd, :], front_bank[kd][:, :], ACT.Identity, scale=modc[:, 3, kd:kd + 1],
                                       bias=modc[:, 2, kd:kd + 1]).then_inc(ht2_ok, 1)

                def normed_high(f):
                    act.wait_ge(ht2_ok, f * KD + KD)
                    for kd in range(KD):
                        act.activation(ht_hi[:, kd, :], ht[:, kd, :], ACT.Copy).then_inc(hth_ok, 1)

                def weight_ratio(f):
                    act.wait_ge(gap_ok, f + 1)
                    act.activation(ratio[:, :], gap[:, :], ACT.Exp).then_inc(ratio_ok, 1)

                def expert_silu(b, e):
                    act.wait_ge(up_mm, b * E + (e + 1))
                    act.wait_ge(inl_ok, b * E + (e + 1))
                    act.activation(silu[:, e % 2, :], up_bank[e % 2][0][:, :], ACT.Silu).then_inc(silu_ok, 1)

                def expert_high(b, e):
                    act.wait_ge(inner_ok, b * E + (2 + e + 1))
                    act.wait_ge(down_mm, b * (BT * E) + BT * (e + 1))
                    act.activation(inner_hi[:, e % 2, :], inner[:, e % 2, :], ACT.Copy).then_inc(inh_ok, 1)

                def turn(b, last):
                    f = b + 1
                    for e in range(E):
                        if e in front_tile and not last:
                            flip_high(f, front_tile[e])
                        if e < E - 1:
                            expert_silu(b, e + 1)
                            if e == LOGITS_AT and not last:
                                normed_high(f)
                            expert_high(b, e + 1)
                        elif not last:
                            expert_silu(f, 0)
                            expert_high(f, 0)
                            weight_ratio(f)
                        if e == NORM_AT and not last:
                            normed(f)

                act.activation(wvo_hi[:, :, :], w_vo[:, :, :], ACT.Copy).then_inc(w_hi, 1)
                flip_high(0, 0, True)
                for i, (n, kd) in enumerate(pieces):
                    act.wait_ge(wi_in[i], 16)
                    act.activation(wi_hi[n][:, kd], stage[i % len(stage)], ACT.Copy).then_inc(w_hi, 1)
                    if i == 1:
                        flip_high(0, 1, True)
                flip_high(0, 2, True)
                act.wait_ge(whole_ok, 1)
                act.activation(wo_hi[:, :, :], wo[:, :, :], ACT.Copy).then_inc(w_hi, 1)
                flip_high(0, 3, True)
                normed(0)
                normed_high(0)
                weight_ratio(0)
                expert_silu(0, 0)
                expert_high(0, 0)
                with act.Fori(0, NB - 1) as b:
                    turn(b, False)
                turn(NB - 1, True)

            @block.vector
            def _(dve):
                def flip_low(f, t, first=False):
                    if not (first and t == 0):
                        dve.wait_ge(att_mm, f * BT + t)
                    for half in range(2):
                        dve.wait_ge(lath_ok, f * (2 * BT) + (2 * t + half + 1))
                        hi = lat_hi[:, 4 * half:4 * half + 4, :].rearrange("p j n -> p (j n)")
                        dve.tensor_tensor(out=lat_lo[:, 4 * half:4 * half + 4, :].rearrange("p j n -> p (j n)"),
                                          in0=front_bank[half][:, :], in1=hi.bitcast(F32), op=ALU.subtract).then_inc(latl_ok, 1)

                def add_attention(f, t):
                    tile = xs[:, bass.ds(f * BT + t, 1), :].rearrange("p a d -> p (a d)")
                    dve.wait_ge(att_mm, f * BT + (t + 1))
                    dve.tensor_tensor(out=tile, in0=front_bank[0][:, 0:D], in1=tile, op=ALU.add).then_inc(y_ok, 1)
                    dve.wait_ge(y_ok, f * BT + (t + 1))
                    dve.memset(turnstile[:, :], 0.0)
                    dve.bn_stats(stats[:, t, :], tile).then_inc(st2_ok, 1)

                def normalise(f):
                    dve.wait_ge(st2_ok, f * BT + BT)
                    dve.memset(turnstile[:, :], 0.0)
                    for t in range(BT):
                        dve.bn_aggr(mv[:, t, :], stats[:, t, :]).then_inc(mv2_ok, 1)
                    dve.wait_ge(mv2_ok, f * BT + BT)
                    dve.tensor_scalar(rstd[:, :], mv[:, :, 1], LN_EPS, None, ALU.add).then_inc(var2_ok, 1)
                    dve.wait_ge(rstd2_ok, f + 1)
                    for t in range(BT):
                        tile = xs[:, bass.ds(f * BT + t, 1), :].rearrange("p a d -> p (a d)")
                        dve.tensor_scalar(xn[:, t, :], tile, mv[:, t, 0:1], rstd[:, t:t + 1], ALU.subtract,
                                          ALU.mult).then_inc(xn2_ok, 1)

                def normed_low(f):
                    for kd in range(KD):
                        dve.wait_ge(hth_ok, f * KD + (kd + 1))
                        dve.tensor_tensor(out=ht_lo[:, kd, :], in0=ht[:, kd, :], in1=ht_hi[:, kd, :].bitcast(F32),
                                          op=ALU.subtract).then_inc(htl_ok, 1)

                def choose(f):
                    dve.wait_ge(lg_mm, f + 1)
                    dve.tensor_copy(logits[:, :, :], front_bank[0][:, 0:BT * E].rearrange("p (t e) -> p t e", e=E)).then_inc(lg_ok, 1)
                    dve.wait_ge(lg_ok, f + 1)
                    dve.memset(turnstile[:, :], 0.0)
                    for t in range(BT):
                        dve.max(top[:, t, :], logits[:, t, :]).then_inc(top_ok, 1)
                    dve.wait_ge(top_ok, f * BT + BT)
                    dve.tensor_tensor(out=gap[:, :], in0=top[:, :, 1], in1=top[:, :, 0], op=ALU.subtract).then_inc(gap_ok, 1)
                    for t in range(BT):
                        dve.max_index(top_at[:, t, :], top[:, t, :], logits[:, t, :]).then_inc(at_ok, 1)
                    dve.wait_ge(at_ok, f * BT + BT)
                    dve.tensor_copy(top_f[:, :, :], top_at[:, :, 0:2]).then_inc(topf_ok, 1)

                def weigh(f):
                    dve.wait_ge(ratio_ok, f + 1)
                    dve.tensor_scalar(total[:, :], ratio[:, :], 1.0, None, ALU.add).then_inc(tot_ok, 1)
                    dve.wait_ge(tot_ok, f + 1)
                    dve.reciprocal(first_w[:, :], total[:, :]).then_inc(w1_ok, 1)
                    dve.wait_ge(w1_ok, f + 1)
                    dve.tensor_tensor(out=second_w[:, :], in0=ratio[:, :], in1=first_w[:, :], op=ALU.mult).then_inc(w2_ok, 1)
                    dve.wait_ge(topf_ok, f + 1)
                    dve.wait_ge(w2_ok, f + 1)
                    for t in range(BT):
                        for n, (to, w) in enumerate(((route1, first_w), (route2, second_w))):
                            dve.tensor_scalar(to[:, t, :], placesf[:, :], top_f[:, t, n:n + 1], w[:, t:t + 1], ALU.is_equal,
                                              ALU.mult).then_inc(routes, 1)
                    dve.wait_ge(routes, f * (2 * BT) + 2 * BT)
                    dve.tensor_tensor(out=route[:, :, :], in0=route1[:, :, :], in1=route2[:, :, :], op=ALU.add).then_inc(route_ok, 1)

                def expert_inner(b, e):
                    dve.wait_ge(silu_ok, b * E + (e + 1))
                    dve.tensor_tensor(out=inner[:, e % 2, :], in0=silu[:, e % 2, :], in1=up_bank[e % 2][1][:, :],
                                      op=ALU.mult).then_inc(inner_ok, 1)

                def expert_low(b, e):
                    dve.wait_ge(inh_ok, b * E + (e + 1))
                    dve.tensor_tensor(out=inner_lo[:, e % 2, :], in0=inner[:, e % 2, :], in1=inner_hi[:, e % 2, :].bitcast(F32),
                                      op=ALU.subtract).then_inc(inl_ok, 1)

                def expert_add(b, e):
                    for t in range(BT):
                        tile = xs[:, bass.ds(b * BT + t, 1), :].rearrange("p a d -> p (a d)")
                        dve.wait_ge(down_mm, b * (BT * E) + (2 * BT + BT * e + t // 2 * 2 + 2))
                        dve.scalar_tensor_tensor(out=tile, in0=down_bank[t // 2][:, (t % 2) * D:(t % 2) * D + D],
                                                 scalar=route[:, t, e:e + 1], in1=tile, op0=ALU.mult,
                                                 op1=ALU.add).then_inc(down_read, 1)

                def turn(b, last):
                    f = b + 1
                    dve.wait_ge(route_ok, f)
                    for e in range(E):
                        if e in front_tile and not last:
                            flip_low(f, front_tile[e])
                        if e < E - 1:
                            expert_inner(b, e + 1)
                            if e == LOGITS_AT and not last:
                                normed_low(f)
                            expert_low(b, e + 1)
                        elif not last:
                            expert_inner(f, 0)
                            expert_low(f, 0)
                        if e in front_tile and not last:
                            add_attention(f, front_tile[e])
                        expert_add(b, e)
                        if e == NORM_AT - 1 and not last:
                            normalise(f)
                        if e == LOGITS_AT and not last:
                            choose(f)
                    if not last:
                        weigh(f)

                dve.sem_inc(inner_ok, 2)
                dve.sem_inc(inl_ok, 2)
                dve.sem_inc(down_read, BT)
                dve.tensor_reduce(out=rden[:, :, :], in_=rowsum[:, :, 0:H, :], axis=AXX, op=ALU.add).then_inc(den_ok, 1)
                dve.wait_ge(den_ok, 1)
                dve.reciprocal(rden[:, :, :], rden[:, :, :]).then_inc(rden_ok, 1)
                dve.wait_ge(w_hi, 1)
                dve.tensor_tensor(out=wvo_lo[:, :, :], in0=w_vo[:, :, :], in1=wvo_hi[:, :, :].bitcast(F32),
                                  op=ALU.subtract).then_inc(w_lo, 1)
                flip_low(0, 0, True)
                dve.wait_ge(dma["wo_in"], 16)
                dve.tensor_tensor(out=wo[:, :, :], in0=wo[:, :, :],
                                  in1=gates[:, 1:2, :].to_broadcast([P, E, D]), op=ALU.mult).then_inc(whole_ok, 1)
                dve.wait_ge(dma["x2_in"], 16)
                add_attention(0, 0)
                for n in range(2):
                    flip_low(0, n + 1, True)
                    for kd in range(KD):
                        i = pieces.index((n, kd))
                        dve.wait_ge(w_hi, 2 + i)
                        dve.tensor_tensor(out=wi_lo[n][:, kd], in0=stage[i % len(stage)], in1=wi_hi[n][:, kd].bitcast(F32),
                                          op=ALU.subtract).then_inc(w_lo, 1)
                    add_attention(0, n + 1)
                dve.wait_ge(w_hi, 6)
                dve.tensor_tensor(out=wo_lo[:, :, :], in0=wo[:, :, :], in1=wo_hi[:, :, :].bitcast(F32),
                                  op=ALU.subtract).then_inc(w_lo, 1)
                flip_low(0, 3, True)
                add_attention(0, 3)
                normalise(0)
                normed_low(0)
                dve.wait_ge(place_f, 1)
                choose(0)
                expert_inner(0, 0)
                expert_low(0, 0)
                weigh(0)
                with dve.Fori(0, NB - 1) as b:
                    turn(b, False)
                turn(NB - 1, True)

            @block.tensor
            def _(pe):
                def flip(f, t):
                    pe.wait_ge(latn_ok, f * BT + (t + 1))
                    if t > 0:
                        pe.wait_ge(y_ok, f * BT + t)
                    flat = lat_n[:, t % 2].rearrange("p h n -> p (h n)")
                    for half in range(2):
                        for j in range(4):
                            at = (4 * half + j) * P
                            last = pe.transpose(front_bank[half][:, j * P:j * P + P], flat[:, at:at + P], ident[:, :])
                        last.then_inc(flipped, 1)

                def project(f, t):
                    pe.wait_ge(lath_ok, f * (2 * BT) + (2 * t + 2))
                    pe.wait_ge(latl_ok, f * (2 * BT) + (2 * t + 2))
                    for g in range(NP):
                        for a, w in PASSES:
                            last = pe.matmul(front_bank[0][:, 0:D], (lat_hi, lat_lo)[a][:, g, :], (wvo_hi, wvo_lo)[w][:, g, :],
                                             start=(g == 0 and a == w), stop=(g == NP - 1 and a == 1))
                    last.then_inc(att_mm, 1)

                def flip_normed(f):
                    pe.wait_ge(xn2_ok, f * BT + BT)
                    for kd in range(KD):
                        for t in range(BT):
                            last = pe.transpose(front_bank[kd][:, t * P:t * P + P], xn[:, t, kd * P:kd * P + P], ident[:, :])
                        last.then_inc(xt2_mm, 1)

                def gate(f):
                    pe.wait_ge(ht2_ok, f * KD + KD)
                    for t in range(BT):
                        for kd in range(KD):
                            last = pe.matmul(front_bank[0][:, t * E:t * E + E], ht[:, kd, t * P:t * P + P], wg[:, kd, :],
                                             start=(kd == 0), stop=(kd == KD - 1))
                    last.then_inc(lg_mm, 1)

                def up(b, e):
                    if e == 0:
                        pe.wait_ge(hth_ok, b * KD + KD)
                        pe.wait_ge(htl_ok, b * KD + KD)
                    pe.wait_ge(inner_ok, b * E + (e + 1))
                    for n in range(2):
                        for kd in range(KD):
                            for w, x in PASSES:
                                last = pe.matmul(up_bank[e % 2][n][:, :], (wi_hi, wi_lo)[w][n][:, kd, e, :],
                                                 (ht_hi, ht_lo)[x][:, kd, :], start=(kd == 0 and w == x),
                                                 stop=(kd == KD - 1 and w == 1))
                    last.then_inc(up_mm, 1)

                def down(b, e):
                    pe.wait_ge(inh_ok, b * E + (e + 1))
                    pe.wait_ge(inl_ok, b * E + (2 + e + 1))
                    for t in range(BT):
                        if t % 2 == 0:
                            pe.wait_ge(down_read, b * (BT * E) + (BT * e + t + 2))
                        to = down_bank[t // 2][:, (t % 2) * D:(t % 2) * D + D]
                        for a, w in PASSES:
                            last = pe.matmul(to, (inner_hi, inner_lo)[a][:, e % 2, t * P:t * P + P], (wo_hi, wo_lo)[w][:, e, :],
                                             start=(a == w), stop=(a == 1))
                        last.then_inc(down_mm, 1)

                def turn(b, last):
                    f = b + 1
                    for e in range(E):
                        if e in front_tile and not last:
                            if front_tile[e] == 0:
                                pe.wait_ge(lg_ok, f)
                            flip(f, front_tile[e])
                        if e < E - 1:
                            up(b, e + 1)
                        elif not last:
                            up(f, 0)
                        if e in front_tile and not last:
                            project(f, front_tile[e])
                        if e == NORM_AT and not last:
                            flip_normed(f)
                        if e == LOGITS_AT and not last:
                            gate(f)
                        down(b, e)

                pe.sem_inc(flipped, 4)
                pe.sem_inc(down_mm, 2 * BT)
                for t in range(BT):
                    flip(0, t)
                    if t == 0:
                        pe.wait_ge(w_lo, 1)
                    project(0, t)
                flip_normed(0)
                pe.wait_ge(dma["wg_in"], 16)
                gate(0)
                pe.wait_ge(w_lo, 2 + 2 * KD)
                up(0, 0)
                with pe.Fori(0, NB - 1) as b:
                    turn(b, False)
                turn(NB - 1, True)


NAMES = ["L0_attn_x", "L0_attn_w_qa", "L0_attn_q_a_norm_w", "L0_attn_w_qb", "L0_attn_w_kva", "L0_attn_kv_a_norm_w",
         "L0_attn_w_kvb", "L0_attn_w_o", "L0_ffn_w_gate", "L0_ffn_wi_0", "L0_ffn_wi_1", "L0_ffn_wo", "L0_c", "L0_wmod"]


def rotary_tables():
    inv = (np.float32(1.0) / np.float32(10000.0) ** (np.arange(0, DR, 2, dtype=np.float32) / np.float32(DR))).astype(np.float32)
    freqs = np.outer(np.arange(S, dtype=np.float32), inv).astype(np.float32)
    emb = np.concatenate((freqs, freqs), -1)
    return np.cos(emb).astype(np.float32), np.sin(emb).astype(np.float32)


def kernel(**inputs):
    import concourse.bacc as bacc
    from concourse.bass_utils import run_bass_kernel_spmd

    nc = bacc.Bacc("TRN2", target_bir_lowering=False, num_devices=1)
    cos, sin = rotary_tables()
    signs = np.where(np.arange(DR) % 2 == 0, np.float32(-1), np.float32(1))
    grouped = [np.ascontiguousarray(t.reshape(BT, NG, P, DR).transpose(3, 1, 0, 2).reshape(DR, S)) for t in (cos, sin)]
    tables = {"rope_cos_by_feature": grouped[0], "rope_sin_by_feature": grouped[1],
              "rope_cos_by_token": cos, "rope_sin_by_token": sin * signs}
    arrays = {f"in_{n}": np.ascontiguousarray(inputs[n]) for n in NAMES} | tables
    args = [nc.dram_tensor(n, a.shape, mybir.dt.from_np(a.dtype), kind="ExternalInput").ap() for n, a in arrays.items()]
    out = nc.dram_tensor("out_0", (1, S, D), F32, kind="ExternalOutput").ap()
    adaln_block_kernel(nc, *args, out)
    result = run_bass_kernel_spmd(nc, [arrays], core_ids=[0])
    return result.results[0]["out_0"]
```

```python
import math
from contextlib import ExitStack

import numpy as np

import concourse.bass as bass
import concourse.mybir as mybir

F32 = mybir.dt.float32
F32R = mybir.dt.float32r
BF16 = mybir.dt.bfloat16
F16 = mybir.dt.float16
U32 = mybir.dt.uint32
ACT = mybir.ActivationFunctionType
ALU = mybir.AluOpType
AXX = mybir.AxisListType.X

P = 128
S, D = 2048, 256
H, QL, KVL = 16, 96, 64
DN, DR, DV = 128, 64, 128
E, M = 8, 128
NT = S // P
NP = H // 2
KD = D // P
BT = 4
NB = NT // BT
BW = BT * P
SCALE = 1.0 / math.sqrt(DN + DR)
LN_EPS, RMS_EPS = 1e-5, 1e-6
MASKED = -1.0e30
P_SCALE = 1024.0

NG = NT // BT
ITEMS = [(g + NG * j, h) for g in range(NG) for j in ((0, 1, 2, 3) if g % 2 else (3, 2, 1, 0)) for h in range(2)]
NI = len(ITEMS)
CHUNKS = []
FIRST = []
for _k, (_i, _h) in enumerate(ITEMS):
    FIRST.append(len(CHUNKS))
    for _c in range(_i // 4 + 1):
        CHUNKS.append((_k, _c, min(4, _i + 1 - 4 * _c)))
NC = len(CHUNKS)
FIRST.append(NC)
S_RING, P_RING, PT_RING, MX_RING = 5, 8, 5, 8
assert NC % S_RING == NC % P_RING == NC % PT_RING == NI % MX_RING == 0
CREDIT = 32
ROUNDS = range(2, NI + 2)
PREP = {2 * BT * c + (1 if c % 2 else 2): c for c in range(NG)}
PART_ROUNDS = (0, 0, 1)
ADD_ROUND = 2
PREP_READS = ({"v": 1, "a": 1}, {"v": 1, "a": 1}, {"v": 1})


def chunks_of(item):
    ahead, k = divmod(item, NI)
    return [ahead * NC + s for s in range(FIRST[k], FIRST[k + 1])]


def evac_on_vector(s):
    return CHUNKS[s % NC][1] == 2


def low_on_vector(s):
    return CHUNKS[s % NC][1] == 0


def prep_parts(r):
    return [(c, part) for start, c in PREP.items() for part, after in enumerate(PART_ROUNDS) if start + after == r]


def prep_sums(r):
    return [c for start, c in PREP.items() if start + ADD_ROUND == r]


USES = []
for _r in ROUNDS:
    USES += [("t", s) for s in chunks_of(_r - 1)] + [("q", c, part) for c, part in prep_parts(_r)]
NU = len(USES)
assert NU % 2 == 0
USE = {u: n for n, u in enumerate(USES)}


def use_of(s):
    turn, at = divmod(s - FIRST[1], NC)
    return turn * NU + USE["t", FIRST[1] + at]


def readers(u):
    if u[0] == "q":
        return PREP_READS[u[2]]
    return {"v" if evac_on_vector(u[1]) else "a": 1}


def reads(e, n):
    return sum(readers(u).get(e, 0) for u in USES[:n])


READS = {e: reads(e, NU) for e in "av"}
FIRST_READS = {e: sum(r.get(e, 0) for r in PREP_READS) for e in "av"}
BASE_READS = {e: CREDIT + FIRST_READS[e] + READS[e] - reads(e, NU - FIRST[1]) for e in "av"}
BASE_USES = CREDIT + len(PREP_READS) + FIRST[1]


def lows(e, n):
    return sum(low_on_vector(s) == (e == "v") for s in range(n))


LOWS = {e: lows(e, NC) for e in "vp"}
MANY = [s for s in range(NC) if ITEMS[CHUNKS[s][0]][0] >= 4]


def adaln_block_kernel(nc, x, w_qa, q_norm, w_qb, w_kva, kv_norm, w_kvb, w_o, w_gate, wi_0, wi_1, wo, c, wmod,
                       cos_t, sin_t, cos_k, sin_k, out):
    stack = ExitStack()

    def sb(scope, name, shape, dt=F32):
        return scope.enter_context(nc.sbuf_tensor(name, shape, dt))

    def sem(name):
        return stack.enter_context(nc.semaphore(name))

    with stack:
        bank = [stack.enter_context(nc.psum_tensor(f"bank{n}", [P, BW], F32)) for n in range(8)]

        lat = sb(stack, "lat", [P, NT, H * KVL])
        w_vo = sb(stack, "w_vo", [P, NP, D])
        rowsum = sb(stack, "rowsum", [P, NT, H + 2, 4])
        ident = sb(stack, "ident", [P, P])
        gates = sb(stack, "gates", [P, 2, D])
        modc = sb(stack, "modc", [P, 4, KD])
        neg_half = sb(stack, "neg_half", [P, NT])
        turnstile = sb(stack, "turnstile", [P, 1])

        attn = ExitStack()
        kt_a_hi = sb(attn, "kt_a_hi", [P, S], F32R)
        kt_a_lo = sb(attn, "kt_a_lo", [P, S], F32R)
        kt_b_hi = sb(attn, "kt_b_hi", [P, S], F32R)
        kt_b_lo = sb(attn, "kt_b_lo", [P, S], F32R)
        ql_hi = sb(attn, "ql_hi", [QL, NG, BT, P], F32R)
        ql_lo = sb(attn, "ql_lo", [QL, NG, BT, P], F32R)
        values = sb(attn, "values", [P, NT, 2 * KVL], F16)
        cos2 = sb(attn, "cos2", [P, S])
        sin2 = sb(attn, "sin2", [P, S])
        ident16 = sb(attn, "ident16", [P, P], BF16)
        mask16 = sb(attn, "mask16", [P, P], BF16)
        wq_dram = nc.dram_tensor("wq_parts", (2, NP + 1, QL, 3 * P), F32, kind="Internal").ap()

        prepare(nc, sb, sem, locals())
        attend(nc, sb, sem, locals())
        attn.close()
        experts(nc, sb, sem, locals())


def prepare(nc, sb, sem, k):
    bank, lat, ident, modc, gates, neg_half = k["bank"], k["lat"], k["ident"], k["modc"], k["gates"], k["neg_half"]
    turnstile = k["turnstile"]
    w_vo, wq_dram, values, ident16, mask16 = k["w_vo"], k["wq_dram"], k["values"], k["ident16"], k["mask16"]
    kt = [(k["kt_a_hi"], k["kt_a_lo"]), (k["kt_b_hi"], k["kt_b_lo"]), (k["ql_hi"], k["ql_lo"])]
    with ExitStack() as own:
        flat = lat[:, :, :].rearrange("p t n -> p (t n)")
        ends = np.cumsum([0, H * (DN + DR), H * (DN + DV), H * D, KD * 6 * D, NT * DR, NT * DR]).tolist()
        wqb, wkvb, wov, wm, ck, sk = (flat[:, a:b] for a, b in zip(ends[:-1], ends[1:]))
        wqb = wqb[0:QL].rearrange("p (h n) -> p h n", h=H)
        wkvb = wkvb[0:KVL].rearrange("p (h n) -> p h n", h=H)
        wov = wov.rearrange("p (h n) -> p h n", h=H)
        wm = wm.rearrange("p (k n) -> p k n", k=KD)
        ck = ck.rearrange("p (t n) -> p t n", t=NT)
        sk = sk.rearrange("p (t n) -> p t n", t=NT)
        xs = sb(own, "xs", [P, NT, D])
        wa = sb(own, "wa", [P, KD, QL + KVL + DR])
        qnw = sb(own, "qnw", [QL, 1])
        kvnw = sb(own, "kvnw", [KVL, 1])
        wqb_t = sb(own, "wqb_t", [P, H, QL])
        wk_t = sb(own, "wk_t", [P, H, KVL])
        wv_t = sb(own, "wv_t", [P, H, KVL])
        wq_hi = sb(own, "wq_hi", [QL, NP, 3 * P], F32R)
        wq_lo = sb(own, "wq_lo", [QL, NP, 3 * P], F32R)
        ccol = sb(own, "ccol", [P, KD])
        csilu = sb(own, "csilu", [P, KD])
        crep = sb(own, "crep", [P, KD, P])
        stats = sb(own, "stats", [P, NT, 6])
        mv = sb(own, "mv", [P, NT, 2])
        rstd = sb(own, "rstd", [P, NT])
        junk = sb(own, "junk", [P, BT, QL + KVL])
        size = junk[:, :, :].rearrange("p t n -> p (t n)")[:, 0:2 * D]
        ms = sb(own, "ms", [P, BT, 2])
        rms = sb(own, "rms", [P, BT, 2])
        kk_place, xn_place, ht_place = (w[:, :, :].rearrange("p h n -> p (h n)") for w in (wv_t, wqb_t, wk_t))
        xn = xn_place[:, 0:BT * D].rearrange("p (t n) -> p t n", t=BT)
        qn = xn_place[:, BT * D:BT * (D + QL)].rearrange("p (t n) -> p t n", t=BT)
        ht = ht_place.rearrange("p (k n) -> p k n", k=KD)
        n_kk = BT * (2 * KVL + DR)
        kk = kk_place[:, 0:n_kk].rearrange("p (t n) -> p t n", t=BT)
        krot = kk_place[:, n_kk:n_kk + BT * DR].rearrange("p (t n) -> p t n", t=BT)

        ld_c, ld_mod, ld_x, ld_qb, ld_kvb = sem("ld_c"), sem("ld_mod"), sem("ld_x"), sem("ld_qb"), sem("ld_kvb")
        ld_o, ld_a, ld_rope, consts, wq_out = sem("ld_o"), sem("ld_a"), sem("ld_rope"), sem("consts"), sem("wq_out")
        silu_c, crep_ok, mod_mm, mod_ok, gate_ok = (sem(n) for n in ("silu_c", "crep_ok", "mod_mm", "mod_ok", "gate_ok"))
        gate_parts, wscaled, wt_mm = sem("gate_parts"), sem("wscaled"), sem("wt_mm")
        wt_a, wt_v, abs_mm, wqh_ok, wql_ok = sem("wt_a"), sem("wt_v"), sem("abs_mm"), sem("wqh_ok"), sem("wql_ok")
        vo_mm, vo_ok = sem("vo_mm"), sem("vo_ok")
        st_ok, mv_ok, var_ok, rstd_ok, xn_ok, xt_mm = (sem(n) for n in ("st_ok", "mv_ok", "var_ok", "rstd_ok", "xn_ok", "xt_mm"))
        ht_ok, a_mm, ms_ok, mse_ok, rms_ok, kk_v, kk_a, kk_ok, kk_mm, hi_ok, lo_ok, vh_ok, vl_ok = (
            sem(n) for n in ("ht_ok", "a_mm", "ms_ok", "mse_ok", "rms_ok", "kk_v", "kk_a", "kk_ok", "kk_mm", "hi_ok", "lo_ok", "vh_ok", "vl_ok"))

        groups = [("k", g) for g in range(2)] + [("v", g) for g in range(2)] + [("q", g) for g in range(4)]

        def group_out(kind, g):
            if kind == "q":
                return wqb_t[:, 4 * g:4 * g + 4, :], bank[g][:, :].rearrange("p (h n) -> p h n", h=4)[:, :, 0:QL]
            n = 4 + g if kind == "k" else 6 + g
            to = wk_t if kind == "k" else wv_t
            return to[:, 8 * g:8 * g + 8, :], bank[n][:, :].rearrange("p (h n) -> p h n", h=8)

        even, odd = (wqb.rearrange("p (g two) n -> p g two n", two=2)[:, :, :, DN:].rearrange(
            "p g two (i e) -> p g two i e", e=2)[:, :, :, :, e] for e in range(2))

        def pair_cols(w, at, e):
            return w[:, :, at:at + DR].rearrange("p g (i e) -> p g i e", e=2)[:, :, :, e]

        moves = []
        for at, hd in ((KVL, 0), (P, 1)):
            moves += [(at, 0, even[:, :, hd], 1.0), (at, 1, odd[:, :, hd], 1.0)]
        for at, hd in ((2 * P, 1), (2 * P + DR, 0)):
            moves += [(at, 0, odd[:, :, hd], -1.0), (at, 1, even[:, :, hd], 1.0)]

        def block_of(w, n, b):
            return w[:, :, bass.ds(b, 1), :].rearrange("p g a n -> p g (a n)") if n == 2 else w[:, bass.ds(b * BW, BW)]

        def product_of(n):
            return bank[6][0:QL, :].rearrange("p (g n) -> p g n", n=P) if n == 2 else bank[6 + n][:, :]

        def abs_view(w, g, hd):
            at = 0 if hd == 0 else P + DR
            return w[:, 4 * g:4 * g + 4, at:at + KVL], bank[g][0:QL, :].rearrange(
                "p (j two n) -> p j two n", two=2, n=KVL)[:, :, hd, :]

        with nc.Block() as block:

            @block.sync
            def _(sp):
                sp.dma_start(wqb, k["w_qb"].rearrange("p (h n) -> p h n", h=H)).then_inc(ld_qb, 16)
                for kd in range(KD):
                    sp.dma_start(ccol[:, kd:kd + 1], k["c"][0, kd * P:kd * P + P].rearrange("(p a) -> p a", a=1)).then_inc(ld_c, 16)
                sp.dma_start(qnw[:, :], k["q_norm"].rearrange("(p a) -> p a", a=1)).then_inc(ld_qb, 16)
                sp.dma_start(wm, k["wmod"].rearrange("(k p) n -> p k n", p=P)).then_inc(ld_mod, 16)
                sp.dma_start(wa[:, :, 0:QL], k["w_qa"].rearrange("(k p) n -> p k n", p=P)).then_inc(ld_a, 16)
                sp.dma_start(wa[:, :, QL:], k["w_kva"].rearrange("(k p) n -> p k n", p=P)).then_inc(ld_a, 16)
                sp.dma_start(wov, k["w_o"].rearrange("(h p) n -> p h n", p=P)).then_inc(ld_o, 16)
                sp.wait_ge(wqh_ok, 4 + len(moves))
                sp.wait_ge(wql_ok, 4 + len(moves))
                for part, w in enumerate((wq_hi, wq_lo)):
                    raw = w[:, :, :].bitcast(F32)
                    sp.dma_start(wq_dram[part, 0:NP].rearrange("g p n -> p g n"), raw).then_inc(wq_out, 16)
                    sp.dma_start(wq_dram[part, NP:NP + 1].rearrange("g p n -> p g n"), raw[:, 0:1, :]).then_inc(wq_out, 16)
                sp.wait_ge(wq_out, 64)

            @block.gpsimd
            def _(pool):
                pool.memset(ident[:, :], 0.0).then_inc(consts, 1)
                pool.memset(ident16[:, :], 0.0).then_inc(consts, 1)
                pool.memset(mask16[:, :], 0.0).then_inc(consts, 1)
                pool.memset(neg_half[:, :], -0.5).then_inc(consts, 1)
                pool.wait_ge(consts, 4)
                for m in (ident, ident16):
                    pool.affine_select(out=m[:, :], in_=m[:, :], compare_op=ALU.not_equal, fill=1.0, base=0,
                                       pattern=[[-1, P]], channel_multiplier=1).then_inc(consts, 1)
                pool.affine_select(out=mask16[:, :], in_=mask16[:, :], compare_op=ALU.is_ge, fill=MASKED, base=0,
                                   pattern=[[-1, P]], channel_multiplier=1).then_inc(consts, 1)
                pool.wait_ge(var_ok, 1)
                pool.tensor_tensor(out=rstd[:, :], in0=rstd[:, :], in1=neg_half[:, :], op=ALU.pow).then_inc(rstd_ok, 1)
                with pool.Fori(0, NB) as b:
                    pool.wait_ge(mse_ok, b + 1)
                    pool.tensor_tensor(out=rms[:, :, :].rearrange("p t n -> p (t n)"),
                                       in0=rms[:, :, :].rearrange("p t n -> p (t n)"), in1=neg_half[:, 0:2 * BT],
                                       op=ALU.pow).then_inc(rms_ok, 1)
                    pool.wait_ge(kk_v, b * 12 + 12)
                    pool.tensor_tensor(out=kk[:, :, KVL:KVL + DR], in0=kk[:, :, KVL:KVL + DR], in1=krot[:, :, :],
                                       op=ALU.add).then_inc(kk_ok, 1)
                    pool.wait_ge(kk_a, b * (3 * BT) + 3 * BT)
                    vb = values[:, bass.ds(b * BT, BT), :]
                    pool.tensor_copy(vb[:, :, 0:KVL], kk[:, :, 0:KVL]).then_inc(vh_ok, 1)
                    pool.wait_ge(vh_ok, b + 1)
                    pool.tensor_tensor(out=vb[:, :, KVL:], in0=kk[:, :, 0:KVL], in1=vb[:, :, 0:KVL],
                                       op=ALU.subtract).then_inc(vl_ok, 1)

            @block.scalar
            def _(act):
                act.dma_start(kvnw[:, :], k["kv_norm"].rearrange("(p a) -> p a", a=1)).then_inc(ld_kvb, 16)
                act.dma_start(wkvb, k["w_kvb"].rearrange("p (h n) -> p h n", h=H)).then_inc(ld_kvb, 16)
                act.dma_start(xs[:, :, :], k["x"].rearrange("a (t p) d -> p (a t) d", p=P)).then_inc(ld_x, 16)
                act.dma_start(ck[:, :, :], k["cos_k"].rearrange("(t p) n -> p t n", p=P)).then_inc(ld_rope, 16)
                act.dma_start(sk[:, :, :], k["sin_k"].rearrange("(t p) n -> p t n", p=P)).then_inc(ld_rope, 16)
                for half in range(2):
                    act.dma_start(k["cos2"][half * DR:half * DR + DR, :], k["cos_t"]).then_inc(ld_rope, 16)
                    act.dma_start(k["sin2"][half * DR:half * DR + DR, :], k["sin_t"]).then_inc(ld_rope, 16)
                act.wait_ge(ld_c, 16 * KD)
                act.activation(csilu[:, :], ccol[:, :], ACT.Silu).then_inc(silu_c, 1)
                for n, (kind, g) in enumerate(groups):
                    if n % 2 == 0:
                        act.wait_ge(wt_mm, n + 1)
                        to, of = group_out(kind, g)
                        act.activation(to, of, ACT.Copy).then_inc(wt_a, 1)
                act.wait_ge(wscaled, 2)
                for at, e, of, sgn in moves:
                    act.activation(pair_cols(wq_hi, at, e), of, ACT.Copy, scale=sgn).then_inc(wqh_ok, 1)
                for g in range(2):
                    act.wait_ge(abs_mm, g + 1)
                    for hd in range(2):
                        to, of = abs_view(wq_hi, g, hd)
                        act.activation(to, of, ACT.Copy).then_inc(wqh_ok, 1)
                act.wait_ge(mod_ok, 2)
                def normed(b):
                    for kd in range(KD):
                        act.wait_ge(xt_mm, b * KD + kd + 1)
                        act.activation(ht[:, kd, :], bank[kd][:, :], ACT.Identity, scale=modc[:, 1, kd:kd + 1],
                                       bias=modc[:, 0, kd:kd + 1]).then_inc(ht_ok, 1)

                def turn(b, last):
                    for t in range(BT):
                        act.wait_ge(a_mm, b * BT + t + 1)
                        of = bank[2 + t][:, :]
                        for n, (a, w) in enumerate(((0, QL), (QL, KVL))):
                            act.activation(junk[:, t, a:a + w], of[:, a:a + w], ACT.Square, scale=1.0 / math.sqrt(w),
                                           accum_out=ms[:, t, n:n + 1]).then_inc(ms_ok, 1)
                    act.wait_ge(rms_ok, b + 1)
                    for t in range(BT):
                        of = bank[2 + t][:, :]
                        act.wait_ge(kk_v, b * (3 * BT) + 3 * t + 3)
                        act.activation(qn[:, t, :], of[:, 0:QL], ACT.Copy, scale=rms[:, t, 0:1]).then_inc(kk_a, 1)
                        for at in (0, KVL + DR):
                            act.activation(kk[:, t, at:at + KVL], of[:, QL:QL + KVL], ACT.Copy,
                                           scale=rms[:, t, 1:2]).then_inc(kk_a, 1)
                    if not last:
                        normed(b + 1)
                    for n, (hi, _) in enumerate(kt):
                        act.wait_ge(kk_mm, b * 3 + n + 1)
                        act.activation(block_of(hi, n, b), product_of(n), ACT.Copy).then_inc(hi_ok, 1)

                normed(0)
                with act.Fori(0, NB - 1) as b:
                    turn(b, False)
                turn(NB - 1, True)

            @block.vector
            def _(dve):
                dve.sem_inc(lo_ok, 3)
                dve.wait_ge(ld_kvb, 32)
                dve.tensor_scalar(wkvb, wkvb, kvnw[:, :], None, ALU.mult).then_inc(wscaled, 1)
                dve.wait_ge(ld_qb, 32)
                dve.tensor_scalar(wqb, wqb, qnw[:, :], SCALE, ALU.mult, ALU.mult).then_inc(wscaled, 1)
                dve.wait_ge(silu_c, 1)
                for kd in range(KD):
                    dve.tensor_copy(crep[:, kd, :], csilu[:, kd:kd + 1].to_broadcast([P, P])).then_inc(crep_ok, 1)
                for n, (kind, g) in enumerate(groups):
                    if n % 2 == 1:
                        dve.wait_ge(wt_mm, n + 1)
                        to, of = group_out(kind, g)
                        dve.tensor_copy(to, of).then_inc(wt_v, 1)
                dve.wait_ge(ld_x, 16)
                for t in range(NT):
                    dve.bn_stats(stats[:, t, :], xs[:, t, :]).then_inc(st_ok, 1)
                dve.wait_ge(st_ok, NT)
                for t in range(NT):
                    dve.bn_aggr(mv[:, t, :], stats[:, t, :]).then_inc(mv_ok, 1)
                dve.wait_ge(mv_ok, NT)
                dve.tensor_scalar(rstd[:, :], mv[:, :, 1], LN_EPS, None, ALU.add).then_inc(var_ok, 1)
                for n, (at, e, of, sgn) in enumerate(moves):
                    dve.wait_ge(wqh_ok, n + 1)
                    hi = pair_cols(wq_hi, at, e).bitcast(F32)
                    dve.scalar_tensor_tensor(out=pair_cols(wq_lo, at, e), in0=of, scalar=sgn, in1=hi, op0=ALU.mult,
                                             op1=ALU.subtract).then_inc(wql_ok, 1)
                for g in range(2):
                    for hd in range(2):
                        dve.wait_ge(wqh_ok, len(moves) + 2 * g + 2)
                        to, of = abs_view(wq_lo, g, hd)
                        hi, _ = abs_view(wq_hi, g, hd)
                        dve.tensor_tensor(out=to, in0=of, in1=hi.bitcast(F32), op=ALU.subtract).then_inc(wql_ok, 1)
                dve.wait_ge(mod_mm, 1)
                dve.tensor_copy(modc[:, :, :], bank[6][:, 0:4 * KD].rearrange("p (j k) -> p j k", k=KD)).then_inc(mod_ok, 1)
                dve.wait_ge(mod_ok, 1)
                odd_rows = modc[:, :, :].rearrange("p (a two) k -> p a two k", two=2)[:, :, 1, :]
                dve.tensor_scalar(odd_rows, odd_rows, 1.0, None, ALU.add).then_inc(mod_ok, 1)
                dve.wait_ge(mod_mm, 2)
                raw = bank[7][:, :]
                both = gates[:, :, :].rearrange("p a n -> p (a n)")
                dve.tensor_scalar(both, raw, 0.0, 2.0, ALU.is_ge, ALU.mult).then_inc(gate_parts, 1)
                dve.wait_ge(gate_parts, 1)
                dve.tensor_scalar(size[:, :], raw, -1.0, None, ALU.mult).then_inc(gate_parts, 1)
                dve.wait_ge(gate_parts, 2)
                dve.tensor_tensor(out=size[:, :], in0=raw, in1=size[:, :], op=ALU.max).then_inc(gate_parts, 1)
                dve.wait_ge(gate_parts, 3)
                dve.tensor_scalar(size[:, :], size[:, :], 0.25, None, ALU.max).then_inc(gate_parts, 1)
                dve.wait_ge(gate_parts, 4)
                dve.scalar_tensor_tensor(out=both, in0=both, scalar=-1.0, in1=size[:, :], op0=ALU.add, op1=ALU.mult).then_inc(gate_ok, 1)
                dve.wait_ge(gate_ok, 1)
                for n in range(NP // 2):
                    dve.wait_ge(vo_mm, n + 1)
                    dve.tensor_tensor(out=w_vo[:, 2 * n:2 * n + 2, :], in0=bank[2 + n][:, :].rearrange("p (a n) -> p a n", a=2),
                                      in1=gates[:, 0:1, :].to_broadcast([P, 2, D]), op=ALU.mult).then_inc(vo_ok, 1)
                dve.wait_ge(ld_rope, 96)

                def normalise(b):
                    for t in range(BT):
                        dve.tensor_scalar(xn[:, t, :], xs[:, bass.ds(b * BT + t, 1), :].rearrange("p a d -> p (a d)"),
                                          mv[:, bass.ds(b * BT + t, 1), 0:1].rearrange("p a n -> p (a n)"),
                                          rstd[:, bass.ds(b * BT + t, 1)], ALU.subtract, ALU.mult).then_inc(xn_ok, 1)

                def turn(b, last):
                    if not last:
                        dve.wait_ge(xt_mm, b * KD + KD)
                        dve.memset(turnstile[:, :], 0.0)
                        normalise(b + 1)
                    dve.wait_ge(ms_ok, b * 2 * BT + 2 * BT)
                    dve.tensor_scalar(rms[:, :, :], ms[:, :, :], RMS_EPS, None, ALU.add).then_inc(mse_ok, 1)
                    for t in range(BT):
                        rope = bank[2 + t][:, QL + KVL:QL + KVL + DR]
                        ckt = ck[:, bass.ds(b * BT + t, 1), :].rearrange("p a n -> p (a n)")
                        skt = sk[:, bass.ds(b * BT + t, 1), :].rearrange("p a n -> p (a n)").rearrange("p (i e) -> p i e", e=2)
                        dve.tensor_tensor(out=kk[:, t, KVL:KVL + DR], in0=rope, in1=ckt, op=ALU.mult).then_inc(kk_v, 1)
                        swapped = rope.rearrange("p (i e) -> p i e", e=2)
                        to = krot[:, t, :].rearrange("p (i e) -> p i e", e=2)
                        for e in range(2):
                            dve.tensor_tensor(out=to[:, :, e], in0=swapped[:, :, 1 - e], in1=skt[:, :, e],
                                              op=ALU.mult).then_inc(kk_v, 1)
                    for n, (hi, lo) in enumerate(kt):
                        dve.wait_ge(hi_ok, b * 3 + n + 1)
                        dve.tensor_tensor(out=block_of(lo, n, b), in0=product_of(n), in1=block_of(hi, n, b).bitcast(F32),
                                          op=ALU.subtract).then_inc(lo_ok, 1)

                dve.wait_ge(rstd_ok, 1)
                normalise(0)
                with dve.Fori(0, NB - 1) as b:
                    turn(b, False)
                turn(NB - 1, True)

            @block.tensor
            def _(pe):
                pe.wait_ge(consts, 7)
                pe.wait_ge(wscaled, 1)
                for kind, g in groups:
                    n, step, rows, of = {"q": (g, 4, QL, wqb), "k": (4 + g, 8, KVL, wkvb), "v": (6 + g, 8, KVL, wkvb)}[kind]
                    at = DN if kind == "v" else 0
                    if kind == "q":
                        pe.wait_ge(wscaled, 2)
                    for j in range(step):
                        last = pe.transpose(bank[n][:, j * (BW // step):j * (BW // step) + rows],
                                            of[:, step * g + j, at:at + P], ident[0:rows, 0:rows])
                    last.then_inc(wt_mm, 1)
                pe.wait_ge(wt_a, 4)
                pe.wait_ge(wt_v, 4)
                for g in range(2):
                    for j in range(8):
                        last = pe.matmul(bank[g][0:QL, j * KVL:j * KVL + KVL], wqb_t[:, 8 * g + j, :], wk_t[:, 8 * g + j, :],
                                         start=True, stop=True)
                    last.then_inc(abs_mm, 1)
                pe.wait_ge(ld_mod, 16)
                pe.wait_ge(silu_c, 1)
                for j, part in enumerate((0, 1, 3, 4)):
                    for kd in range(KD):
                        at = part * D + kd * P
                        for kk_ in range(KD):
                            last = pe.matmul(bank[6][:, j * KD + kd:j * KD + kd + 1], wm[:, kk_, at:at + P],
                                             csilu[:, kk_:kk_ + 1], start=(kk_ == 0), stop=(kk_ == KD - 1))
                last.then_inc(mod_mm, 1)
                pe.wait_ge(crep_ok, KD)
                for j, part in enumerate((2, 5)):
                    for kk_ in range(KD):
                        last = pe.matmul(bank[7][:, j * D:j * D + D], crep[:, kk_, :], wm[:, kk_, part * D:part * D + D],
                                         start=(kk_ == 0), stop=(kk_ == KD - 1))
                last.then_inc(mod_mm, 1)
                pe.wait_ge(ld_o, 16)
                for n in range(NP // 2):
                    for j in range(4):
                        h = 4 * n + j
                        last = pe.matmul(bank[2 + n][(h % 2) * KVL:(h % 2) * KVL + KVL, (j // 2) * D:(j // 2) * D + D],
                                         wv_t[:, h, :], wov[:, h, :], start=True, stop=True)
                    last.then_inc(vo_mm, 1)
                pe.wait_ge(wql_ok, 4 + len(moves))
                pe.wait_ge(vo_ok, NP // 2)
                pe.wait_ge(ld_a, 32)

                def flip(b):
                    pe.wait_ge(xn_ok, b * BT + BT)
                    for kd in range(KD):
                        for t in range(BT):
                            last = pe.transpose(bank[kd][:, t * P:t * P + P], xn[:, t, kd * P:kd * P + P], ident[:, :])
                        last.then_inc(xt_mm, 1)

                def turn(b, last_turn):
                    pe.wait_ge(ht_ok, b * KD + KD)
                    for t in range(BT):
                        for kd in range(KD):
                            last = pe.matmul(bank[2 + t][:, 0:QL + KVL + DR], ht[:, kd, t * P:t * P + P], wa[:, kd, :],
                                             start=(kd == 0), stop=(kd == KD - 1))
                        last.then_inc(a_mm, 1)
                    if not last_turn:
                        flip(b + 1)
                    pe.wait_ge(kk_ok, b + 1)
                    pe.wait_ge(kk_a, b * (3 * BT) + 3 * BT)
                    for n, at in enumerate((0, KVL)):
                        pe.wait_ge(lo_ok, b * 3 + 3)
                        for t in range(BT):
                            last = pe.transpose(bank[6 + n][:, t * P:t * P + P], kk[:, t, at:at + P], ident[:, :])
                        last.then_inc(kk_mm, 1)
                    pe.wait_ge(lo_ok, b * 3 + (3 + 1))
                    for t in range(BT):
                        last = pe.transpose(bank[6][0:QL, t * P:t * P + P], qn[:, t, :], ident[:, :])
                    last.then_inc(kk_mm, 1)

                flip(0)
                with pe.Fori(0, NB - 1) as b:
                    turn(b, False)
                turn(NB - 1, True)


def attend(nc, sb, sem, k):
    bank, lat, rowsum, ident, wq_dram, values = k["bank"], k["lat"], k["rowsum"], k["ident"], k["wq_dram"], k["values"]
    cos2, sin2, ident16, mask16 = k["cos2"], k["sin2"], k["ident16"], k["mask16"]
    kt_hi, kt_lo = (k["kt_a_hi"], k["kt_b_hi"]), (k["kt_a_lo"], k["kt_b_lo"])
    ql = (k["ql_hi"], k["ql_lo"])
    BEFORE = len(PREP_READS) + FIRST[1]
    s_bank, t_bank, o_bank = bank[0:S_RING], bank[S_RING:S_RING + 2], bank[S_RING + 2]
    with ExitStack() as own:
        wq = [sb(own, f"wq_pair_{p}", [QL, 3 * P], F32R) for p in ("hi", "lo")]
        q_hi = sb(own, "q_hi", [P, 2, 2, BW], F32R)
        q_lo = sb(own, "q_lo", [P, 2, 2, BW], F32R)
        qf = sb(own, "qf", [P, 2, BW])
        qs = sb(own, "qs", [P, BW])
        probs = sb(own, "probs", [P, P_RING, BW])
        pt = sb(own, "pt", [P, PT_RING, BW])
        pt_lo = sb(own, "pt_lo", [P, PT_RING, BW], F16)
        mx = sb(own, "mx", [P, MX_RING, 4])
        nmx = sb(own, "nmx", [P, MX_RING])

        wq_in = sem("wq_in")
        q_sum = sem("q_sum")
        q_hi_ok = sem("q_hi_ok")
        q_lo_ok = sem("q_lo_ok")
        sc_done = sem("sc_done")
        chunk_max = sem("chunk_max")
        row_max = sem("row_max")
        exp_done = sem("exp_done")
        use_done = sem("use_done")
        bank_read = {e: sem(f"bank_read_{e}") for e in "av"}
        low_ok = {e: sem(f"low_ok_{e}") for e in "vp"}
        pv_done = sem("pv_done")
        sum_read = sem("sum_read")
        zeroed = sem("zeroed")

        def count(n, turn, per_turn):
            return n if turn is None else turn * per_turn + n

        def wait_read(eng, hp, n):
            for e, steps in readers(USES[n % NU]).items():
                before = reads(e, n % NU) - (READS[e] if n < 0 else 0)
                eng.wait_ge(bank_read[e], count(BASE_READS[e] + before + steps, hp, READS[e]))

        def bank_of(use):
            return t_bank[use % 2]

        def query_products(pe, g, part, use):
            w = [wq[p][:, part * P:part * P + P] for p in range(2)]
            x = [ql[p][:, g].rearrange("p t n -> p (t n)") for p in range(2)]
            for n, (a, b) in enumerate(((0, 0), (0, 1), (1, 0))):
                last = pe.matmul(bank_of(use)[:, :], w[a], x[b], start=(n == 0), stop=(n == 2))
            last.then_inc(use_done, 1)

        ROT, PLAIN = (slice(DR, P), slice(0, DR)), (slice(0, DR), slice(DR, P))

        def query_cosine(dve, g, part, use):
            at = slice(g * BW, g * BW + BW)
            if part < 2:
                rot = ROT[part]
                dve.tensor_tensor(out=qf[rot, part, :], in0=bank_of(use)[rot, :], in1=cos2[rot, at],
                                  op=ALU.mult).then_inc(bank_read["v"], 1)
            else:
                dve.tensor_tensor(out=qs[:, :], in0=bank_of(use)[:, :], in1=sin2[:, at], op=ALU.mult).then_inc(bank_read["v"], 1)

        def query_plain(act, part, use):
            act.activation(qf[PLAIN[part], part, :], bank_of(use)[PLAIN[part], :], ACT.Copy).then_inc(bank_read["a"], 1)

        def query_sum(dve, hd):
            dve.tensor_tensor(out=qf[ROT[hd], hd, :], in0=qf[ROT[hd], hd, :], in1=qs[ROT[hd], :], op=ALU.add).then_inc(q_sum, 1)

        def query_high(act, g, hd, n):
            act.wait_ge(q_sum, n * 2 + (hd + 1))
            act.activation(q_hi[:, g % 2, hd, :], qf[:, hd, :], ACT.Copy).then_inc(q_hi_ok, 1)

        def query_low(pool, g, hd, n):
            pool.wait_ge(q_hi_ok, n * 2 + (hd + 1))
            pool.tensor_tensor(out=q_lo[:, g % 2, hd, :], in0=qf[:, hd, :], in1=q_hi[:, g % 2, hd, :].bitcast(F32),
                               op=ALU.subtract).then_inc(q_lo_ok, 1)

        with nc.Block() as block:

            @block.sync
            def _(sp):
                for part in range(2):
                    sp.dma_start(wq[part][:, :].bitcast(F32), wq_dram[part, 0]).then_inc(wq_in, 16)
                with sp.Fori(0, NP) as hp:
                    sp.wait_ge(use_done, hp * NU + (BASE_USES + USE["q", NG - 2, 2] + 1))
                    for part in range(2):
                        sp.dma_start(wq[part][:, :].bitcast(F32),
                                     wq_dram[part, bass.ds(hp + 1, 1)].rearrange("g p n -> (g p) n")).then_inc(wq_in, 16)
                sp.wait_ge(wq_in, 32 * (NP + 1))

            @block.gpsimd
            def _(pool):
                pool.memset(rowsum[:, :, :, :], 0.0).then_inc(zeroed, 1)
                for hd in range(2):
                    query_low(pool, 0, hd, 0)

                def low_parts(hp, s):
                    wait_read(pool, hp, use_of(s))
                    n = CHUNKS[s % NC][2] * P
                    full = pt[:, s % PT_RING, 0:n]
                    pool.tensor_tensor(out=pt_lo[:, s % PT_RING, 0:n], in0=full, in1=cut(full),
                                       op=ALU.subtract).then_inc(low_ok["p"], 1)

                for s in chunks_of(0):
                    if not low_on_vector(s):
                        low_parts(None, s)
                with pool.Fori(0, NP) as hp:
                    for r in ROUNDS:
                        for s in chunks_of(r - 1):
                            if not low_on_vector(s):
                                low_parts(hp, s)
                        for c in prep_sums(r):
                            for hd in range(2):
                                query_low(pool, (c + 1) % NG, hd, hp * NG + (c + 1))

            @block.scalar
            def _(act):
                act.sem_inc(exp_done, CREDIT)
                act.sem_inc(bank_read["a"], CREDIT)
                act.wait_ge(zeroed, 1)
                for part in range(2):
                    act.wait_ge(use_done, CREDIT + part + 1)
                    query_plain(act, part, part - BEFORE)
                for hd in range(2):
                    query_high(act, 0, hd, 0)

                def exponentials(hp, s):
                    item, c, n = CHUNKS[s % NC]
                    i, h = ITEMS[item]
                    ahead = s // NC
                    act.wait_ge(row_max, count(ahead * NI + item + 1, hp, NI))
                    if not (hp is None and s < P_RING):
                        act.wait_ge(use_done, count(BASE_USES + use_of(s - P_RING) + 1, hp, NU))
                    act.activation(probs[:, s % P_RING, 0:n * P], s_bank[s % S_RING][:, 0:n * P], ACT.Exp,
                                   bias=nmx[:, item % MX_RING:item % MX_RING + 1],
                                   accum_out=rowsum[:, i, h, c:c + 1] if hp is None else
                                   rowsum[:, i, bass.ds(hp * 2 + (2 * ahead + h), 1), c]).then_inc(exp_done, 1)

                def evacuate(hp, s):
                    u, n = use_of(s), CHUNKS[s % NC][2]
                    act.wait_ge(use_done, count(BASE_USES + u + 1, hp, NU))
                    act.wait_ge(pv_done, count(CREDIT + s - PT_RING + 1, hp, NC))
                    act.activation(pt[:, s % PT_RING, 0:n * P], bank_of(u)[:, 0:n * P], ACT.Copy, scale=P_SCALE).then_inc(bank_read["a"], 1)

                def round_of(hp, r):
                    moves = [s for s in chunks_of(r - 1) if r >= 1 and not evac_on_vector(s)]
                    for s in moves[:2]:
                        evacuate(hp, s)
                    moves = moves[2:]
                    for s in chunks_of(r):
                        exponentials(hp, s)
                        if moves:
                            evacuate(hp, moves.pop(0))
                    for s in moves:
                        evacuate(hp, s)

                for r in range(2):
                    round_of(None, r)
                with act.Fori(0, NP) as hp:
                    for r in ROUNDS:
                        round_of(hp, r)
                        for c, part in prep_parts(r):
                            if part < 2:
                                use = USE["q", c, part]
                                act.wait_ge(use_done, hp * NU + (BASE_USES + use + 1))
                                act.wait_ge(q_lo_ok, hp * (2 * NG) + (2 * (c + 1)))
                                query_plain(act, part, use)
                        for c in prep_sums(r):
                            for hd in range(2):
                                query_high(act, (c + 1) % NG, hd, hp * NG + (c + 1))

            @block.vector
            def _(dve):
                dve.sem_inc(bank_read["v"], CREDIT)
                dve.sem_inc(sum_read, 1)
                for part in range(3):
                    dve.wait_ge(use_done, CREDIT + part + 1)
                    query_cosine(dve, 0, part, part - BEFORE)
                for e in "va":
                    dve.wait_ge(bank_read[e], CREDIT + FIRST_READS[e])
                for hd in range(2):
                    query_sum(dve, hd)

                def maximum(hp, item):
                    slot, chunks = item % MX_RING, chunks_of(item)
                    for s in chunks:
                        _, c, n = CHUNKS[s % NC]
                        of = s_bank[s % S_RING][:, 0:n * P]
                        dve.wait_ge(sc_done, count(s + 1, hp, NC))
                        if len(chunks) > 1:
                            dve.tensor_reduce(out=mx[:, slot, c:c + 1], in_=of, axis=AXX, op=ALU.max).then_inc(chunk_max, 1)
                        else:
                            dve.tensor_reduce(out=nmx[:, slot:slot + 1], in_=of, axis=AXX, op=ALU.max,
                                              negate=True).then_inc(row_max, 1)
                    if len(chunks) > 1:
                        ahead, s = divmod(chunks[-1], NC)
                        dve.wait_ge(chunk_max, count((ahead * len(MANY) + MANY.index(s) + 1), hp, len(MANY)))
                        dve.tensor_reduce(out=nmx[:, slot:slot + 1], in_=mx[:, slot, 0:len(chunks)], axis=AXX, op=ALU.max,
                                          negate=True).then_inc(row_max, 1)

                def move(hp, item):
                    for s in chunks_of(item):
                        u, n = use_of(s), CHUNKS[s % NC][2]
                        full = pt[:, s % PT_RING, 0:n * P]
                        if evac_on_vector(s):
                            dve.wait_ge(use_done, count(BASE_USES + u + 1, hp, NU))
                            dve.wait_ge(pv_done, count(CREDIT + s - PT_RING + 1, hp, NC))
                            dve.tensor_scalar(full, bank_of(u)[:, 0:n * P], P_SCALE, None, ALU.mult).then_inc(bank_read["v"], 1)
                        if low_on_vector(s):
                            wait_read(dve, hp, u)
                            dve.tensor_tensor(out=pt_lo[:, s % PT_RING, 0:n * P], in0=full, in1=cut(full),
                                              op=ALU.subtract).then_inc(low_ok["v"], 1)

                for r in range(2):
                    maximum(None, r)
                    if r == 1:
                        move(None, 0)
                with dve.Fori(0, NP) as hp:
                    for r in ROUNDS:
                        maximum(hp, r)
                        for c in prep_sums(r):
                            for hd in range(2):
                                for part in (hd, 2):
                                    wait_read(dve, hp, USE["q", c, part])
                                query_sum(dve, hd)
                        move(hp, r - 1)
                        i, h = ITEMS[r - 2]
                        dve.wait_ge(pv_done, hp * NC + (CREDIT + FIRST[r - 1]))
                        dve.tensor_reduce(out=lat[:, i, bass.ds(hp * (2 * KVL) + h * KVL, KVL)],
                                          in_=o_bank[:, 0:2 * KVL].rearrange("p (a n) -> p n a", a=2), axis=AXX,
                                          op=ALU.add).then_inc(sum_read, 1)
                        for c, part in prep_parts(r):
                            use = USE["q", c, part]
                            dve.wait_ge(q_lo_ok, hp * (2 * NG) + (2 * (c + 1)))
                            dve.wait_ge(use_done, hp * NU + (BASE_USES + use + 1))
                            query_cosine(dve, (c + 1) % NG, part, use)

            @block.tensor
            def _(pe):
                pe.sem_inc(use_done, CREDIT)
                pe.sem_inc(pv_done, CREDIT)
                pe.wait_ge(wq_in, 32)
                for part in range(3):
                    if part == 2:
                        for e in "av":
                            pe.wait_ge(bank_read[e], CREDIT + PREP_READS[0][e])
                    query_products(pe, 0, part, part - BEFORE)
                for e in "av":
                    pe.wait_ge(bank_read[e], CREDIT + FIRST_READS[e])

                def scores(hp, item):
                    i, h = ITEMS[item % NI]
                    g, ahead = i % NG, item // NI
                    tok = (i // NG) * P
                    q = [w[:, g % 2, h, tok:tok + P] for w in (q_hi, q_lo)]
                    if item % (2 * BT) == 0:
                        pe.wait_ge(q_lo_ok, count(2 * (NG * ahead + g + 1), hp, 2 * NG))
                    for s in chunks_of(item):
                        _, c, n = CHUNKS[s % NC]
                        to = s_bank[s % S_RING]
                        cols = max(n * P, 2 * P)
                        at = slice(c * BW, c * BW + cols)
                        keys = [kt_hi[h][:, at], kt_lo[h][:, at]]
                        diagonal = s == chunks_of(item)[-1]
                        pe.wait_ge(exp_done, count(CREDIT + s - S_RING + 1, hp, NC))
                        for m, (a, b) in enumerate(((0, 0), (0, 1), (1, 0))):
                            last = pe.matmul(to[:, 0:cols], q[a], keys[b], start=(m == 0), stop=(m == 2 and not diagonal))
                        if diagonal:
                            last = pe.matmul(to[:, (n - 1) * P:n * P], ident16[:, :], mask16[:, :], start=False, stop=True)
                        last.then_inc(sc_done, 1)

                def transpose(hp, s):
                    u, n = use_of(s), CHUNKS[s % NC][2]
                    pe.wait_ge(exp_done, count(CREDIT + s + 1, hp, NC))
                    if not (hp is None and s < 2):
                        wait_read(pe, hp, u - 2)
                    for j in range(n):
                        last = pe.transpose(bank_of(u)[:, j * P:j * P + P], probs[:, s % P_RING, j * P:j * P + P], ident[:, :])
                    last.then_inc(use_done, 1)

                def weigh(hp, s):
                    item, c, n = CHUNKS[s]
                    e = "v" if low_on_vector(s) else "p"
                    pe.wait_ge(low_ok[e], hp * LOWS[e] + lows(e, s + 1))
                    if s == FIRST[item]:
                        pe.wait_ge(sum_read, hp * NI + (item + 1))
                    for j in range(n):
                        key = 4 * c + j
                        high = cut(pt[:, s % PT_RING, j * P:j * P + P])
                        end = s == FIRST[item + 1] - 1 and j == n - 1
                        pe.matmul(o_bank[:, 0:2 * KVL], high, values[:, key, :], start=(c == 0 and j == 0), stop=False)
                        last = pe.matmul(o_bank[:, 0:KVL], pt_lo[:, s % PT_RING, j * P:j * P + P], values[:, key, 0:KVL],
                                         start=False, stop=end)
                    last.then_inc(pv_done, 1)

                scores(None, 0)
                scores(None, 1)
                for s in chunks_of(0):
                    transpose(None, s)
                with pe.Fori(0, NP) as hp:
                    for r in ROUNDS:
                        scores(hp, r)
                        new, old = chunks_of(r - 1), chunks_of(r - 2)
                        while new or old:
                            for s in new[:2]:
                                transpose(hp, s)
                            for s in old[:2]:
                                weigh(hp, s)
                            new, old = new[2:], old[2:]
                        for c, part in prep_parts(r):
                            if c == NG - 1 and part == 0:
                                pe.wait_ge(wq_in, hp * 32 + 64)
                            use = USE["q", c, part]
                            wait_read(pe, hp, use - 2)
                            query_products(pe, (c + 1) % NG, part, use)


def cut(a):
    return a.bitcast(BF16).rearrange("p (n e) -> p n e", e=2)[:, :, 1]


def experts(nc, sb, sem, k):
    bank, lat, rowsum, ident, gates = k["bank"], k["lat"], k["rowsum"], k["ident"], k["gates"]
    modc, neg_half, turnstile = k["modc"], k["neg_half"], k["turnstile"]
    up_bank = ((bank[0], bank[1]), (bank[6], bank[7]))
    down_bank, front_bank = bank[2:4], bank[4:6]
    with ExitStack() as own:
        xs = sb(own, "xs_again", [P, NT, D])
        w_vo = k["w_vo"]
        wvo_hi = sb(own, "wvo_hi", [P, NP, D], F32R)
        wvo_lo = sb(own, "wvo_lo", [P, NP, D], F32R)
        wi_hi = [sb(own, f"wi_{n}_hi", [P, KD, E, M], F32R) for n in range(2)]
        wi_lo = [sb(own, f"wi_{n}_lo", [P, KD, E, M], F32R) for n in range(2)]
        wo_hi = sb(own, "wo_hi", [P, E, D], F32R)
        wo_lo = sb(own, "wo_lo", [P, E, D], F32R)
        wo = w_vo
        wg = sb(own, "wg", [P, KD, E])
        rden = sb(own, "rden", [P, NT, H])
        lat_n = sb(own, "lat_n", [P, 2, H, KVL])
        lat_hi = sb(own, "lat_hi", [P, NP, P], F32R)
        lat_lo = sb(own, "lat_lo", [P, NP, P], F32R)
        stats = sb(own, "stats2", [P, BT, 6])
        mv = sb(own, "mv2", [P, BT, 2])
        rstd = sb(own, "rstd2", [P, BT])
        euler = sb(own, "euler", [P, BT])
        xn = sb(own, "xn2", [P, BT, D])
        ht = sb(own, "ht2", [P, KD, BW])
        ht_hi = sb(own, "ht2_hi", [P, KD, BW], F32R)
        ht_lo = sb(own, "ht2_lo", [P, KD, BW], F32R)
        silu = sb(own, "expert_silu", [P, 2, BW])
        stage = [xn[:, :, :].rearrange("p t (a m) -> p (t a) m", m=M), ht[:, :, :].rearrange("p k (a m) -> p (k a) m", m=M),
                 silu[:, :, :].rearrange("p k (a m) -> p (k a) m", m=M)]
        pieces = [(n, kd) for n in range(2) for kd in range(KD)]
        places = sb(own, "places", [P, E], mybir.dt.int32)
        placesf = sb(own, "placesf", [P, E])
        logits = sb(own, "logits", [P, BT, E])
        top = sb(own, "top", [P, BT, 8])
        top_at = sb(own, "top_at", [P, BT, 8], U32)
        top_f = sb(own, "top_f", [P, BT, 2])
        gap = sb(own, "gap", [P, BT])
        ratio = sb(own, "ratio", [P, BT])
        total = sb(own, "total", [P, BT])
        first_w = sb(own, "first_w", [P, BT])
        second_w = sb(own, "second_w", [P, BT])
        route1 = sb(own, "route1", [P, BT, E])
        route2 = sb(own, "route2", [P, BT, E])
        route = sb(own, "route", [P, BT, E])
        inner = silu
        inner_hi = sb(own, "inner_hi", [P, 2, BW], F32R)
        inner_lo = sb(own, "inner_lo", [P, 2, BW], F32R)

        dma = {n: sem(n) for n in "x2_in wo_in wg_in out_ok".split()}
        wi_in = [sem(f"wi_in_{i}") for i in range(len(pieces))]
        place_i, place_f = sem("place_i"), sem("place_f")
        whole_ok, w_hi, w_lo = sem("whole_ok"), sem("w_hi"), sem("w_lo")
        den_ok, rden_ok, latn_ok = sem("den_ok"), sem("rden_ok"), sem("latn_ok")
        flipped = sem("flipped")
        lath_ok, latl_ok = sem("lath_ok"), sem("latl_ok")
        att_mm, y_ok = sem("att_mm"), sem("y_ok")
        st2_ok, mv2_ok, var2_ok, rstd2_ok, xn2_ok = (sem(n) for n in ("st2_ok", "mv2_ok", "var2_ok", "rstd2_ok", "xn2_ok"))
        xt2_mm, ht2_ok, hth_ok, htl_ok = sem("xt2_mm"), sem("ht2_ok"), sem("hth_ok"), sem("htl_ok")
        lg_mm, lg_ok, top_ok, gap_ok, at_ok, topf_ok = (sem(n) for n in ("lg_mm", "lg_ok", "top_ok", "gap_ok", "at_ok", "topf_ok"))
        ratio_ok, tot_ok, w1_ok, w2_ok = sem("ratio_ok"), sem("tot_ok"), sem("w1_ok"), sem("w2_ok")
        routes, route_ok = sem("routes"), sem("route_ok")
        up_mm = sem("up_mm")
        silu_ok = sem("silu_ok")
        inner_ok = sem("inner_ok")
        inh_ok, inl_ok = sem("inh_ok"), sem("inl_ok")
        down_mm = sem("down_mm")
        down_read = sem("down_read")

        lat_slots = ((lat_hi, lat_lo), tuple(w[:, :, :].rearrange("p a (j n) -> p (a j) n", n=P) for w in (inner_hi, inner_lo)))

        def lat_slot(t, first):
            return lat_slots[t % 2 if first else 0]

        def att_bank(t, first):
            return down_bank[t % 2] if first else front_bank[0]

        PASSES = ((0, 0), (0, 1), (1, 0))
        front_tile = {e: e for e in range(BT)}
        NORM_AT = BT

        with nc.Block() as block:

            @block.sync
            def _(sp):
                sp.dma_start(xs[:, :, :], k["x"].rearrange("a (t p) d -> p (a t) d", p=P)).then_inc(dma["x2_in"], 16)
                for i, (n, kd) in enumerate(pieces):
                    if i == len(stage):
                        sp.wait_ge(w_lo, 1)
                        sp.dma_start(wo[:, :, :], k["wo"].rearrange("e p d -> p e d")).then_inc(dma["wo_in"], 16)
                    if i >= len(stage):
                        sp.wait_ge(w_lo, 2 + i - len(stage))
                    sp.dma_start(stage[i % len(stage)], k[f"wi_{n}"].rearrange("e (k p) m -> k p e m", p=P)[kd]).then_inc(wi_in[i], 16)
                sp.dma_start(wg[:, :, :], k["w_gate"].rearrange("(k p) e -> p k e", p=P)).then_inc(dma["wg_in"], 16)
                rows = k["out"].rearrange("a (t p) d -> p (a t) d", p=P)
                with sp.Fori(0, NB) as b:
                    sp.wait_ge(down_read, b * (BT * E) + (BT + BT * E))
                    sp.dma_start(rows[:, bass.ds(b * BT, BT), :], xs[:, bass.ds(b * BT, BT), :]).then_inc(dma["out_ok"], 16)
                sp.wait_ge(dma["out_ok"], 16 * NB)

            @block.gpsimd
            def _(pool):
                pool.iota(places[:, :], pattern=[[1, E]], base=0, channel_multiplier=0).then_inc(place_i, 1)
                pool.wait_ge(place_i, 1)
                pool.tensor_copy(placesf[:, :], places[:, :]).then_inc(place_f, 1)
                pool.memset(euler[:, :], math.e).then_inc(place_f, 1)

                def normalise_sums(f, t):
                    pool.wait_ge(flipped, f * (2 * BT) + (2 * t + 2))
                    tile = bass.ds(f * BT + t, 1)
                    pool.tensor_tensor(out=lat_n[:, t % 2], in0=lat[:, tile, :].rearrange("p a (h n) -> p (a h) n", h=H),
                                       in1=rden[:, tile, :].rearrange("p a h -> p (a h)").unsqueeze(2).to_broadcast([P, H, KVL]),
                                       op=ALU.mult).then_inc(latn_ok, 1)

                def turn(f, last):
                    for t in (2, 3):
                        normalise_sums(f, t)
                    pool.wait_ge(var2_ok, f + 1)
                    pool.tensor_tensor(out=rstd[:, :], in0=rstd[:, :], in1=neg_half[:, 0:BT], op=ALU.pow).then_inc(rstd2_ok, 1)
                    if not last:
                        for t in (0, 1):
                            normalise_sums(f + 1, t)
                    pool.wait_ge(gap_ok, f + 1)
                    pool.tensor_tensor(out=ratio[:, :], in0=euler[:, :], in1=gap[:, :], op=ALU.pow).then_inc(ratio_ok, 1)

                pool.wait_ge(place_f, 2)
                pool.wait_ge(rden_ok, 1)
                for t in (0, 1):
                    normalise_sums(0, t)
                pool.wait_ge(rden_ok, 2)
                with pool.Fori(0, NB - 1) as f:
                    turn(f, False)
                turn(NB - 1, True)

            @block.scalar
            def _(act):
                def flip_high(f, t, first=False):
                    if not first:
                        act.wait_ge(att_mm, f * BT + t)
                    elif t >= 2:
                        act.wait_ge(att_mm, t - 1)
                    for half in range(2):
                        act.wait_ge(flipped, f * (2 * BT) + (4 + 2 * t + half + 1))
                        act.activation(lat_slot(t, first)[0][:, 4 * half:4 * half + 4, :].rearrange("p j n -> p (j n)"),
                                       front_bank[half][:, :], ACT.Copy).then_inc(lath_ok, 1)

                def normed(f):
                    for kd in range(KD):
                        act.wait_ge(xt2_mm, f * KD + (kd + 1))
                        act.activation(ht[:, kd, :], front_bank[kd][:, :], ACT.Identity, scale=modc[:, 3, kd:kd + 1],
                                       bias=modc[:, 2, kd:kd + 1]).then_inc(ht2_ok, 1)

                def normed_high(f):
                    act.wait_ge(ht2_ok, f * KD + KD)
                    for kd in range(KD):
                        act.activation(ht_hi[:, kd, :], ht[:, kd, :], ACT.Copy).then_inc(hth_ok, 1)

                def expert_silu(b, e):
                    act.wait_ge(up_mm, b * E + (e + 1))
                    act.wait_ge(inl_ok, b * E + (e + 1))
                    act.activation(silu[:, e % 2, :], up_bank[e % 2][0][:, :], ACT.Silu).then_inc(silu_ok, 1)

                def expert_high(b, e):
                    act.wait_ge(inner_ok, b * E + (2 + e + 1))
                    act.wait_ge(down_mm, b * (BT * E) + BT * (e + 1))
                    act.activation(inner_hi[:, e % 2, :], inner[:, e % 2, :], ACT.Copy).then_inc(inh_ok, 1)

                def turn(b, last):
                    f = b + 1
                    for e in range(E):
                        if e in front_tile and not last:
                            flip_high(f, front_tile[e])
                        if e == E - 2 and not last:
                            act.wait_ge(up_mm, b * E + E)
                            normed_high(f)
                        if e < E - 1:
                            expert_silu(b, e + 1)
                            expert_high(b, e + 1)
                        elif not last:
                            expert_silu(f, 0)
                            expert_high(f, 0)
                        if e == NORM_AT and not last:
                            normed(f)

                act.activation(wvo_hi[:, :, :], w_vo[:, :, :], ACT.Copy).then_inc(w_hi, 1)
                flip_high(0, 0, True)
                for i, (n, kd) in enumerate(pieces):
                    if i + 1 < BT:
                        flip_high(0, i + 1, True)
                    act.wait_ge(wi_in[i], 16)
                    act.activation(wi_hi[n][:, kd], stage[i % len(stage)], ACT.Copy).then_inc(w_hi, 1)
                normed(0)
                normed_high(0)
                act.wait_ge(whole_ok, 1)
                act.activation(wo_hi[:, :, :], wo[:, :, :], ACT.Copy).then_inc(w_hi, 1)
                expert_silu(0, 0)
                expert_high(0, 0)
                with act.Fori(0, NB - 1) as b:
                    turn(b, False)
                turn(NB - 1, True)

            @block.vector
            def _(dve):
                def flip_low(f, t, first=False):
                    hi, lo = (w[:, :, :].rearrange("p j n -> p (j n)") for w in lat_slot(t, first))
                    for half in range(2):
                        at = slice(half * BW, half * BW + BW)
                        dve.wait_ge(lath_ok, f * (2 * BT) + (2 * t + half + 1))
                        dve.tensor_tensor(out=lo[:, at], in0=front_bank[half][:, :], in1=hi[:, at].bitcast(F32),
                                          op=ALU.subtract).then_inc(latl_ok, 1)

                def add_attention(f, t, first=False):
                    tile = xs[:, bass.ds(f * BT + t, 1), :].rearrange("p a d -> p (a d)")
                    dve.wait_ge(att_mm, f * BT + (t + 1))
                    dve.tensor_tensor(out=tile, in0=att_bank(t, first)[:, 0:D], in1=tile, op=ALU.add).then_inc(y_ok, 1)
                    dve.wait_ge(y_ok, f * BT + (t + 1))
                    dve.memset(turnstile[:, :], 0.0)
                    dve.bn_stats(stats[:, t, :], tile).then_inc(st2_ok, 1)

                def normalise(f):
                    dve.wait_ge(st2_ok, f * BT + BT)
                    dve.memset(turnstile[:, :], 0.0)
                    for t in range(BT):
                        dve.bn_aggr(mv[:, t, :], stats[:, t, :]).then_inc(mv2_ok, 1)
                    dve.wait_ge(mv2_ok, f * BT + BT)
                    dve.tensor_scalar(rstd[:, :], mv[:, :, 1], LN_EPS, None, ALU.add).then_inc(var2_ok, 1)
                    dve.wait_ge(rstd2_ok, f + 1)
                    for t in range(BT):
                        tile = xs[:, bass.ds(f * BT + t, 1), :].rearrange("p a d -> p (a d)")
                        dve.tensor_scalar(xn[:, t, :], tile, mv[:, t, 0:1], rstd[:, t:t + 1], ALU.subtract,
                                          ALU.mult).then_inc(xn2_ok, 1)

                def normed_low(f):
                    for kd in range(KD):
                        dve.wait_ge(hth_ok, f * KD + (kd + 1))
                        dve.tensor_tensor(out=ht_lo[:, kd, :], in0=ht[:, kd, :], in1=ht_hi[:, kd, :].bitcast(F32),
                                          op=ALU.subtract).then_inc(htl_ok, 1)

                def choose(f):
                    dve.wait_ge(lg_mm, f + 1)
                    dve.tensor_copy(logits[:, :, :], front_bank[0][:, 0:BT * E].rearrange("p (t e) -> p t e", e=E)).then_inc(lg_ok, 1)
                    dve.wait_ge(lg_ok, f + 1)
                    dve.memset(turnstile[:, :], 0.0)
                    for t in range(BT):
                        dve.max(top[:, t, :], logits[:, t, :]).then_inc(top_ok, 1)
                    dve.wait_ge(top_ok, f * BT + BT)
                    dve.tensor_tensor(out=gap[:, :], in0=top[:, :, 1], in1=top[:, :, 0], op=ALU.subtract).then_inc(gap_ok, 1)
                    for t in range(BT):
                        dve.max_index(top_at[:, t, :], top[:, t, :], logits[:, t, :]).then_inc(at_ok, 1)
                    dve.wait_ge(at_ok, f * BT + BT)
                    dve.tensor_copy(top_f[:, :, :], top_at[:, :, 0:2]).then_inc(topf_ok, 1)

                def weigh(f):
                    dve.wait_ge(ratio_ok, f + 1)
                    dve.tensor_scalar(total[:, :], ratio[:, :], 1.0, None, ALU.add).then_inc(tot_ok, 1)
                    dve.wait_ge(tot_ok, f + 1)
                    dve.reciprocal(first_w[:, :], total[:, :]).then_inc(w1_ok, 1)
                    dve.wait_ge(w1_ok, f + 1)
                    dve.tensor_tensor(out=second_w[:, :], in0=ratio[:, :], in1=first_w[:, :], op=ALU.mult).then_inc(w2_ok, 1)
                    dve.wait_ge(topf_ok, f + 1)
                    dve.wait_ge(w2_ok, f + 1)
                    for t in range(BT):
                        for n, (to, w) in enumerate(((route1, first_w), (route2, second_w))):
                            dve.tensor_scalar(to[:, t, :], placesf[:, :], top_f[:, t, n:n + 1], w[:, t:t + 1], ALU.is_equal,
                                              ALU.mult).then_inc(routes, 1)
                    dve.wait_ge(routes, f * (2 * BT) + 2 * BT)
                    dve.tensor_tensor(out=route[:, :, :], in0=route1[:, :, :], in1=route2[:, :, :], op=ALU.add).then_inc(route_ok, 1)
                    dve.wait_ge(route_ok, f + 1)

                def expert_inner(b, e):
                    dve.wait_ge(silu_ok, b * E + (e + 1))
                    dve.tensor_tensor(out=inner[:, e % 2, :], in0=silu[:, e % 2, :], in1=up_bank[e % 2][1][:, :],
                                      op=ALU.mult).then_inc(inner_ok, 1)

                def expert_low(b, e):
                    dve.wait_ge(inh_ok, b * E + (e + 1))
                    dve.tensor_tensor(out=inner_lo[:, e % 2, :], in0=inner[:, e % 2, :], in1=inner_hi[:, e % 2, :].bitcast(F32),
                                      op=ALU.subtract).then_inc(inl_ok, 1)

                def expert_add(b, e):
                    for t in range(BT):
                        tile = xs[:, bass.ds(b * BT + t, 1), :].rearrange("p a d -> p (a d)")
                        dve.wait_ge(down_mm, b * (BT * E) + (2 * BT + BT * e + t // 2 * 2 + 2))
                        dve.scalar_tensor_tensor(out=tile, in0=down_bank[t // 2][:, (t % 2) * D:(t % 2) * D + D],
                                                 scalar=route[:, t, e:e + 1], in1=tile, op0=ALU.mult,
                                                 op1=ALU.add).then_inc(down_read, 1)

                def turn(b, last):
                    f = b + 1
                    for e in range(E):
                        if e in front_tile and not last:
                            flip_low(f, front_tile[e])
                        if e == NORM_AT and not last:
                            normalise(f)
                        if e == E - 2 and not last:
                            normed_low(f)
                        if e < E - 1:
                            expert_inner(b, e + 1)
                            expert_low(b, e + 1)
                        elif not last:
                            expert_inner(f, 0)
                            expert_low(f, 0)
                        if e in front_tile and not last:
                            add_attention(f, front_tile[e])
                        if e == 0:
                            weigh(b)
                        expert_add(b, e)
                        if e == E - 2 and not last:
                            choose(f)
                dve.sem_inc(inner_ok, 2)
                dve.sem_inc(inl_ok, 2)
                dve.sem_inc(down_read, BT)
                for n, tiles in enumerate((slice(0, BT), slice(BT, NT))):
                    dve.tensor_reduce(out=rden[:, tiles, :], in_=rowsum[:, tiles, 0:H, :], axis=AXX, op=ALU.add).then_inc(den_ok, 1)
                    dve.wait_ge(den_ok, 2 * n + 1)
                    dve.tensor_scalar(rden[:, tiles, :], rden[:, tiles, :], P_SCALE, None, ALU.mult).then_inc(den_ok, 1)
                    dve.wait_ge(den_ok, 2 * n + 2)
                    dve.reciprocal(rden[:, tiles, :], rden[:, tiles, :]).then_inc(rden_ok, 1)
                dve.wait_ge(w_hi, 1)
                dve.tensor_tensor(out=wvo_lo[:, :, :], in0=w_vo[:, :, :], in1=wvo_hi[:, :, :].bitcast(F32),
                                  op=ALU.subtract).then_inc(w_lo, 1)
                def piece_low(i):
                    n, kd = pieces[i]
                    dve.wait_ge(w_hi, 2 + i)
                    dve.tensor_tensor(out=wi_lo[n][:, kd], in0=stage[i % len(stage)], in1=wi_hi[n][:, kd].bitcast(F32),
                                      op=ALU.subtract).then_inc(w_lo, 1)

                flip_low(0, 0, True)
                dve.wait_ge(dma["x2_in"], 16)
                for t in range(BT):
                    if t + 1 < BT:
                        flip_low(0, t + 1, True)
                    add_attention(0, t, True)
                    if t < len(pieces) - 1:
                        piece_low(t)
                piece_low(len(pieces) - 1)
                normalise(0)
                dve.wait_ge(dma["wo_in"], 16)
                dve.tensor_tensor(out=wo[:, :, :], in0=wo[:, :, :],
                                  in1=gates[:, 1:2, :].to_broadcast([P, E, D]), op=ALU.mult).then_inc(whole_ok, 1)
                normed_low(0)
                dve.wait_ge(w_hi, 2 + len(pieces))
                dve.tensor_tensor(out=wo_lo[:, :, :], in0=wo[:, :, :], in1=wo_hi[:, :, :].bitcast(F32),
                                  op=ALU.subtract).then_inc(w_lo, 1)
                dve.wait_ge(place_f, 2)
                choose(0)
                expert_inner(0, 0)
                expert_low(0, 0)
                with dve.Fori(0, NB - 1) as b:
                    turn(b, False)
                turn(NB - 1, True)

            @block.tensor
            def _(pe):
                def flip(f, t, first=False):
                    pe.wait_ge(latn_ok, f * BT + (t + 1))
                    if t > 0 and first:
                        pe.wait_ge(lath_ok, 2 * t)
                        pe.wait_ge(latl_ok, 2 * t)
                    elif t > 0:
                        pe.wait_ge(y_ok, f * BT + t)
                    flat = lat_n[:, t % 2].rearrange("p h n -> p (h n)")
                    for half in range(2):
                        for j in range(4):
                            at = (4 * half + j) * P
                            last = pe.transpose(front_bank[half][:, j * P:j * P + P], flat[:, at:at + P], ident[:, :])
                        last.then_inc(flipped, 1)

                def project(f, t, first=False):
                    pe.wait_ge(lath_ok, f * (2 * BT) + (2 * t + 2))
                    pe.wait_ge(latl_ok, f * (2 * BT) + (2 * t + 2))
                    if first and t >= 2:
                        pe.wait_ge(y_ok, t - 1)
                    for g in range(NP):
                        for a, w in PASSES:
                            last = pe.matmul(att_bank(t, first)[:, 0:D], lat_slot(t, first)[a][:, g, :], (wvo_hi, wvo_lo)[w][:, g, :],
                                             start=(g == 0 and a == w), stop=(g == NP - 1 and a == 1))
                    last.then_inc(att_mm, 1)

                def flip_normed(f):
                    pe.wait_ge(xn2_ok, f * BT + BT)
                    for kd in range(KD):
                        for t in range(BT):
                            last = pe.transpose(front_bank[kd][:, t * P:t * P + P], xn[:, t, kd * P:kd * P + P], ident[:, :])
                        last.then_inc(xt2_mm, 1)

                def gate(f):
                    pe.wait_ge(ht2_ok, f * KD + KD)
                    for t in range(BT):
                        for kd in range(KD):
                            last = pe.matmul(front_bank[0][:, t * E:t * E + E], ht[:, kd, t * P:t * P + P], wg[:, kd, :],
                                             start=(kd == 0), stop=(kd == KD - 1))
                    last.then_inc(lg_mm, 1)

                def up(b, e):
                    if e == 0:
                        pe.wait_ge(hth_ok, b * KD + KD)
                        pe.wait_ge(htl_ok, b * KD + KD)
                    pe.wait_ge(inner_ok, b * E + (e + 1))
                    for n in range(2):
                        for kd in range(KD):
                            for w, x in PASSES:
                                last = pe.matmul(up_bank[e % 2][n][:, :], (wi_hi, wi_lo)[w][n][:, kd, e, :],
                                                 (ht_hi, ht_lo)[x][:, kd, :], start=(kd == 0 and w == x),
                                                 stop=(kd == KD - 1 and w == 1))
                    last.then_inc(up_mm, 1)

                def down(b, e):
                    pe.wait_ge(inh_ok, b * E + (e + 1))
                    pe.wait_ge(inl_ok, b * E + (2 + e + 1))
                    for t in range(BT):
                        if t % 2 == 0:
                            pe.wait_ge(down_read, b * (BT * E) + (BT * e + t + 2))
                        to = down_bank[t // 2][:, (t % 2) * D:(t % 2) * D + D]
                        for a, w in PASSES:
                            last = pe.matmul(to, (inner_hi, inner_lo)[a][:, e % 2, t * P:t * P + P], (wo_hi, wo_lo)[w][:, e, :],
                                             start=(a == w), stop=(a == 1))
                        last.then_inc(down_mm, 1)

                def turn(b, last):
                    f = b + 1
                    for e in range(E):
                        if e in front_tile and not last:
                            if front_tile[e] == 0:
                                pe.wait_ge(lg_ok, f)
                            flip(f, front_tile[e])
                        if e < E - 1:
                            up(b, e + 1)
                        elif not last:
                            up(f, 0)
                        if e in front_tile and not last:
                            project(f, front_tile[e])
                        if e == NORM_AT + 1 and not last:
                            flip_normed(f)
                        down(b, e)
                        if e == E - 2 and not last:
                            gate(f)

                pe.sem_inc(flipped, 4)
                pe.sem_inc(down_mm, 2 * BT)
                flip(0, 0, True)
                for t in range(BT):
                    if t + 1 < BT:
                        flip(0, t + 1, True)
                    if t == 0:
                        pe.wait_ge(w_lo, 1)
                    project(0, t, True)
                flip_normed(0)
                pe.wait_ge(dma["wg_in"], 16)
                gate(0)
                pe.wait_ge(w_lo, 1 + len(pieces))
                up(0, 0)
                pe.wait_ge(w_lo, 2 + len(pieces))
                with pe.Fori(0, NB - 1) as b:
                    turn(b, False)
                turn(NB - 1, True)


NAMES = ["L0_attn_x", "L0_attn_w_qa", "L0_attn_q_a_norm_w", "L0_attn_w_qb", "L0_attn_w_kva", "L0_attn_kv_a_norm_w",
         "L0_attn_w_kvb", "L0_attn_w_o", "L0_ffn_w_gate", "L0_ffn_wi_0", "L0_ffn_wi_1", "L0_ffn_wo", "L0_c", "L0_wmod"]


def rotary_tables():
    inv = (np.float32(1.0) / np.float32(10000.0) ** (np.arange(0, DR, 2, dtype=np.float32) / np.float32(DR))).astype(np.float32)
    freqs = np.outer(np.arange(S, dtype=np.float32), inv).astype(np.float32)
    emb = np.concatenate((freqs, freqs), -1)
    return np.cos(emb).astype(np.float32), np.sin(emb).astype(np.float32)


def kernel(**inputs):
    import concourse.bacc as bacc
    from concourse.bass_utils import run_bass_kernel_spmd

    nc = bacc.Bacc("TRN2", target_bir_lowering=False, num_devices=1)
    cos, sin = rotary_tables()
    signs = np.where(np.arange(DR) % 2 == 0, np.float32(-1), np.float32(1))
    grouped = [np.ascontiguousarray(t.reshape(BT, NG, P, DR).transpose(3, 1, 0, 2).reshape(DR, S)) for t in (cos, sin)]
    tables = {"rope_cos_by_feature": grouped[0], "rope_sin_by_feature": grouped[1],
              "rope_cos_by_token": cos, "rope_sin_by_token": sin * signs}
    arrays = {f"in_{n}": np.ascontiguousarray(inputs[n]) for n in NAMES} | tables
    args = [nc.dram_tensor(n, a.shape, mybir.dt.from_np(a.dtype), kind="ExternalInput").ap() for n, a in arrays.items()]
    out = nc.dram_tensor("out_0", (1, S, D), F32, kind="ExternalOutput").ap()
    adaln_block_kernel(nc, *args, out)
    result = run_bass_kernel_spmd(nc, [arrays], core_ids=[0])
    return result.results[0]["out_0"]
```
